# Optimizing a Trainium2 kernel written in Bass

```python
import numpy as np
import jax
import jax.numpy as jnp

def _softmax(x, axis=-1):
    return jax.nn.softmax(x, axis=axis)

def _gelu(x):
    return jax.nn.gelu(x, approximate=True)

def _silu(x):
    return jax.nn.silu(x)

def _sigmoid(x):
    return jax.nn.sigmoid(x)

def _layernorm(x, axis=-1, eps=1e-05):
    m = jnp.mean(x, axis=axis, keepdims=True)
    v = jnp.var(x, axis=axis, keepdims=True)
    return (x - m) / jnp.sqrt(v + eps)

def _scatter_add(tgt, idx, src, axis=0):
    return tgt.at[idx].add(src)

def _segment_sum(src, seg, n):
    return jax.ops.segment_sum(src, seg, n)
kernel_name = 'mk_vit_tower_cls_d1_tok_img1024_r4_1e375f'

def setup_inputs(seed: int=0):
    np.random.seed(seed)
    _w = jnp.asarray

    def _rec_inputs():
        import jax
        import jax.numpy as jnp
        _rk = jax.random.key(seed)
        x = -0.000125008 + 0.999885 * jax.random.normal(jax.random.fold_in(_rk, 1), (8, 512, 256, 4), jnp.float32)
        cls_tok = 0.02 * jax.random.normal(jax.random.fold_in(_rk, 5), (1, 1, 256), jnp.float32)
        return (x, cls_tok)
    x, cls_tok = _rec_inputs()

    def _L0_tok_setup():
        import jax, jax.numpy as jnp
        import numpy as np
        key = jax.random.key(seed)
        k1, k2, k3 = jax.random.split(key, 3)
        B, H, I, O, Dp1 = (4, 512, 256, 256, 4)
        x = jax.random.normal(k1, (B, H, I, Dp1), dtype=jnp.float32)
        weight = 0.1 * jax.random.normal(k2, (O, Dp1), dtype=jnp.float32)
        weighted_sum = 0.1 * jax.random.normal(k3, (O, I), dtype=jnp.float32)
        return {'x': x, 'weight': weight, 'weighted_sum': weighted_sum}
    _L0_tok_all = _L0_tok_setup()
    _L0_tok_in = {k: v for k, v in _L0_tok_all.items() if k in ('weight', 'weighted_sum')}
    del _L0_tok_all

    def _L0_attn_setup():
        import jax, jax.numpy as jnp
        import numpy as np
        EMBED_DIM = 256
        NUM_HEADS = 16
        key = jax.random.key(seed)
        k1, k2, k3 = jax.random.split(key, 3)
        B, N, C = (8, 1024, EMBED_DIM)
        x = jax.random.normal(k1, (B, N, C), dtype=jnp.float32)
        w_qkv = jax.random.normal(k2, (3 * C, C), dtype=jnp.float32) * C ** (-0.5)
        b_qkv = jnp.zeros((3 * C,), dtype=jnp.float32)
        w_out = jax.random.normal(k3, (C, C), dtype=jnp.float32) * C ** (-0.5)
        b_out = jnp.zeros((C,), dtype=jnp.float32)
        return {'x': x, 'w_qkv': w_qkv, 'b_qkv': b_qkv, 'w_out': w_out, 'b_out': b_out}
    _L0_attn_all = _L0_attn_setup()
    _L0_attn_in = {k: v for k, v in _L0_attn_all.items() if k in ('w_qkv', 'b_qkv', 'w_out', 'b_out')}
    del _L0_attn_all

    def _L0_ffn_setup():
        import jax, jax.numpy as jnp
        import numpy as np
        B, S, D = (2, 512, 256)
        M = 512
        E = 8
        TOP_K = 2
        key = jax.random.key(seed)
        ks = jax.random.split(key, 5)
        std = 0.02
        return {'residual': jax.random.normal(ks[0], (B, S, D), jnp.float32), 'W_router': jax.random.normal(ks[1], (D, E), jnp.float32) * std, 'W_gate': jax.random.normal(ks[2], (E, D, M), jnp.float32) * std, 'b_gate': jnp.zeros((E, M), jnp.float32), 'W_up': jax.random.normal(ks[3], (E, D, M), jnp.float32) * std, 'b_up': jnp.zeros((E, M), jnp.float32), 'W_out': jax.random.normal(ks[4], (E, M, D), jnp.float32) * std, 'b_out': jnp.zeros((E, D), jnp.float32)}
    _L0_ffn_all = _L0_ffn_setup()
    _L0_ffn_in = {k: v for k, v in _L0_ffn_all.items() if k in ('W_router', 'W_gate', 'b_gate', 'W_up', 'b_up', 'W_out', 'b_out')}
    del _L0_ffn_all
    return {'x': x, 'cls_tok': cls_tok, 'L0_tok_weight': _L0_tok_in['weight'], 'L0_tok_weighted_sum': _L0_tok_in['weighted_sum'], 'L0_attn_w_qkv': _L0_attn_in['w_qkv'], 'L0_attn_b_qkv': _L0_attn_in['b_qkv'], 'L0_attn_w_out': _L0_attn_in['w_out'], 'L0_attn_b_out': _L0_attn_in['b_out'], 'L0_ffn_W_router': _L0_ffn_in['W_router'], 'L0_ffn_W_gate': _L0_ffn_in['W_gate'], 'L0_ffn_b_gate': _L0_ffn_in['b_gate'], 'L0_ffn_W_up': _L0_ffn_in['W_up'], 'L0_ffn_b_up': _L0_ffn_in['b_up'], 'L0_ffn_W_out': _L0_ffn_in['W_out'], 'L0_ffn_b_out': _L0_ffn_in['b_out']}

def reference(x, cls_tok, L0_tok_weight, L0_tok_weighted_sum, L0_attn_w_qkv, L0_attn_b_qkv, L0_attn_w_out, L0_attn_b_out, L0_ffn_W_router, L0_ffn_W_gate, L0_ffn_b_gate, L0_ffn_W_up, L0_ffn_b_up, L0_ffn_W_out, L0_ffn_b_out):
    import jax
    import jax.numpy as jnp

    def _L0_tok_ref(x, weight, weighted_sum):
        import jax, jax.numpy as jnp
        import numpy as np
        return jnp.einsum('bhid,oi,od->bho', x, weighted_sum, weight)

    def _L0_attn_ref(x, w_qkv, b_qkv, w_out, b_out):
        import jax, jax.numpy as jnp
        import numpy as np
        EMBED_DIM = 256
        NUM_HEADS = 16
        B, N, C = x.shape
        H = NUM_HEADS
        d = C // H
        scaling = C ** (-0.5)
        qkv = (jnp.einsum('bnc,oc->bno', x, w_qkv) + b_qkv).reshape(B, N, 3, H, d)
        q, k, v = (qkv[:, :, 0], qkv[:, :, 1], qkv[:, :, 2])
        attn_logits = jnp.einsum('bnhd,bngd->bnhg', q, k) * scaling
        attn_probs = jax.nn.softmax(attn_logits, axis=-1)
        attn_out = jnp.einsum('bnhg,bngd->bnhd', attn_probs, v)
        attn_out = jnp.transpose(attn_out, (0, 2, 1, 3)).reshape(B, N, C)
        return jnp.einsum('bnc,oc->bno', attn_out, w_out) + b_out

    def _L0_ffn_ref(residual, W_router, W_gate, b_gate, W_up, b_up, W_out, b_out):
        import jax, jax.numpy as jnp
        import numpy as np
        B, S, D = (2, 512, 256)
        M = 512
        E = 8
        TOP_K = 2
        router_logits = jnp.einsum('bsd,de->bse', residual, W_router)
        router_probs = jax.nn.softmax(router_logits, axis=-1)
        top_k_probs, top_k_idx = jax.lax.top_k(router_probs, TOP_K)
        top_k_probs = top_k_probs / (jnp.sum(top_k_probs, -1, keepdims=True) + 1e-08)
        one_hot = jax.nn.one_hot(top_k_idx, E, dtype=residual.dtype)
        expert_weights = jnp.einsum('bsk,bske->bse', top_k_probs, one_hot)
        gate = jax.nn.silu(jnp.einsum('bsd,edm->ebsm', residual, W_gate) + b_gate[:, None, None, :])
        up = jnp.einsum('bsd,edm->ebsm', residual, W_up) + b_up[:, None, None, :]
        hidden = gate * up
        expert_out = jnp.einsum('ebsm,emd->ebsd', hidden, W_out) + b_out[:, None, None, :]
        output = jnp.einsum('bse,ebsd->bsd', expert_weights, expert_out)
        return output
    h = _L0_tok_ref(x, L0_tok_weight, L0_tok_weighted_sum)
    h = jnp.concatenate([jnp.broadcast_to(cls_tok, (h.shape[0], 1, h.shape[2])), h], axis=1)
    h = h + _L0_attn_ref(_layernorm(h, axis=-1), L0_attn_w_qkv, L0_attn_b_qkv, L0_attn_w_out, L0_attn_b_out)
    h = h + _L0_ffn_ref(_layernorm(h, axis=-1), L0_ffn_W_router, L0_ffn_W_gate, L0_ffn_b_gate, L0_ffn_W_up, L0_ffn_b_up, L0_ffn_W_out, L0_ffn_b_out)
    return h

_drawn_inputs = setup_inputs


def setup_inputs(seed=0):
    import zlib

    import numpy as np

    out = dict(_drawn_inputs(seed))
    spreads = {'L0_attn_b_qkv': (0.0, 0.1),
     'L0_attn_b_out': (0.0, 0.1),
     'L0_ffn_b_gate': (0.0, 0.613),
     'L0_ffn_b_up': (0.0, 0.628),
     'L0_ffn_b_out': (0.0, 0.1)}
    factors = {}
    for name, (base, spread) in spreads.items():
        noise = np.random.default_rng([zlib.crc32(name.encode()), seed]).standard_normal(out[name].shape)
        drawn = base * np.exp(spread * noise) if base else spread * noise
        out[name] = jnp.asarray(drawn.astype(out[name].dtype))
    for name, factor in factors.items():
        out[name] = (out[name] * factor).astype(out[name].dtype)
    return out
```

```python
import concourse.bass as bass
from concourse import mybir
from contextlib import ExitStack

F32 = mybir.dt.float32
F16 = mybir.dt.float16
BF16 = mybir.dt.bfloat16
I32 = mybir.dt.int32
U32 = mybir.dt.uint32
ALU = mybir.AluOpType
ACT = mybir.ActivationFunctionType
AX = mybir.AxisListType

B, S, C, D1 = 8, 512, 256, 4
NH, HD = 16, 16
E, M, TOPK = 8, 512, 2
P = 128
KC = C // P
XC = C * D1 // P
MC = M // P
GU = KC * 2 * M
TPB = S // P
NT = B * TPB + 1
NTOK = B * (S + 1)
RING = 4
REG = NTOK + P
NJ = (NTOK * TOPK + E * (P - 1)) // P
ROW = C + 2
OUT_ROWS = NTOK * TOPK
FAR = 1 << 20
ZS = 256.0
WS = 16384.0
POOL_HEADS = 5
DVE_HEADS = NH - POOL_HEADS
SCALE = float(C) ** -0.5
EPS = 1e-5
T_IOTA, T_BASE, T_TARGET, T_FAR, T_PART, T_COLS = 0, E, 2 * E, 2 * E + 2, 2 * E + 3, 2 * E + 4


def tile_at(t, n):
    return (t // RING, t % RING) if 0 <= t < n else None


def pipeline(eng, n, ahead, behind, first, step, odd=0):
    loops = (n - odd - ahead - first) // RING
    for i in range(-ahead, first):
        u = i - (first - RING)
        step(lambda lag, i=i: tile_at(i - lag, n), u, -1)
    with eng.Fori(0, loops) as m:
        for u in range(RING):
            step(lambda lag, u=u: (m + (first + u - lag) // RING, (first + u - lag) % RING), u, m)
    for i in range(first + loops * RING, n + behind):
        step(lambda lag, i=i: tile_at(i - lag, n), None, None)


def wait(eng, sem, value):
    if not isinstance(value, int) or value > 0:
        eng.wait_ge(sem, value)


def apart(eng):
    eng.nop(nofuse=True)


class Chain:

    def __init__(self, eng, sem, per):
        self.eng, self.sem, self.per = eng, sem, per

    def start(self, n):
        self.base, self.k = n * self.per, 0

    def link(self, ins):
        ins.then_inc(self.sem, 1)
        self.k += 1
        assert self.k <= self.per
        self.eng.wait_ge(self.sem, self.base + self.k)


def is_cls(ts):
    return isinstance(ts[0], int) and ts[0] * RING + ts[1] == NT - 1


def rows_of(ts):
    return B if is_cls(ts) else P


def rows_at(ap, start, n):
    return ap[start:start + n, :] if isinstance(start, int) else ap[bass.ds(start, n), :]


def dyn_row(ap, n):
    if isinstance(n, int):
        return ap[n]
    return ap[bass.ds(n, 1)].rearrange("a p n -> (a p) n")


def vit_block(nc, x_t, cls, tok_w, tok_ws, w_qkv, b_qkv, w_o, b_o, w_router, w_gu, b_gate, b_up,
              w_down, b_down, ident, upper, table, steps, out):
    with ExitStack() as ctx:
        ctx.enter_context(nc.allow_low_precision("fp16 halves of fp32 values; masks of zeros and ones"))

        def sb(name, shape, dt=F32):
            return ctx.enter_context(nc.sbuf_tensor(name, shape, dt))

        routed = nc.dram_tensor("routed", [E * REG + P, ROW], F32, kind="Internal").ap()
        expert_out = nc.dram_tensor("expert_out", [OUT_ROWS, C], F32, kind="Internal").ap()
        h_dram = nc.dram_tensor("h_dram", [NTOK, C], F32, kind="Internal").ap()
        att_dram = nc.dram_tensor("att_dram", [B, NH, S + 1, HD], F32, kind="Internal").ap()
        h2_dram = nc.dram_tensor("h2_dram", [NTOK, C], F32, kind="Internal").ap()

        kept = dict(
            gu_hi=sb("gu_hi", [P, E * GU], F16),
            gu_lo=sb("gu_lo", [P, E * GU], F16),
            down=sb("down", [P, E * MC * C]),
            bg=sb("bg", [P, E * MC]),
            bu=sb("bu", [P, E * MC]),
            bd=sb("bd", [P, E * C]),
            inv_scale=sb("inv_scale", [P, E]),
            id16=sb("id16", [P, P], F16),
            step_tab=sb("step_tab", [1, 2 * NJ], I32),
            banks=[ctx.enter_context(nc.psum_tensor(f"bank{i}", [P, 512], F32)) for i in range(8)],
        )
        attend_stage(nc, kept["banks"], x_t, cls, tok_w, tok_ws, w_qkv, b_qkv, ident, h_dram, att_dram)
        route_stage(nc, kept, w_o, b_o, w_router, w_gu, b_gate, b_up, w_down, b_down, ident, upper, table, steps,
                    h_dram, att_dram, routed, h2_dram)
        expert_stage(nc, kept, routed, expert_out)
        combine_stage(nc, expert_out, h2_dram, out)


def attend_stage(nc, banks, x_t, cls, tok_w, tok_ws, w_qkv, b_qkv, ident, h_dram, att_dram):
    H_BANK, QK_BANK, V_BANK, Z1T_BANK = banks[0:4]
    with ExitStack() as ctx:
        def sb(name, shape, dt=F32):
            return ctx.enter_context(nc.sbuf_tensor(name, shape, dt))

        def sem(name):
            return ctx.enter_context(nc.semaphore(name))

        xs = sb("xs", [P, 2, XC * P])
        wtok = sb("wtok", [P, XC, C])
        wqkv = sb("wqkv", [P, KC, 3 * C])
        bqkv = sb("bqkv", [1, 3 * C])
        id32 = sb("id32", [P, P])
        ones_row = sb("ones_row", [1, P])
        half = sb("half", [P, 1])
        h = sb("h", [P, RING, C])
        stats = sb("stats", [P, 6])
        mv = sb("mv", [P, 2, 2])
        rstd = sb("rstd", [P, 2, 2])
        z1 = sb("z1", [P, 2, C])
        z1t = sb("z1t", [P, 2, KC, P])
        qkv = sb("qkv", [P, RING, 3 * C])
        prod = sb("prod", [P, DVE_HEADS * NH * HD])
        tokw = prod[:, 0:D1 * C].rearrange("p (d c) -> p d c", d=D1)
        tokws = prod[:, D1 * C:(D1 + KC) * C].rearrange("p (k c) -> p k c", k=KC)
        pq = sb("pq", [P, POOL_HEADS * NH * HD])
        pv = sb("pv", [P, POOL_HEADS * NH * HD])
        logits = sb("logits", [P, 2, NH * NH])
        lmax = sb("lmax", [P, NH])
        prob = sb("prob", [P, 2, NH * NH])
        psums = sb("psums", [P, 2, NH])
        att = sb("att", [P, RING, C])

        first_consts, consts = sem("first_consts"), sem("consts")
        filled, wtok_ready = sem("filled"), sem("wtok_ready")
        x_loaded = [sem("x_loaded0"), sem("x_loaded1")]
        cls_loaded, h_done, h_copied = sem("cls_loaded"), sem("h_done"), sem("h_copied")
        stats_done, eps_added, rstd_done, z1_done = (sem(n) for n in ("stats_done", "eps_added", "rstd_done", "z1_done"))
        z1t_done, z1t_copied = sem("z1t_done"), sem("z1t_copied")
        qkv_done, qkv_copied = sem("qkv_done"), sem("qkv_copied")
        pq_done, logits_done, prob_done, pv_done = sem("pq_done"), sem("logits_done"), sem("prob_done"), sem("pv_done")
        att_done = sem("att_done")
        h_stored = [sem(f"h_stored{s}") for s in range(RING)]
        att_stored = [sem(f"att_stored{s}") for s in range(RING)]
        links = {n: sem(f"{n}_link") for n in ("stats", "qk", "pv")}

        N_CONSTS = 16 * 3
        block = ctx.enter_context(nc.Block())

        @block.sync
        def _(sp):
            def load(dst, src, s):
                sp.dma_start(dst, src).then_inc(s, 16)

            load(tokw[:, :, :], tok_w.unsqueeze(0).broadcast_to([P, D1, C]), first_consts)
            load(tokws[:, :, :], tok_ws, first_consts)
            for t in range(2):
                load(xs[:, t, :], x_t[t], x_loaded[t])
            load(id32[:, :], ident, consts)
            load(wqkv[:, :, :], w_qkv, consts)
            load(bqkv[:, :], b_qkv, consts)

            def step(at, u, m):
                if ts := at(-1):
                    q, s = ts
                    n = q * RING + s
                    if is_cls(ts):
                        sp.wait_ge(h_stored[s], 16 * q)
                        sp.wait_ge(z1_done, n - 3)
                        load(h[0:B, s, :], cls.broadcast_to([B, C]), cls_loaded)
                    elif not isinstance(n, int) or n >= 2:
                        wait(sp, h_done, n - 1)
                        load(xs[:, s % 2, :], dyn_row(x_t, n), x_loaded[s % 2])
                if ts := at(0):
                    (q, s), r = ts, rows_of(ts)
                    n = q * RING + s
                    if is_cls(ts):
                        sp.wait_ge(cls_loaded, 16)
                    else:
                        sp.wait_ge(h_copied, n + 1)
                    sp.dma_start(rows_at(h_dram, n * P, r), h[0:r, s, :]).then_inc(h_stored[s], 16)
                if ts := at(3):
                    (q, s), r = ts, rows_of(ts)
                    n = q * RING + s
                    sp.wait_ge(att_done, n + 1)
                    if is_cls(ts):
                        dst = att_dram[:, :, 0, :]
                    else:
                        dst = att_dram[q] if isinstance(q, int) else att_dram[bass.ds(q, 1)].rearrange("b h n d -> (b h) n d")
                        dst = dst[:, 1:, :].rearrange("h (p t) d -> p t h d", t=TPB)[:, s, :, :]
                    sp.dma_start(dst, att[0:r, s, :].rearrange("p (h d) -> p h d", h=NH)).then_inc(att_stored[s], 16)

            pipeline(sp, NT, 1, 3, RING + 1, step, odd=1)
            for s in range(RING):
                tiles = (NT - 1 - s) // RING + 1
                sp.wait_ge(h_stored[s], 16 * tiles)
                sp.wait_ge(att_stored[s], 16 * tiles)

        @block.gpsimd
        def _(pool):
            pool.memset(half[:, :], -0.5).then_inc(filled, 1)
            pool.memset(ones_row[:, :], 1.0).then_inc(filled, 1)
            pool.wait_ge(filled, 1)

            def inverse_root(ts, ready, used, added, done, m, r_):
                (q, s), r = ts, rows_of(ts)
                n = q * RING + s
                pool.wait_ge(ready, n + 1)
                wait(pool, used, n - 1)
                apart(pool)
                pool.tensor_scalar(r_[0:r, s % 2, 0:1], m[0:r, s % 2, 1:2], EPS, None, ALU.add).then_inc(added, 1)
                pool.wait_ge(added, n + 1)
                pool.tensor_tensor(r_[0:r, s % 2, 1:2], r_[0:r, s % 2, 0:1], half[0:r, :], ALU.pow).then_inc(done, 1)

            def step(at, u, m):
                if ts := at(0):
                    inverse_root(ts, stats_done, z1_done, eps_added, rstd_done, mv, rstd)
                if ts := at(1):
                    (q, s), r = ts, rows_of(ts)
                    n = q * RING + s
                    pool.wait_ge(qkv_copied, n + 1)
                    wait(pool, logits_done, n)
                    q_ = qkv[0:r, s, DVE_HEADS * HD:C].rearrange("p (h d) -> p h d", h=POOL_HEADS)
                    k_ = qkv[0:r, s, C:2 * C].rearrange("p (g d) -> p g d", g=NH)
                    pool.tensor_tensor(
                        pq[0:r, :].rearrange("p (h g d) -> p h g d", h=POOL_HEADS, g=NH),
                        q_.unsqueeze(2).broadcast_to([r, POOL_HEADS, NH, HD]),
                        k_.unsqueeze(1).broadcast_to([r, POOL_HEADS, NH, HD]), ALU.mult).then_inc(pq_done, 1)
                if ts := at(2):
                    (q, s), r = ts, rows_of(ts)
                    n = q * RING + s
                    pool.wait_ge(prob_done, n + 1)
                    wait(pool, att_done, n)
                    p_ = prob[0:r, s % 2, DVE_HEADS * NH:].rearrange("p (h g) -> p h g", h=POOL_HEADS)
                    v_ = qkv[0:r, s, 2 * C:].rearrange("p (d g) -> p d g", g=NH)
                    pool.tensor_tensor(
                        pv[0:r, :].rearrange("p (h d g) -> p h d g", h=POOL_HEADS, d=HD),
                        p_.unsqueeze(2).broadcast_to([r, POOL_HEADS, HD, NH]),
                        v_.unsqueeze(1).broadcast_to([r, POOL_HEADS, HD, NH]), ALU.mult).then_inc(pv_done, 1)

            pipeline(pool, NT, 1, 3, RING + 1, step, odd=1)

        @block.scalar
        def _(act):
            def copy(done, dst, src):
                act.activation(dst, src, ACT.Copy).then_inc(done, 1)

            def step(at, u, m):
                if ts := at(0):
                    (q, s), r = ts, rows_of(ts)
                    n = q * RING + s
                    act.wait_ge(z1t_done, n + 1)
                    wait(act, qkv_done, n - 1)
                    copy(z1t_copied, z1t[:, s % 2, :, 0:r], Z1T_BANK[:, 0:KC * P].rearrange("p (k t) -> p k t", k=KC)[:, :, 0:r])
                if (ts := at(-1)) and not is_cls(ts):
                    q, s = ts
                    n = q * RING + s
                    act.wait_ge(h_done, n + 1)
                    wait(act, h_stored[s], 16 * q)
                    wait(act, z1_done, n - 3)
                    copy(h_copied, h[:, s, :], H_BANK[:, 0:C])
                if ts := at(0):
                    (q, s), r = ts, rows_of(ts)
                    n = q * RING + s
                    act.wait_ge(qkv_done, n + 1)
                    wait(act, att_done, n - 3)
                    wait(act, pv_done, n - 3)
                    act.activation(qkv[0:r, s, 0:2 * C], QK_BANK[0:r, :], ACT.Copy)
                    copy(qkv_copied, qkv[0:r, s, 2 * C:], V_BANK[0:r, 0:C])
                if ts := at(1):
                    (q, s), r = ts, rows_of(ts)
                    n = q * RING + s
                    act.wait_ge(logits_done, n + 1)
                    wait(act, att_done, n - 1)
                    wait(act, pv_done, n - 1)
                    act.activation(prob[0:r, s % 2, :], logits[0:r, s % 2, :], ACT.Exp, scale=SCALE).then_inc(prob_done, 1)

            pipeline(act, NT, 1, 3, RING + 1, step, odd=1)

        @block.tensor
        def _(pe):
            def step(at, u, m):
                if (ts := at(-1)) and not is_cls(ts):
                    q, s = ts
                    n = q * RING + s
                    pe.wait_ge(x_loaded[s % 2], 16 * (2 * q + s // 2 + 1))
                    wait(pe, h_copied, n)
                    for c in range(XC):
                        last = pe.matmul(H_BANK[:, 0:C], xs[:, s % 2, c * P:(c + 1) * P], wtok[:, c, :],
                                         start=c == 0, stop=c == XC - 1)
                    last.then_inc(h_done, 1)
                if ts := at(0):
                    (q, s), r = ts, rows_of(ts)
                    n = q * RING + s
                    pe.wait_ge(z1_done, n + 1)
                    wait(pe, z1t_copied, n)
                    for c in range(KC):
                        last = pe.transpose(Z1T_BANK[:, c * P:c * P + r], z1[0:r, s % 2, c * P:(c + 1) * P], id32[0:r, 0:r])
                    last.then_inc(z1t_done, 1)
                    pe.wait_ge(z1t_copied, n + 1)
                    wait(pe, qkv_copied, n)
                    for bank, lo, hi in ((QK_BANK, 0, 2 * C), (V_BANK, 2 * C, 3 * C)):
                        pe.matmul(bank[0:r, 0:hi - lo], ones_row[:, 0:r], bqkv[:, lo:hi], start=True, stop=False)
                        for c in range(KC):
                            last = pe.matmul(bank[0:r, 0:hi - lo], z1t[:, s % 2, c, 0:r], wqkv[:, c, lo:hi],
                                             start=False, stop=c == KC - 1)
                    last.then_inc(qkv_done, 1)

            pe.wait_ge(wtok_ready, XC)
            pe.wait_ge(consts, N_CONSTS)
            pe.wait_ge(filled, 2)
            pipeline(pe, NT, 1, 3, RING + 1, step, odd=1)

        @block.vector
        def _(dve):
            chain = {n: Chain(dve, links[n], per) for n, per in dict(stats=1, qk=3, pv=5).items()}

            dve.wait_ge(first_consts, 32)
            for d in range(D1):
                for c in range(KC):
                    dve.tensor_tensor(wtok[:, d * KC + c, :], tokws[:, c, :], tokw[:, d, :], ALU.mult).then_inc(wtok_ready, 1)
            dve.wait_ge(wtok_ready, XC)

            def stats_of(ts):
                (q, s), r = ts, rows_of(ts)
                n = q * RING + s
                if is_cls(ts):
                    dve.wait_ge(cls_loaded, 16)
                else:
                    dve.wait_ge(h_copied, n + 1)
                chain["stats"].start(n)
                chain["stats"].link(dve.bn_stats(stats[0:r, :], h[0:r, s, :]))
                apart(dve)
                dve.bn_aggr(mv[0:r, s % 2, :], stats[0:r, :]).then_inc(stats_done, 1)

            def normalise(ts):
                (q, s), r = ts, rows_of(ts)
                n = q * RING + s
                dve.wait_ge(rstd_done, n + 1)
                wait(dve, z1t_done, n - 1)
                dve.tensor_scalar(z1[0:r, s % 2, :], h[0:r, s, :], mv[0:r, s % 2, 0:1], rstd[0:r, s % 2, 1:2],
                                  ALU.subtract, ALU.mult).then_inc(z1_done, 1)

            def qk_product(ts):
                (q, s), r = ts, rows_of(ts)
                n = q * RING + s
                dve.wait_ge(qkv_copied, n + 1)
                chain["qk"].start(n)
                q_ = qkv[0:r, s, 0:DVE_HEADS * HD].rearrange("p (h d) -> p h d", h=DVE_HEADS)
                k_ = qkv[0:r, s, C:2 * C].rearrange("p (g d) -> p g d", g=NH)
                chain["qk"].link(dve.tensor_tensor(
                    prod[0:r, :].rearrange("p (h g d) -> p h g d", h=DVE_HEADS, g=NH),
                    q_.unsqueeze(2).broadcast_to([r, DVE_HEADS, NH, HD]),
                    k_.unsqueeze(1).broadcast_to([r, DVE_HEADS, NH, HD]), ALU.mult))

            def qk_reduce(ts):
                (q, s), r = ts, rows_of(ts)
                n = q * RING + s
                c = chain["qk"]
                c.base, c.k = n * c.per, 1
                wait(dve, prob_done, n - 1)
                lg = logits[0:r, s % 2, :]
                dve.tensor_reduce(lg[:, 0:DVE_HEADS * NH], prod[0:r, :].rearrange("p (a d) -> p a d", d=HD), AX.X, ALU.add)
                dve.wait_ge(pq_done, n + 1)
                c.link(dve.tensor_reduce(lg[:, DVE_HEADS * NH:], pq[0:r, :].rearrange("p (a d) -> p a d", d=HD), AX.X, ALU.add))
                lg = lg.rearrange("p (h g) -> p h g", h=NH)
                c.link(dve.tensor_reduce(lmax[0:r, :], lg, AX.X, ALU.max))
                dve.tensor_tensor(lg, lg, lmax[0:r, :].unsqueeze(2).broadcast_to([r, NH, NH]), ALU.subtract).then_inc(logits_done, 1)

            def attend(ts):
                (q, s), r = ts, rows_of(ts)
                n = q * RING + s
                c = chain["pv"]
                c.start(n)
                dve.wait_ge(prob_done, n + 1)
                p_ = prob[0:r, s % 2, :].rearrange("p (h g) -> p h g", h=NH)
                v_ = qkv[0:r, s, 2 * C:].rearrange("p (d g) -> p d g", g=NH)
                dve.tensor_tensor(
                    prod[0:r, :].rearrange("p (h d g) -> p h d g", h=DVE_HEADS, d=HD),
                    p_[:, 0:DVE_HEADS, :].unsqueeze(2).broadcast_to([r, DVE_HEADS, HD, NH]),
                    v_.unsqueeze(1).broadcast_to([r, DVE_HEADS, HD, NH]), ALU.mult).then_inc(c.sem, 1)
                c.k = 1
                c.link(dve.tensor_reduce(psums[0:r, 0, :], p_, AX.X, ALU.add))
                c.link(dve.reciprocal(psums[0:r, 1, :], psums[0:r, 0, :]))
                wait(dve, att_stored[s], 16 * q)
                a = att[0:r, s, :]
                c.link(dve.tensor_reduce(a[:, 0:DVE_HEADS * HD], prod[0:r, :].rearrange("p (a g) -> p a g", g=NH), AX.X, ALU.add))
                dve.wait_ge(pv_done, n + 1)
                c.link(dve.tensor_reduce(a[:, DVE_HEADS * HD:], pv[0:r, :].rearrange("p (a g) -> p a g", g=NH), AX.X, ALU.add))
                a = a.rearrange("p (h d) -> p h d", h=NH)
                dve.tensor_tensor(a, a, psums[0:r, 1, :].unsqueeze(2).broadcast_to([r, NH, HD]), ALU.mult).then_inc(att_done, 1)

            def step(at, u, m):
                if ts := at(0):
                    stats_of(ts)
                if ts := at(1):
                    qk_product(ts)
                if ts := at(0):
                    normalise(ts)
                if ts := at(1):
                    qk_reduce(ts)
                if ts := at(2):
                    attend(ts)

            pipeline(dve, NT, 1, 3, RING + 1, step, odd=1)


def route_stage(nc, kept, w_o, b_o, w_router, w_gu, b_gate, b_up, w_down, b_down, ident, upper, table, steps,
                h_dram, att_dram, routed, h2_dram):
    gu_hi, gu_lo, inv_scale, id16 = kept["gu_hi"], kept["gu_lo"], kept["inv_scale"], kept["id16"]
    bu, step_tab, banks = kept["bu"], kept["step_tab"], kept["banks"]
    ATTT_BANK, Y_BANK, Z2T_BANK, RL_BANK, R_BANK = banks[0:5]
    with ExitStack() as ctx:
        def sb(name, shape, dt=F32):
            return ctx.enter_context(nc.sbuf_tensor(name, shape, dt))

        def sem(name):
            return ctx.enter_context(nc.semaphore(name))

        wo = sb("wo", [P, KC, C])
        bo = sb("bo", [1, C])
        wr = sb("wr", [P, KC, E])
        gu_in = sb("gu_in", [P, GU])
        tab = sb("tab", [P, T_COLS])
        id32 = sb("id32b", [P, P])
        upper32 = sb("upper32", [P, P])
        upper16 = sb("upper16", [P, P], BF16)
        ones16 = sb("ones16", [P, P], BF16)
        ones_row = sb("ones_row_b", [1, P])
        half = sb("half_b", [P, 1])
        steps_in = sb("steps_in", [1, NJ + NT + 1])
        sel = sb("sel", [1, 3, NJ, E])
        tiles_cmp = sb("tiles_cmp", [1, E, NT + 1])
        step_f = sb("step_f", [1, 4, NJ])
        h = sb("h_ring", [P, RING, C])
        att = sb("att_rows", [P, RING, C])
        attt = sb("attt", [P, 2, KC, P])
        stats2 = sb("stats2", [P, 6])
        mv2 = sb("mv2", [P, 2, 2])
        rstd2 = sb("rstd2", [P, 2, 2])
        z2 = sb("z2", [P, 2, C])
        z2t = sb("z2t", [P, 2, KC, P])
        zx = sb("zx", [P, 2, TOPK, ROW])
        rl = sb("rl", [P, E])
        top = sb("top", [P, 2, E])
        neg_top = sb("neg_top", [P, 2, 1])
        ex = sb("ex", [P, 2, E + 1])
        top_i = sb("top_i", [P, E], U32)
        top_f = sb("top_f", [P, TOPK])
        rsum = sb("rsum", [P, 1])
        pk = sb("pk", [P, TOPK])
        den = sb("den", [P, 2])
        mask = sb("mask", [P, 2, TOPK, E])
        mask16 = sb("mask16", [P, 2, E], BF16)
        count = sb("count", [P, E])
        ranks = sb("ranks", [P, E])
        ranked = sb("ranked", [P, TOPK, E])
        slot_f = sb("slot_f", [P, TOPK])
        slot = sb("slot", [P, 2, TOPK], U32)
        target = sb("target", [P, TOPK])
        gmax = sb("gmax", [P, 5])
        pad_row = sb("pad_row", [P, ROW])
        pad_f = sb("pad_f", [P, E + 1])
        pad_slot = sb("pad_slot", [P, E + 1], U32)
        n_f = sb("n_f", [1, 5, E])

        consts, filled, cast, pads_filled = sem("consts_b"), sem("filled_b"), sem("cast"), sem("pads_filled")
        h_loaded = [sem(f"h_loaded{s}") for s in range(RING)]
        att_loaded = [sem(f"att_loaded{s}") for s in range(RING)]
        h2_stored = [sem(f"h2_stored{s}") for s in range(RING)]
        attt_done, attt_copied, y_done, h2_done = sem("attt_done"), sem("attt_copied"), sem("y_done"), sem("h2_done")
        stats2_done, eps2_added, rstd2_done, z2_done = (sem(n) for n in ("stats2_done", "eps2_added", "rstd2_done", "z2_done"))
        z2t_done, z2t_copied, rl_done, rl_read = sem("z2t_done"), sem("z2t_copied"), sem("rl_done"), sem("rl_read")
        sorted_done, ex_done, zx_done = sem("sorted_done"), sem("ex_done"), sem("zx_done")
        mask_done, rank_done, slot_done, rank_read = sem("mask_done"), sem("rank_done"), sem("slot_done"), sem("rank_read")
        scattered = [sem("scattered0"), sem("scattered1")]
        gu_loaded, gmax_done, gmax_all = sem("gu_loaded"), sem("gmax_done"), sem("gmax_all")
        scale_done, gu_hi_done, gu_split = sem("scale_done"), sem("gu_hi_done"), sem("gu_split")
        pad_slots_done, padded, expert_loaded = sem("pad_slots_done"), sem("padded"), sem("expert_loaded")
        links = {n: sem(f"{n}_link") for n in ("stats2", "zx", "sort", "weight", "slot", "scale", "table")}

        N_CONSTS = 16 * 8
        block = ctx.enter_context(nc.Block())

        @block.sync
        def _(sp):
            def load(dst, src, s):
                sp.dma_start(dst, src).then_inc(s, 16)

            load(id32[:, :], ident, consts)
            load(wo[:, :, :], w_o, consts)
            load(bo[:, :], b_o, consts)
            load(gu_in[:, :], w_gu[0], gu_loaded)
            load(wr[:, :, :], w_router, consts)
            load(tab[:, :], table, consts)
            load(steps_in[:, :], steps, consts)
            load(upper32[:, :], upper, consts)
            load(bu[:, :], b_up, consts)

            def step(at, u, m):
                if ts := at(-1):
                    (q, s), r = ts, rows_of(ts)
                    n = q * RING + s
                    wait(sp, h2_stored[s], 16 * q)
                    apart(sp)
                    wait(sp, z2_done, n - 3)
                    sp.dma_start(h[0:r, s, :], rows_at(h_dram, n * P, r)).then_inc(h_loaded[s], 16)
                    wait(sp, attt_done, n - 3)
                    if is_cls(ts):
                        src = att_dram.rearrange("b h n d -> b (h n d)")[:, 0:C]
                    else:
                        src = rows_at(att_rows, q * (S + 1) + 1, S).rearrange("(p t) c -> p t c", t=TPB)[:, s, :]
                    sp.dma_start(att[0:r, s, :], src).then_inc(att_loaded[s], 16)
                if u == 0:
                    sp.wait_ge(gu_split, m + 2)
                    sp.dma_start(gu_in[:, :], dyn_row(w_gu, m + 2)).then_inc(gu_loaded, 16)
                if ts := at(2):
                    (q, s), r = ts, rows_of(ts)
                    n = q * RING + s
                    sp.wait_ge(h2_done, n + 1)
                    sp.dma_start(rows_at(h2_dram, n * P, r), h[0:r, s, :]).then_inc(h2_stored[s], 16)

            att_rows = att_dram.rearrange("b h n d -> (b h n d)").rearrange("(r c) -> r c", c=C)
            pipeline(sp, NT, 1, RING, RING + 1, step, odd=1)
            load(kept["bg"][:, :], b_gate, expert_loaded)
            load(kept["down"][:, :], w_down, expert_loaded)
            load(kept["bd"][:, :], b_down.broadcast_to([P, E * C]), expert_loaded)
            for s in range(RING):
                sp.wait_ge(h2_stored[s], 16 * ((NT - 1 - s) // RING + 1))
            sp.wait_ge(expert_loaded, 48)

        @block.gpsimd
        def _(pool):
            pool.memset(half[:, :], -0.5).then_inc(filled, 1)
            pool.memset(ones16[:, :], 1.0).then_inc(filled, 1)
            pool.memset(ones_row[:, :], 1.0).then_inc(filled, 1)
            pool.memset(pad_row[:, :], 0.0).then_inc(pads_filled, 1)
            pool.wait_ge(pads_filled, 1)
            pool.wait_ge(consts, N_CONSTS)
            pool.tensor_copy(pad_row[:, ROW - 1:ROW].bitcast(U32), tab[:, T_FAR:T_FAR + 1]).then_inc(pads_filled, 1)
            pool.tensor_copy(upper16[:, :], upper32[:, :]).then_inc(cast, 1)
            pool.tensor_copy(id16[:, :], id32[:, :]).then_inc(cast, 1)

            def weight_max(e):
                pool.wait_ge(gmax_done, e + 1)
                apart(pool)
                pool.partition_all_reduce(gmax[:, 1:2], gmax[:, 0:1], P, bass.bass_isa.ReduceOp.max).then_inc(gmax_all, 1)

            def inverse_root(ts, ready, used, added, done, m, r_):
                (q, s), r = ts, rows_of(ts)
                n = q * RING + s
                pool.wait_ge(ready, n + 1)
                wait(pool, used, n - 1)
                apart(pool)
                pool.tensor_scalar(r_[0:r, s % 2, 0:1], m[0:r, s % 2, 1:2], EPS, None, ALU.add).then_inc(added, 1)
                pool.wait_ge(added, n + 1)
                pool.tensor_tensor(r_[0:r, s % 2, 1:2], r_[0:r, s % 2, 0:1], half[0:r, :], ALU.pow).then_inc(done, 1)

            def step(at, u, m):
                if ts := at(1):
                    inverse_root(ts, stats2_done, z2_done, eps2_added, rstd2_done, mv2, rstd2)
                if u == 1:
                    weight_max(m + 2)
                if ts := at(3):
                    (q, s), r = ts, rows_of(ts)
                    pool.wait_ge(zx_done, q * RING + s + 1)
                    pool.wait_ge(slot_done, q * RING + s + 1)
                    apart(pool)
                    for k in range(TOPK):
                        pool.indirect_dma_start(
                            out=routed[:, :], out_offset=bass.IndirectOffsetOnAxis(ap=slot[0:r, s % 2, k:k + 1], axis=0),
                            in_=zx[0:r, s % 2, k, :], in_offset=None).then_inc(scattered[s % 2], 16)

            weight_max(0)
            pipeline(pool, NT, 1, RING, RING + 1, step, odd=1)
            pool.wait_ge(pads_filled, 2)
            pool.wait_ge(pad_slots_done, 1)
            for e in range(E + 1):
                pool.indirect_dma_start(
                    out=routed[:, :], out_offset=bass.IndirectOffsetOnAxis(ap=pad_slot[:, e:e + 1], axis=0),
                    in_=pad_row[:, :], in_offset=None).then_inc(padded, 16)
            pool.wait_ge(padded, 16 * (E + 1))
            pool.wait_ge(scattered[0], 16 * TOPK * ((NT + 1) // 2))
            pool.wait_ge(scattered[1], 16 * TOPK * (NT // 2))

        @block.scalar
        def _(act):
            def copy(done, dst, src):
                act.activation(dst, src, ACT.Copy).then_inc(done, 1)

            def split_high(e):
                act.wait_ge(scale_done, e + 1)
                dst = gu_hi[:, e * GU:(e + 1) * GU] if isinstance(e, int) else gu_hi[:, bass.ds(e * GU, GU)]
                act.activation(dst, gu_in[:, :], ACT.Copy, scale=gmax[:, 4:5]).then_inc(gu_hi_done, 1)

            def step(at, u, m):
                if ts := at(2):
                    (q, s), r = ts, rows_of(ts)
                    n = q * RING + s
                    act.wait_ge(sorted_done, n + 1)
                    wait(act, zx_done, n - 1)
                    act.activation(ex[0:r, s % 2, 0:E], top[0:r, s % 2, :], ACT.Exp, bias=neg_top[0:r, s % 2, :],
                                   accum_out=ex[0:r, s % 2, E:E + 1]).then_inc(ex_done, 1)
                if ts := at(1):
                    (q, s), r = ts, rows_of(ts)
                    n = q * RING + s
                    act.wait_ge(z2t_done, n + 1)
                    wait(act, rl_done, n - 1)
                    copy(z2t_copied, z2t[:, s % 2, :, 0:r], Z2T_BANK[:, 0:KC * P].rearrange("p (k t) -> p k t", k=KC)[:, :, 0:r])
                if ts := at(0):
                    (q, s), r = ts, rows_of(ts)
                    n = q * RING + s
                    act.wait_ge(attt_done, n + 1)
                    wait(act, y_done, n - 1)
                    copy(attt_copied, attt[:, s % 2, :, 0:r], ATTT_BANK[:, 0:KC * P].rearrange("p (k t) -> p k t", k=KC)[:, :, 0:r])
                if u == 2:
                    split_high(m + 2)

            split_high(0)
            pipeline(act, NT, 1, RING, RING + 1, step, odd=1)

        @block.tensor
        def _(pe):
            def transpose(bank, src, r):
                for c in range(KC):
                    last = pe.transpose(bank[:, c * P:c * P + r], src[0:r, c * P:(c + 1) * P], id32[0:r, 0:r])
                return last

            def step(at, u, m):
                if ts := at(3):
                    (q, s), r = ts, rows_of(ts)
                    n = q * RING + s
                    pe.wait_ge(mask_done, n + 1)
                    wait(pe, rank_read, n)
                    pe.matmul(R_BANK[0:r, E:2 * E], upper16[0:r, 0:r], mask16[0:r, s % 2, :], start=True, stop=True)
                    pe.matmul(R_BANK[:, 2 * E:3 * E], ones16[0:r, :], mask16[0:r, s % 2, :], start=True, stop=True).then_inc(rank_done, 1)
                if ts := at(1):
                    (q, s), r = ts, rows_of(ts)
                    n = q * RING + s
                    pe.wait_ge(z2_done, n + 1)
                    wait(pe, z2t_copied, n)
                    transpose(Z2T_BANK, z2[:, s % 2, :], r).then_inc(z2t_done, 1)
                    pe.wait_ge(z2t_copied, n + 1)
                    wait(pe, rl_read, n)
                    for c in range(KC):
                        last = pe.matmul(RL_BANK[0:r, 0:E], z2t[:, s % 2, c, 0:r], wr[:, c, :], start=c == 0, stop=c == KC - 1)
                    last.then_inc(rl_done, 1)
                if ts := at(0):
                    (q, s), r = ts, rows_of(ts)
                    n = q * RING + s
                    pe.wait_ge(att_loaded[s], 16 * (q + 1))
                    wait(pe, attt_copied, n)
                    transpose(ATTT_BANK, att[:, s, :], r).then_inc(attt_done, 1)
                    pe.wait_ge(attt_copied, n + 1)
                    wait(pe, h2_done, n)
                    pe.matmul(Y_BANK[0:r, 0:C], ones_row[:, 0:r], bo[:, :], start=True, stop=False)
                    for c in range(KC):
                        last = pe.matmul(Y_BANK[0:r, 0:C], attt[:, s % 2, c, 0:r], wo[:, c, :], start=False, stop=c == KC - 1)
                    last.then_inc(y_done, 1)

            pe.wait_ge(consts, N_CONSTS)
            pe.wait_ge(cast, 2)
            pe.wait_ge(filled, 3)
            pipeline(pe, NT, 1, RING, RING + 1, step, odd=1)

        @block.vector
        def _(dve):
            chain = {n: Chain(dve, links[n], per) for n, per in
                     dict(stats2=1, zx=2, sort=5, weight=5, slot=3, scale=4, table=40).items()}
            dve.wait_ge(consts, N_CONSTS)
            dve.tensor_copy(count[:, :], tab[:, T_BASE:T_BASE + E])
            dve.tensor_copy(target[:, :], tab[:, T_TARGET:T_TARGET + TOPK])

            def weight_size(e):
                dve.wait_ge(gu_loaded, 16 * (e + 1))
                dve.tensor_reduce(gmax[:, 0:1], gu_in[:, :], AX.X, ALU.max, apply_absolute_value=True).then_inc(gmax_done, 1)

            def weight_scale(e):
                c = chain["scale"]
                c.start(e)
                dve.wait_ge(gmax_all, e + 1)
                c.link(dve.tensor_scalar(gmax[:, 2:3].bitcast(U32), gmax[:, 1:2].bitcast(U32), 0x7F800000, None, ALU.bitwise_and))
                c.link(dve.tensor_scalar(gmax[:, 2:3], gmax[:, 2:3], 2.0 ** -60, None, ALU.max))
                c.link(dve.reciprocal(gmax[:, 3:4], gmax[:, 2:3]))
                c.link(dve.tensor_scalar(gmax[:, 4:5], gmax[:, 3:4], WS, None, ALU.mult))
                inv = inv_scale[:, e:e + 1] if isinstance(e, int) else inv_scale[:, bass.ds(e, 1)]
                b = bu[:, e * MC:(e + 1) * MC] if isinstance(e, int) else bu[:, bass.ds(e * MC, MC)]
                dve.tensor_scalar(inv, gmax[:, 2:3], 1.0 / (WS * ZS), None, ALU.mult)
                dve.tensor_scalar(b, b, gmax[:, 4:5], ZS, ALU.mult, ALU.mult).then_inc(scale_done, 1)

            def split_low(e):
                dve.wait_ge(gu_hi_done, e + 1)
                lo, hi = ((t[:, e * GU:(e + 1) * GU] if isinstance(e, int) else t[:, bass.ds(e * GU, GU)]) for t in (gu_lo, gu_hi))
                dve.scalar_tensor_tensor(lo, gu_in[:, :], gmax[:, 4:5], hi, ALU.mult, ALU.subtract).then_inc(gu_split, 1)

            def slots_of(ts):
                (q, s), r = ts, rows_of(ts)
                n = q * RING + s
                c = chain["slot"]
                c.start(n)
                dve.wait_ge(rank_done, n + 1)
                c.link(dve.tensor_tensor(ranks[0:r, :], R_BANK[0:r, E:2 * E], count[0:r, :], ALU.add))
                c.link(dve.tensor_tensor(ranked[0:r, :, :], mask[0:r, s % 2, :, :],
                                         ranks[0:r, :].unsqueeze(1).broadcast_to([r, TOPK, E]), ALU.mult))
                c.link(dve.tensor_reduce(slot_f[0:r, :], ranked[0:r, :, :], AX.X, ALU.add))
                dve.tensor_copy(slot[0:r, s % 2, :], slot_f[0:r, :]).then_inc(slot_done, 1)
                dve.tensor_tensor(count[:, :], R_BANK[:, 2 * E:3 * E], count[:, :], ALU.add).then_inc(rank_read, 1)

            def residual(ts):
                (q, s), r = ts, rows_of(ts)
                n = q * RING + s
                dve.wait_ge(y_done, n + 1)
                dve.wait_ge(h_loaded[s], 16 * (q + 1))
                dve.tensor_tensor(h[0:r, s, :], Y_BANK[0:r, 0:C], h[0:r, s, :], ALU.add).then_inc(h2_done, 1)
                dve.wait_ge(h2_done, n + 1)
                chain["stats2"].start(n)
                chain["stats2"].link(dve.bn_stats(stats2[0:r, :], h[0:r, s, :]))
                apart(dve)
                dve.bn_aggr(mv2[0:r, s % 2, :], stats2[0:r, :]).then_inc(stats2_done, 1)

            def normalise2(ts):
                (q, s), r = ts, rows_of(ts)
                n = q * RING + s
                c = chain["zx"]
                c.start(n)
                dve.wait_ge(rstd2_done, n + 1)
                wait(dve, z2t_done, n - 1)
                dve.tensor_scalar(z2[0:r, s % 2, :], h[0:r, s, :], mv2[0:r, s % 2, 0:1], rstd2[0:r, s % 2, 1:2],
                                  ALU.subtract, ALU.mult).then_inc(z2_done, 1)
                wait(dve, scattered[s % 2], 16 * TOPK * (2 * q + s // 2))
                dve.wait_ge(z2_done, n + 1)
                halves = [zx[0:r, s % 2, k, 0:C].bitcast(F16) for k in range(TOPK)]
                c.link(dve.tensor_scalar(halves[0][:, 0:C], z2[0:r, s % 2, :], ZS, None, ALU.mult))
                c.link(dve.scalar_tensor_tensor(halves[0][:, C:], z2[0:r, s % 2, :], ZS, halves[0][:, 0:C], ALU.mult, ALU.subtract))
                dve.tensor_copy(halves[1], halves[0])

            def route(ts):
                (q, s), r = ts, rows_of(ts)
                n = q * RING + s
                c = chain["sort"]
                c.start(n)
                dve.wait_ge(rl_done, n + 1)
                dve.tensor_copy(rl[0:r, :], RL_BANK[0:r, 0:E]).then_inc(rl_read, 1)
                dve.wait_ge(rl_read, n + 1)
                apart(dve)
                c.link(dve.max(top[0:r, s % 2, :], rl[0:r, :]))
                dve.tensor_scalar(neg_top[0:r, s % 2, :], top[0:r, s % 2, 0:1], -1.0, None, ALU.mult).then_inc(sorted_done, 1)
                c.link(dve.max_index(top_i[0:r, :], top[0:r, s % 2, :], rl[0:r, :]))
                c.link(dve.tensor_copy(top_f[0:r, :], top_i[0:r, 0:TOPK]))
                for k in range(TOPK):
                    c.link(dve.tensor_scalar(mask[0:r, s % 2, k, :], tab[0:r, T_IOTA:T_IOTA + E], top_f[0:r, k:k + 1], None, ALU.is_equal))
                wait(dve, rank_done, n - 1)
                dve.tensor_tensor(mask16[0:r, s % 2, :], mask[0:r, s % 2, 0, :], mask[0:r, s % 2, 1, :], ALU.add).then_inc(mask_done, 1)

            def weights_of(ts):
                (q, s), r = ts, rows_of(ts)
                n = q * RING + s
                c = chain["weight"]
                c.start(n)
                dve.wait_ge(ex_done, n + 1)
                c.link(dve.reciprocal(rsum[0:r, :], ex[0:r, s % 2, E:E + 1]))
                c.link(dve.tensor_scalar(pk[0:r, :], ex[0:r, s % 2, 0:TOPK], rsum[0:r, :], None, ALU.mult))
                c.link(dve.tensor_scalar(den[0:r, 0:1], pk[0:r, 0:1], pk[0:r, 1:2], 1e-8, ALU.add, ALU.add))
                c.link(dve.reciprocal(den[0:r, 1:2], den[0:r, 0:1]))
                dve.tensor_scalar(zx[0:r, s % 2, :, C], pk[0:r, :], den[0:r, 1:2], None, ALU.mult)
                c.link(dve.tensor_copy(zx[0:r, s % 2, :, C + 1].bitcast(U32), target[0:r, :]))
                dve.tensor_scalar(target[:, :], target[:, :], float(TOPK * P), None, ALU.add).then_inc(zx_done, 1)

            def step(at, u, m):
                if ts := at(3):
                    slots_of(ts)
                if ts := at(2):
                    route(ts)
                if ts := at(1):
                    normalise2(ts)
                if ts := at(0):
                    residual(ts)
                if ts := at(2):
                    weights_of(ts)
                if u == 0:
                    weight_size(m + 2)
                if u == 1:
                    weight_scale(m + 2)
                if u == 2:
                    split_low(m + 2)

            weight_size(0)
            weight_scale(0)
            split_low(0)
            pipeline(dve, NT, 1, RING, RING + 1, step, odd=1)

            c = chain["table"]
            c.start(0)
            dve.wait_ge(rank_read, NT)
            dve.tensor_scalar(pad_f[:, 0:E], count[:, :], tab[:, T_PART:T_PART + 1], None, ALU.add)
            c.link(dve.tensor_scalar(pad_f[:, E:E + 1], tab[:, T_PART:T_PART + 1], float(E * REG), None, ALU.add))
            dve.tensor_copy(pad_slot[:, :], pad_f[:, :]).then_inc(pad_slots_done, 1)
            rows_, tiles_, end_, begin_, start_ = (n_f[:, i, :] for i in range(5))
            c.link(dve.tensor_tensor(rows_, count[0:1, :], tab[0:1, T_BASE:T_BASE + E], ALU.subtract))
            c.link(dve.tensor_tensor(tiles_cmp[:, :, :], rows_.unsqueeze(2).broadcast_to([1, E, NT + 1]),
                                     steps_in[:, NJ:].unsqueeze(1).broadcast_to([1, E, NT + 1]), ALU.is_gt))
            c.link(dve.tensor_reduce(tiles_, tiles_cmp[:, :, :], AX.X, ALU.add))
            c.link(dve.tensor_tensor_scan(end_, tiles_, tiles_, 0.0, ALU.add, ALU.bypass))
            c.link(dve.tensor_tensor(begin_, end_, tiles_, ALU.subtract))
            c.link(dve.scalar_tensor_tensor(start_, begin_, -float(P), tab[0:1, T_BASE:T_BASE + E], ALU.mult, ALU.add))
            j_ = steps_in[:, 0:NJ]
            j_b = j_.unsqueeze(2).broadcast_to([1, NJ, E])
            past, reached, mine = (sel[:, i, :, :] for i in range(3))
            c.link(dve.tensor_tensor(past, j_b, end_.unsqueeze(1).broadcast_to([1, NJ, E]), ALU.is_ge))
            c.link(dve.tensor_tensor(reached, j_b, begin_.unsqueeze(1).broadcast_to([1, NJ, E]), ALU.is_ge))
            c.link(dve.tensor_tensor(mine, reached, past, ALU.subtract))
            c.link(dve.tensor_tensor(mine, mine, start_.unsqueeze(1).broadcast_to([1, NJ, E]), ALU.mult))
            expert_, row_, used_, tmp_ = (step_f[:, i, :] for i in range(4))
            c.link(dve.tensor_reduce(expert_, past, AX.X, ALU.add))
            c.link(dve.tensor_reduce(tmp_, mine, AX.X, ALU.add))
            c.link(dve.scalar_tensor_tensor(row_, j_, float(P), tmp_, ALU.mult, ALU.add))
            c.link(dve.tensor_scalar(used_, expert_, float(E), None, ALU.is_lt))
            c.link(dve.tensor_scalar(row_, row_, -float(E * REG), None, ALU.add))
            c.link(dve.tensor_tensor(row_, row_, used_, ALU.mult))
            c.link(dve.tensor_scalar(step_tab[:, NJ:], row_, float(E * REG), None, ALU.add))
            c.link(dve.tensor_scalar(step_tab[:, 0:NJ], expert_, float(E - 1), None, ALU.min))


def expert_stage(nc, kept, routed, expert_out):
    gu_hi, gu_lo, down, bg, bu, bd = (kept[n] for n in ("gu_hi", "gu_lo", "down", "bg", "bu", "bd"))
    inv_scale, id16, step_tab, banks = (kept[n] for n in ("inv_scale", "id16", "step_tab", "banks"))
    ZT_BANK, G_BANK, U_BANK, Y_BANK = banks[0:2], banks[2:4], banks[4:6], banks[6:8]
    with ExitStack() as ctx:
        def sb(name, shape, dt=F32):
            return ctx.enter_context(nc.sbuf_tensor(name, shape, dt))

        def sem(name):
            return ctx.enter_context(nc.semaphore(name))

        zg = sb("zg", [P, RING, ROW])
        zt = sb("zt", [P, 2, 2 * KC * P], F16)
        sg = sb("sg", [P, 2, M])
        hid = sb("hid", [P, 2, M])
        ye = sb("ye", [P, 2, C])
        yw = sb("yw", [P, 2, C])
        loaded = [sem(f"loaded{s}") for s in range(RING)]
        stored = [sem("stored0"), sem("stored1")]
        zt_done, zt_copied, gate_done, up_done = sem("zt_done"), sem("zt_copied"), sem("gate_done"), sem("up_done")
        silu_done, hid_done, y_done, ye_done, yw_done = (sem(n) for n in ("silu_done", "hid_done", "ye_psum", "ye_done", "yw_done"))
        block = ctx.enter_context(nc.Block())

        def expert(eng, n):
            return eng.value_load(step_tab[0:1, n:n + 1] if isinstance(n, int) else step_tab[0:1, bass.ds(n, 1)],
                                  min_val=0, max_val=E - 1)

        def run(eng, step):
            pipeline(eng, NJ, 2, 1, 3, step)

        @block.sync
        def _(sp):
            def step(at, u, m):
                if ts := at(-2):
                    q, s = ts
                    n = q * RING + s
                    wait(sp, stored[s % 2], 16 * (2 * q + s // 2 - 1))
                    i = NJ + n
                    row = sp.value_load(step_tab[0:1, i:i + 1] if isinstance(i, int) else step_tab[0:1, bass.ds(i, 1)],
                                        min_val=0, max_val=E * REG)
                    sp.dma_start(zg[:, s, :], routed[bass.ds(row, P), :]).then_inc(loaded[s], 16)

            run(sp, step)

        @block.gpsimd
        def _(pool):
            def step(at, u, m):
                if ts := at(1):
                    q, s = ts
                    pool.wait_ge(yw_done, q * RING + s + 1)
                    apart(pool)
                    pool.indirect_dma_start(
                        out=expert_out[:, :],
                        out_offset=bass.IndirectOffsetOnAxis(ap=zg[:, s, ROW - 1:ROW].bitcast(U32), axis=0),
                        in_=yw[:, s % 2, :], in_offset=None, bounds_check=OUT_ROWS - 1, oob_is_err=False).then_inc(stored[s % 2], 16)

            run(pool, step)
            pool.wait_ge(stored[0], 16 * (NJ // 2))
            pool.wait_ge(stored[1], 16 * (NJ // 2))

        @block.scalar
        def _(act):
            def step(at, u, m):
                if ts := at(-1):
                    q, s = ts
                    n = q * RING + s
                    act.wait_ge(zt_done, n + 1)
                    wait(act, up_done, n - 1)
                    act.activation(zt[:, s % 2, :], ZT_BANK[s % 2][:, 0:C].bitcast(F16), ACT.Copy).then_inc(zt_copied, 1)
                if ts := at(0):
                    q, s = ts
                    n = q * RING + s
                    e = expert(act, n)
                    act.wait_ge(gate_done, n + 1)
                    wait(act, hid_done, n - 1)
                    for c in range(MC):
                        cols = slice(c * P, (c + 1) * P)
                        last = act.activation(sg[:, s % 2, cols], G_BANK[s % 2][:, cols], ACT.Silu,
                                              scale=inv_scale[:, bass.ds(e, 1)], bias=bg[:, bass.ds(e * MC + c, 1)])
                    last.then_inc(silu_done, 1)
                if ts := at(1):
                    q, s = ts
                    act.wait_ge(ye_done, q * RING + s + 1)
                    wait(act, stored[s % 2], 16 * (2 * q + s // 2))
                    act.activation(yw[:, s % 2, :], ye[:, s % 2, :], ACT.Copy, scale=zg[:, s, C:C + 1]).then_inc(yw_done, 1)

            run(act, step)

        @block.vector
        def _(dve):
            def step(at, u, m):
                if ts := at(0):
                    q, s = ts
                    n = q * RING + s
                    e = expert(dve, n)
                    dve.wait_ge(silu_done, n + 1)
                    dve.wait_ge(up_done, n + 1)
                    wait(dve, y_done, n - 1)
                    for c in range(MC):
                        cols = slice(c * P, (c + 1) * P)
                        last = dve.scalar_tensor_tensor(hid[:, s % 2, cols], U_BANK[s % 2][:, cols], bu[:, bass.ds(e * MC + c, 1)],
                                                        sg[:, s % 2, cols], ALU.add, ALU.mult)
                    last.then_inc(hid_done, 1)
                if ts := at(1):
                    q, s = ts
                    n = q * RING + s
                    e = expert(dve, n)
                    dve.wait_ge(y_done, n + 1)
                    wait(dve, yw_done, n - 1)
                    dve.scalar_tensor_tensor(ye[:, s % 2, :], Y_BANK[s % 2][:, 0:C], inv_scale[:, bass.ds(e, 1)],
                                             bd[:, bass.ds(e * C, C)], ALU.mult, ALU.add).then_inc(ye_done, 1)

            run(dve, step)

        @block.tensor
        def _(pe):
            def step(at, u, m):
                if ts := at(-1):
                    q, s = ts
                    n = q * RING + s
                    pe.wait_ge(loaded[s], 16 * (q + 1))
                    wait(pe, zt_copied, n - 1)
                    halves = zg[:, s, 0:C].bitcast(F16)
                    bank = ZT_BANK[s % 2][:, 0:C].bitcast(F16)
                    for c in range(2 * KC):
                        last = pe.transpose(bank[:, c * P:(c + 1) * P], halves[:, c * P:(c + 1) * P], id16[:, :])
                    last.then_inc(zt_done, 1)
                if ts := at(0):
                    q, s = ts
                    n = q * RING + s
                    e = expert(pe, n)
                    pe.wait_ge(zt_copied, n + 1)
                    for half_, bank, used, done in ((0, G_BANK, silu_done, gate_done), (1, U_BANK, hid_done, up_done)):
                        wait(pe, used, n - 1)
                        for c in range(MC):
                            dst = bank[s % 2][:, c * P:(c + 1) * P]
                            for k in range(KC):
                                at_ = e * GU + (k * 2 * M + half_ * M + c * P)
                                hi, lo = gu_hi[:, bass.ds(at_, P)], gu_lo[:, bass.ds(at_, P)]
                                z_hi = zt[:, s % 2, k * P:(k + 1) * P]
                                z_lo = zt[:, s % 2, (KC + k) * P:(KC + k + 1) * P]
                                pe.matmul(dst, hi, z_hi, start=k == 0, stop=False)
                                pe.matmul(dst, hi, z_lo, start=False, stop=False)
                                last = pe.matmul(dst, lo, z_hi, start=False, stop=k == KC - 1)
                        last.then_inc(done, 1)
                if ts := at(1):
                    q, s = ts
                    n = q * RING + s
                    e = expert(pe, n)
                    pe.wait_ge(hid_done, n + 1)
                    wait(pe, ye_done, n - 1)
                    for c in range(MC):
                        last = pe.matmul(Y_BANK[s % 2][:, 0:C], hid[:, s % 2, c * P:(c + 1) * P],
                                         down[:, bass.ds(e * (MC * C) + c * C, C)], start=c == 0, stop=c == MC - 1)
                    last.then_inc(y_done, 1)

            run(pe, step)


def dyn_batch(ap, n):
    if isinstance(n, int):
        return ap[n]
    return ap[bass.ds(n, 1)].rearrange("a p t n -> (a p) t n")


def combine_stage(nc, expert_out, h2_dram, out):
    SP_ = S // P
    with ExitStack() as ctx:
        def sb(name, shape, dt=F32):
            return ctx.enter_context(nc.sbuf_tensor(name, shape, dt))

        def sem(name):
            return ctx.enter_context(nc.semaphore(name))

        eo = sb("eo", [P, 2, SP_, TOPK, C])
        hh = sb("hh", [P, 2, SP_, C])
        oo = sb("oo", [P, 2, SP_, C])
        cls_eo = sb("cls_eo", [B, TOPK, C])
        cls_h = sb("cls_h", [B, C])
        in_loaded = [sem("in_loaded0"), sem("in_loaded1")]
        summed, half_summed = sem("summed"), sem("half_summed")
        out_stored = [sem("out_stored0"), sem("out_stored1")]
        cls_in, cls_sum, cls_out = sem("cls_in"), sem("cls_sum"), sem("cls_out")
        block = ctx.enter_context(nc.Block())
        eo_v = expert_out[0:TOPK * B * S, :].rearrange("(b t p k) c -> b p t (k c)", b=B, p=P, k=TOPK)
        h_v = h2_dram[0:B * S, :].rearrange("(b t p) c -> b p t c", b=B, p=P)

        @block.sync
        def _(sp):
            sp.dma_start(cls_eo[:, :, :], expert_out[TOPK * B * S:, :].rearrange("(b k) c -> b k c", k=TOPK)).then_inc(cls_in, 16)
            sp.dma_start(cls_h[:, :], h2_dram[B * S:, :]).then_inc(cls_in, 16)

            def load(m):
                for s in range(2):
                    wait(sp, summed, m * 2 + s - 1)
                    sp.dma_start(eo[:, s, :, :, :].rearrange("p t k c -> p t (k c)"), dyn_batch(eo_v, m * 2 + s)).then_inc(in_loaded[s], 16)
                    sp.dma_start(hh[:, s, :, :], dyn_batch(h_v, m * 2 + s)).then_inc(in_loaded[s], 16)

            load(0)
            with sp.Fori(1, B // 2) as m:
                load(m)

        @block.vector
        def _(dve):
            dve.wait_ge(cls_in, 32)
            dve.tensor_tensor(cls_eo[:, 0, :], cls_eo[:, 0, :], cls_eo[:, 1, :], ALU.add).then_inc(cls_sum, 1)
            dve.wait_ge(cls_sum, 1)
            dve.tensor_tensor(cls_h[:, :], cls_h[:, :], cls_eo[:, 0, :], ALU.add).then_inc(cls_sum, 1)

            def add(m):
                for s in range(2):
                    dve.wait_ge(in_loaded[s], m * 32 + 32)
                    wait(dve, out_stored[s], m * 16)
                    dve.tensor_tensor(oo[:, s, :, :], eo[:, s, :, 0, :], eo[:, s, :, 1, :], ALU.add).then_inc(half_summed, 1)
                    dve.wait_ge(half_summed, m * 2 + s + 1)
                    dve.tensor_tensor(oo[:, s, :, :], oo[:, s, :, :], hh[:, s, :, :], ALU.add).then_inc(summed, 1)

            add(0)
            with dve.Fori(1, B // 2) as m:
                add(m)

        @block.scalar
        def _(act):
            act.wait_ge(cls_sum, 2)
            act.dma_start(out[:, 0, :], cls_h[:, :]).then_inc(cls_out, 16)
            with act.Fori(0, B // 2) as m:
                for s in range(2):
                    act.wait_ge(summed, m * 2 + s + 1)
                    dst = out[bass.ds(m * 2 + s, 1), 1:, :].rearrange("b (p s) c -> (b p) (s c)", s=SP_)
                    act.dma_start(dst, oo[:, s, :, :].rearrange("p s c -> p (s c)")).then_inc(out_stored[s], 16)
            act.wait_ge(cls_out, 16)
            act.wait_ge(out_stored[0], 16 * (B // 2))
            act.wait_ge(out_stored[1], 16 * (B // 2))


def kernel(x, cls_tok, L0_tok_weight, L0_tok_weighted_sum, L0_attn_w_qkv, L0_attn_b_qkv, L0_attn_w_out, L0_attn_b_out,
           L0_ffn_W_router, L0_ffn_W_gate, L0_ffn_b_gate, L0_ffn_W_up, L0_ffn_b_up, L0_ffn_W_out, L0_ffn_b_out):
    import numpy as np
    import concourse.bacc as bacc
    from concourse.bass_utils import run_bass_kernel_spmd as run

    def chunked(w):
        return w.reshape(w.shape[0] // P, P, w.shape[1]).transpose(1, 0, 2)

    a = {k: np.asarray(v) for k, v in dict(
        x=x, cls=cls_tok, tw=L0_tok_weight, tws=L0_tok_weighted_sum, wqkv=L0_attn_w_qkv, bqkv=L0_attn_b_qkv,
        wo=L0_attn_w_out, bo=L0_attn_b_out, wr=L0_ffn_W_router, wg=L0_ffn_W_gate, bg=L0_ffn_b_gate, wu=L0_ffn_W_up,
        bu=L0_ffn_b_up, wd=L0_ffn_W_out, bd=L0_ffn_b_out).items()}
    perm = np.concatenate([np.arange(2 * C), 2 * C + np.arange(C).reshape(NH, HD).T.ravel()])
    gu = np.stack([a["wg"], a["wu"]], 2).reshape(E, KC, P, 2 * M).transpose(0, 2, 1, 3).reshape(E, P, GU)
    table = np.zeros((P, T_COLS), np.float32)
    table[:, T_IOTA:T_IOTA + E] = np.arange(E)
    table[:, T_BASE:T_BASE + E] = np.arange(E) * REG
    table[:, T_TARGET:T_TARGET + TOPK] = np.arange(P)[:, None] * TOPK + np.arange(TOPK)
    table[:, T_FAR] = FAR
    table[:, T_PART] = np.arange(P)
    arrays = dict(
        x_t=a["x"].reshape(B, P, TPB, KC, P, D1).transpose(0, 2, 4, 5, 3, 1).reshape(NT - 1, P, XC * P),
        cls=a["cls"].reshape(1, C),
        tok_w=a["tw"].T,
        tok_ws=chunked(a["tws"].T),
        w_qkv=chunked(a["wqkv"][perm].T),
        b_qkv=a["bqkv"][perm].reshape(1, 3 * C),
        w_o=chunked(a["wo"].T),
        b_o=a["bo"].reshape(1, C),
        w_router=chunked(a["wr"]),
        w_gu=gu,
        b_gate=a["bg"].reshape(E, MC, P).transpose(2, 0, 1).reshape(P, E * MC),
        b_up=a["bu"].reshape(E, MC, P).transpose(2, 0, 1).reshape(P, E * MC),
        w_down=a["wd"].reshape(E, MC, P, C).transpose(2, 0, 1, 3).reshape(P, E * MC * C),
        b_down=a["bd"].reshape(1, E * C),
        ident=np.eye(P, dtype=np.float32),
        upper=np.triu(np.ones((P, P), np.float32), 1),
        table=table,
        steps=np.concatenate([np.arange(NJ), P * np.arange(NT + 1)]).astype(np.float32).reshape(1, -1),
    )
    nc = bacc.Bacc("TRN2", target_bir_lowering=False, num_devices=1)
    ins, aps = {}, {}
    for name, v in arrays.items():
        ins[f"in_{name}"] = np.ascontiguousarray(v)
        aps[name] = nc.dram_tensor(f"in_{name}", v.shape, mybir.dt.from_np(v.dtype), kind="ExternalInput").ap()
    aps["out"] = nc.dram_tensor("result", (B, S + 1, C), F32, kind="ExternalOutput").ap()
    vit_block(nc, **aps)
    return run(nc, [ins], core_ids=[0]).results[0]["result"]
```

```python
import concourse.bass as bass
from concourse import mybir
from contextlib import ExitStack

F32 = mybir.dt.float32
F16 = mybir.dt.float16
BF16 = mybir.dt.bfloat16
I32 = mybir.dt.int32
U32 = mybir.dt.uint32
ALU = mybir.AluOpType
ACT = mybir.ActivationFunctionType
AX = mybir.AxisListType

B, S, C, D1 = 8, 512, 256, 4
NH, HD = 16, 16
E, M, TOPK = 8, 512, 2
P = 128
KC = C // P
XC = C * D1 // P
MC = M // P
GU = KC * 2 * M
TPB = S // P
NT = B * TPB + 1
NTOK = B * (S + 1)
RING = 4
RT = 2
TR = RT * P
REG = NTOK + TR
NJ = (NTOK * TOPK + E * (TR - 1)) // TR
NR = NTOK // TR + 1
ROW = C + 2
OUT_ROWS = NTOK * TOPK
FAR = 1 << 20
ZS = 256.0
WS = 16384.0
POOL_HEADS = 5
DVE_HEADS = NH - POOL_HEADS
SCALE = float(C) ** -0.5
EPS = 1e-5
T_IOTA, T_BASE, T_TARGET, T_FAR, T_PART, T_COLS = 0, E, 2 * E, 2 * E + 2, 2 * E + 3, 2 * E + 4


def tile_at(t, n):
    return (t // RING, t % RING) if 0 <= t < n else None


def pipeline(eng, n, ahead, behind, first, step, odd=0):
    loops = (n - odd - ahead - first) // RING
    for i in range(-ahead, first):
        step(lambda lag, i=i: tile_at(i - lag, n), (i - first) % RING, (i - first) // RING)
    with eng.Fori(0, loops) as m:
        for u in range(RING):
            step(lambda lag, u=u: (m + (first + u - lag) // RING, (first + u - lag) % RING), u, m)
    for i in range(first + loops * RING, n + behind):
        step(lambda lag, i=i: tile_at(i - lag, n), None, None)


def wait(eng, sem, value):
    if not isinstance(value, int) or value > 0:
        eng.wait_ge(sem, value)


def apart(eng):
    eng.nop(nofuse=True)


class Chain:

    def __init__(self, eng, sem, per):
        self.eng, self.sem, self.per = eng, sem, per

    def start(self, n):
        self.base, self.k = n * self.per, 0

    def link(self, ins):
        ins.then_inc(self.sem, 1)
        self.k += 1
        assert self.k <= self.per
        self.eng.wait_ge(self.sem, self.base + self.k)


def is_cls(ts):
    return isinstance(ts[0], int) and ts[0] * RING + ts[1] == NT - 1


def rows_of(ts):
    return B if is_cls(ts) else P


def rows_at(ap, start, n):
    return ap[start:start + n, :] if isinstance(start, int) else ap[bass.ds(start, n), :]


def dyn_row(ap, n):
    if isinstance(n, int):
        return ap[n]
    return ap[bass.ds(n, 1)].rearrange("a p n -> (a p) n")


def vit_block(nc, x_t, cls, tok_w, tok_ws, w_qkv, b_qkv, w_o, b_o, w_router, w_gu, b_gate, b_up,
              w_down, b_down, ident, upper, table, steps, out):
    with ExitStack() as ctx:
        ctx.enter_context(nc.allow_low_precision("fp16 halves of fp32 values; masks of zeros and ones"))

        def sb(name, shape, dt=F32):
            return ctx.enter_context(nc.sbuf_tensor(name, shape, dt))

        routed = nc.dram_tensor("routed", [E * REG + TR, ROW], F32, kind="Internal").ap()
        expert_out = nc.dram_tensor("expert_out", [OUT_ROWS, C], F32, kind="Internal").ap()
        h_dram = nc.dram_tensor("h_dram", [NTOK, C], F32, kind="Internal").ap()
        att_dram = nc.dram_tensor("att_dram", [B, NH, S + 1, HD], F32, kind="Internal").ap()
        h2_dram = nc.dram_tensor("h2_dram", [NTOK, C], F32, kind="Internal").ap()

        kept = dict(
            gu_hi=sb("gu_hi", [P, E * GU], F16),
            gu_lo=sb("gu_lo", [P, E * GU], F16),
            down=sb("down", [P, E * MC * C]),
            bg=sb("bg", [P, E * MC]),
            bu=sb("bu", [P, E * MC]),
            bd=sb("bd", [P, E * C]),
            inv_scale=sb("inv_scale", [P, E]),
            id16=sb("id16", [P, P], F16),
            step_tab=sb("step_tab", [1, 2 * NJ], I32),
            banks=[ctx.enter_context(nc.psum_tensor(f"bank{i}", [P, 512], F32)) for i in range(8)],
        )
        attend_stage(nc, kept["banks"], x_t, cls, tok_w, tok_ws, w_qkv, b_qkv, ident, h_dram, att_dram)
        route_stage(nc, kept, w_o, b_o, w_router, w_gu, b_gate, b_up, w_down, b_down, ident, upper, table, steps,
                    h_dram, att_dram, routed, h2_dram)
        expert_stage(nc, kept, routed, expert_out)
        combine_stage(nc, expert_out, h2_dram, out)


def attend_stage(nc, banks, x_t, cls, tok_w, tok_ws, w_qkv, b_qkv, ident, h_dram, att_dram):
    H_BANK, QK_BANK, V_BANK, Z1T_BANK = banks[0:4]
    with ExitStack() as ctx:
        def sb(name, shape, dt=F32):
            return ctx.enter_context(nc.sbuf_tensor(name, shape, dt))

        def sem(name):
            return ctx.enter_context(nc.semaphore(name))

        xs = sb("xs", [P, 2, XC * P])
        wtok = sb("wtok", [P, XC, C])
        wqkv = sb("wqkv", [P, KC, 3 * C])
        bqkv = sb("bqkv", [1, 3 * C])
        id32 = sb("id32", [P, P])
        ones_row = sb("ones_row", [1, P])
        half = sb("half", [P, 1])
        h = sb("h", [P, RING, C])
        stats = sb("stats", [P, 6])
        mv = sb("mv", [P, 2, 2])
        rstd = sb("rstd", [P, 2, 2])
        z1 = sb("z1", [P, 2, C])
        z1t = sb("z1t", [P, 2, KC, P])
        qkv = sb("qkv", [P, RING, 3 * C])
        prod = sb("prod", [P, DVE_HEADS * NH * HD])
        tokw = prod[:, 0:D1 * C].rearrange("p (d c) -> p d c", d=D1)
        tokws = prod[:, D1 * C:(D1 + KC) * C].rearrange("p (k c) -> p k c", k=KC)
        pq = sb("pq", [P, POOL_HEADS * NH * HD])
        pv = sb("pv", [P, POOL_HEADS * NH * HD])
        logits = sb("logits", [P, 2, NH * NH])
        lmax = sb("lmax", [P, NH])
        prob = sb("prob", [P, 2, NH * NH])
        psums = sb("psums", [P, 2, NH])
        att = sb("att", [P, RING, C])

        first_consts, consts = sem("first_consts"), sem("consts")
        filled, wtok_ready = sem("filled"), sem("wtok_ready")
        x_loaded = [sem("x_loaded0"), sem("x_loaded1")]
        cls_loaded, h_done, h_copied = sem("cls_loaded"), sem("h_done"), sem("h_copied")
        stats_done, eps_added, rstd_done, z1_done = (sem(n) for n in ("stats_done", "eps_added", "rstd_done", "z1_done"))
        z1t_done, z1t_copied = sem("z1t_done"), sem("z1t_copied")
        qkv_done, qkv_copied = sem("qkv_done"), sem("qkv_copied")
        pq_done, logits_done, prob_done, pv_done = sem("pq_done"), sem("logits_done"), sem("prob_done"), sem("pv_done")
        att_done = sem("att_done")
        h_stored = [sem(f"h_stored{s}") for s in range(RING)]
        att_stored = [sem(f"att_stored{s}") for s in range(RING)]
        links = {n: sem(f"{n}_link") for n in ("stats", "qk", "pv")}

        N_CONSTS = 16 * 3
        block = ctx.enter_context(nc.Block())

        @block.sync
        def _(sp):
            def load(dst, src, s):
                sp.dma_start(dst, src).then_inc(s, 16)

            load(tokw[:, :, :], tok_w.unsqueeze(0).broadcast_to([P, D1, C]), first_consts)
            load(tokws[:, :, :], tok_ws, first_consts)
            for t in range(2):
                load(xs[:, t, :], x_t[t], x_loaded[t])
            load(id32[:, :], ident, consts)
            load(wqkv[:, :, :], w_qkv, consts)
            load(bqkv[:, :], b_qkv, consts)

            def step(at, u, m):
                if ts := at(-1):
                    q, s = ts
                    n = q * RING + s
                    if is_cls(ts):
                        sp.wait_ge(h_stored[s], 16 * q)
                        sp.wait_ge(z1_done, n - 3)
                        load(h[0:B, s, :], cls.broadcast_to([B, C]), cls_loaded)
                    elif not isinstance(n, int) or n >= 2:
                        wait(sp, h_done, n - 1)
                        load(xs[:, s % 2, :], dyn_row(x_t, n), x_loaded[s % 2])
                if ts := at(0):
                    (q, s), r = ts, rows_of(ts)
                    n = q * RING + s
                    if is_cls(ts):
                        sp.wait_ge(cls_loaded, 16)
                    else:
                        sp.wait_ge(h_copied, n + 1)
                    sp.dma_start(rows_at(h_dram, n * P, r), h[0:r, s, :]).then_inc(h_stored[s], 16)
                if ts := at(3):
                    (q, s), r = ts, rows_of(ts)
                    n = q * RING + s
                    sp.wait_ge(att_done, n + 1)
                    if is_cls(ts):
                        dst = att_dram[:, :, 0, :]
                    else:
                        dst = att_dram[q] if isinstance(q, int) else att_dram[bass.ds(q, 1)].rearrange("b h n d -> (b h) n d")
                        dst = dst[:, 1:, :].rearrange("h (p t) d -> p t h d", t=TPB)[:, s, :, :]
                    sp.dma_start(dst, att[0:r, s, :].rearrange("p (h d) -> p h d", h=NH)).then_inc(att_stored[s], 16)

            pipeline(sp, NT, 1, 3, RING + 1, step, odd=1)
            for s in range(RING):
                tiles = (NT - 1 - s) // RING + 1
                sp.wait_ge(h_stored[s], 16 * tiles)
                sp.wait_ge(att_stored[s], 16 * tiles)

        @block.gpsimd
        def _(pool):
            pool.memset(half[:, :], -0.5).then_inc(filled, 1)
            pool.memset(ones_row[:, :], 1.0).then_inc(filled, 1)
            pool.wait_ge(filled, 1)

            def inverse_root(ts, ready, used, added, done, m, r_):
                (q, s), r = ts, rows_of(ts)
                n = q * RING + s
                pool.wait_ge(ready, n + 1)
                wait(pool, used, n - 1)
                apart(pool)
                pool.tensor_scalar(r_[0:r, s % 2, 0:1], m[0:r, s % 2, 1:2], EPS, None, ALU.add).then_inc(added, 1)
                pool.wait_ge(added, n + 1)
                pool.tensor_tensor(r_[0:r, s % 2, 1:2], r_[0:r, s % 2, 0:1], half[0:r, :], ALU.pow).then_inc(done, 1)

            def step(at, u, m):
                if ts := at(0):
                    inverse_root(ts, stats_done, z1_done, eps_added, rstd_done, mv, rstd)
                if ts := at(1):
                    (q, s), r = ts, rows_of(ts)
                    n = q * RING + s
                    pool.wait_ge(qkv_copied, n + 1)
                    wait(pool, logits_done, n)
                    q_ = qkv[0:r, s, DVE_HEADS * HD:C].rearrange("p (h d) -> p h d", h=POOL_HEADS)
                    k_ = qkv[0:r, s, C:2 * C].rearrange("p (g d) -> p g d", g=NH)
                    pool.tensor_tensor(
                        pq[0:r, :].rearrange("p (h g d) -> p h g d", h=POOL_HEADS, g=NH),
                        q_.unsqueeze(2).broadcast_to([r, POOL_HEADS, NH, HD]),
                        k_.unsqueeze(1).broadcast_to([r, POOL_HEADS, NH, HD]), ALU.mult).then_inc(pq_done, 1)
                if ts := at(2):
                    (q, s), r = ts, rows_of(ts)
                    n = q * RING + s
                    pool.wait_ge(prob_done, n + 1)
                    wait(pool, att_done, n)
                    p_ = prob[0:r, s % 2, DVE_HEADS * NH:].rearrange("p (h g) -> p h g", h=POOL_HEADS)
                    v_ = qkv[0:r, s, 2 * C:].rearrange("p (d g) -> p d g", g=NH)
                    pool.tensor_tensor(
                        pv[0:r, :].rearrange("p (h d g) -> p h d g", h=POOL_HEADS, d=HD),
                        p_.unsqueeze(2).broadcast_to([r, POOL_HEADS, HD, NH]),
                        v_.unsqueeze(1).broadcast_to([r, POOL_HEADS, HD, NH]), ALU.mult).then_inc(pv_done, 1)

            pipeline(pool, NT, 1, 3, RING + 1, step, odd=1)

        @block.scalar
        def _(act):
            def copy(done, dst, src):
                act.activation(dst, src, ACT.Copy).then_inc(done, 1)

            def step(at, u, m):
                if ts := at(0):
                    (q, s), r = ts, rows_of(ts)
                    n = q * RING + s
                    act.wait_ge(z1t_done, n + 1)
                    wait(act, qkv_done, n - 1)
                    copy(z1t_copied, z1t[:, s % 2, :, 0:r], Z1T_BANK[:, 0:KC * P].rearrange("p (k t) -> p k t", k=KC)[:, :, 0:r])
                if (ts := at(-1)) and not is_cls(ts):
                    q, s = ts
                    n = q * RING + s
                    act.wait_ge(h_done, n + 1)
                    wait(act, h_stored[s], 16 * q)
                    wait(act, z1_done, n - 3)
                    copy(h_copied, h[:, s, :], H_BANK[:, 0:C])
                if ts := at(0):
                    (q, s), r = ts, rows_of(ts)
                    n = q * RING + s
                    act.wait_ge(qkv_done, n + 1)
                    wait(act, att_done, n - 3)
                    wait(act, pv_done, n - 3)
                    act.activation(qkv[0:r, s, 0:2 * C], QK_BANK[0:r, :], ACT.Copy)
                    copy(qkv_copied, qkv[0:r, s, 2 * C:], V_BANK[0:r, 0:C])
                if ts := at(1):
                    (q, s), r = ts, rows_of(ts)
                    n = q * RING + s
                    act.wait_ge(logits_done, n + 1)
                    wait(act, att_done, n - 1)
                    wait(act, pv_done, n - 1)
                    act.activation(prob[0:r, s % 2, :], logits[0:r, s % 2, :], ACT.Exp, scale=SCALE).then_inc(prob_done, 1)

            pipeline(act, NT, 1, 3, RING + 1, step, odd=1)

        @block.tensor
        def _(pe):
            def step(at, u, m):
                if (ts := at(-1)) and not is_cls(ts):
                    q, s = ts
                    n = q * RING + s
                    pe.wait_ge(x_loaded[s % 2], 16 * (2 * q + s // 2 + 1))
                    wait(pe, h_copied, n)
                    for c in range(XC):
                        last = pe.matmul(H_BANK[:, 0:C], xs[:, s % 2, c * P:(c + 1) * P], wtok[:, c, :],
                                         start=c == 0, stop=c == XC - 1)
                    last.then_inc(h_done, 1)
                if ts := at(0):
                    (q, s), r = ts, rows_of(ts)
                    n = q * RING + s
                    pe.wait_ge(z1_done, n + 1)
                    wait(pe, z1t_copied, n)
                    for c in range(KC):
                        last = pe.transpose(Z1T_BANK[:, c * P:c * P + r], z1[0:r, s % 2, c * P:(c + 1) * P], id32[0:r, 0:r])
                    last.then_inc(z1t_done, 1)
                    pe.wait_ge(z1t_copied, n + 1)
                    wait(pe, qkv_copied, n)
                    for bank, lo, hi in ((QK_BANK, 0, 2 * C), (V_BANK, 2 * C, 3 * C)):
                        pe.matmul(bank[0:r, 0:hi - lo], ones_row[:, 0:r], bqkv[:, lo:hi], start=True, stop=False)
                        for c in range(KC):
                            last = pe.matmul(bank[0:r, 0:hi - lo], z1t[:, s % 2, c, 0:r], wqkv[:, c, lo:hi],
                                             start=False, stop=c == KC - 1)
                    last.then_inc(qkv_done, 1)

            pe.wait_ge(wtok_ready, XC)
            pe.wait_ge(consts, N_CONSTS)
            pe.wait_ge(filled, 2)
            pipeline(pe, NT, 1, 3, RING + 1, step, odd=1)

        @block.vector
        def _(dve):
            chain = {n: Chain(dve, links[n], per) for n, per in dict(stats=1, qk=3, pv=5).items()}

            dve.wait_ge(first_consts, 32)
            for d in range(D1):
                for c in range(KC):
                    dve.tensor_tensor(wtok[:, d * KC + c, :], tokws[:, c, :], tokw[:, d, :], ALU.mult).then_inc(wtok_ready, 1)
            dve.wait_ge(wtok_ready, XC)

            def stats_of(ts):
                (q, s), r = ts, rows_of(ts)
                n = q * RING + s
                if is_cls(ts):
                    dve.wait_ge(cls_loaded, 16)
                else:
                    dve.wait_ge(h_copied, n + 1)
                chain["stats"].start(n)
                chain["stats"].link(dve.bn_stats(stats[0:r, :], h[0:r, s, :]))
                apart(dve)
                dve.bn_aggr(mv[0:r, s % 2, :], stats[0:r, :]).then_inc(stats_done, 1)

            def normalise(ts):
                (q, s), r = ts, rows_of(ts)
                n = q * RING + s
                dve.wait_ge(rstd_done, n + 1)
                wait(dve, z1t_done, n - 1)
                dve.tensor_scalar(z1[0:r, s % 2, :], h[0:r, s, :], mv[0:r, s % 2, 0:1], rstd[0:r, s % 2, 1:2],
                                  ALU.subtract, ALU.mult).then_inc(z1_done, 1)

            def qk_product(ts):
                (q, s), r = ts, rows_of(ts)
                n = q * RING + s
                dve.wait_ge(qkv_copied, n + 1)
                chain["qk"].start(n)
                q_ = qkv[0:r, s, 0:DVE_HEADS * HD].rearrange("p (h d) -> p h d", h=DVE_HEADS)
                k_ = qkv[0:r, s, C:2 * C].rearrange("p (g d) -> p g d", g=NH)
                chain["qk"].link(dve.tensor_tensor(
                    prod[0:r, :].rearrange("p (h g d) -> p h g d", h=DVE_HEADS, g=NH),
                    q_.unsqueeze(2).broadcast_to([r, DVE_HEADS, NH, HD]),
                    k_.unsqueeze(1).broadcast_to([r, DVE_HEADS, NH, HD]), ALU.mult))

            def qk_reduce(ts):
                (q, s), r = ts, rows_of(ts)
                n = q * RING + s
                c = chain["qk"]
                c.base, c.k = n * c.per, 1
                wait(dve, prob_done, n - 1)
                lg = logits[0:r, s % 2, :]
                dve.tensor_reduce(lg[:, 0:DVE_HEADS * NH], prod[0:r, :].rearrange("p (a d) -> p a d", d=HD), AX.X, ALU.add)
                dve.wait_ge(pq_done, n + 1)
                c.link(dve.tensor_reduce(lg[:, DVE_HEADS * NH:], pq[0:r, :].rearrange("p (a d) -> p a d", d=HD), AX.X, ALU.add))
                lg = lg.rearrange("p (h g) -> p h g", h=NH)
                c.link(dve.tensor_reduce(lmax[0:r, :], lg, AX.X, ALU.max))
                dve.tensor_tensor(lg, lg, lmax[0:r, :].unsqueeze(2).broadcast_to([r, NH, NH]), ALU.subtract).then_inc(logits_done, 1)

            def attend(ts):
                (q, s), r = ts, rows_of(ts)
                n = q * RING + s
                c = chain["pv"]
                c.start(n)
                dve.wait_ge(prob_done, n + 1)
                p_ = prob[0:r, s % 2, :].rearrange("p (h g) -> p h g", h=NH)
                v_ = qkv[0:r, s, 2 * C:].rearrange("p (d g) -> p d g", g=NH)
                dve.tensor_tensor(
                    prod[0:r, :].rearrange("p (h d g) -> p h d g", h=DVE_HEADS, d=HD),
                    p_[:, 0:DVE_HEADS, :].unsqueeze(2).broadcast_to([r, DVE_HEADS, HD, NH]),
                    v_.unsqueeze(1).broadcast_to([r, DVE_HEADS, HD, NH]), ALU.mult).then_inc(c.sem, 1)
                c.k = 1
                c.link(dve.tensor_reduce(psums[0:r, 0, :], p_, AX.X, ALU.add))
                c.link(dve.reciprocal(psums[0:r, 1, :], psums[0:r, 0, :]))
                wait(dve, att_stored[s], 16 * q)
                a = att[0:r, s, :]
                c.link(dve.tensor_reduce(a[:, 0:DVE_HEADS * HD], prod[0:r, :].rearrange("p (a g) -> p a g", g=NH), AX.X, ALU.add))
                dve.wait_ge(pv_done, n + 1)
                c.link(dve.tensor_reduce(a[:, DVE_HEADS * HD:], pv[0:r, :].rearrange("p (a g) -> p a g", g=NH), AX.X, ALU.add))
                a = a.rearrange("p (h d) -> p h d", h=NH)
                dve.tensor_tensor(a, a, psums[0:r, 1, :].unsqueeze(2).broadcast_to([r, NH, HD]), ALU.mult).then_inc(att_done, 1)

            def step(at, u, m):
                if ts := at(0):
                    stats_of(ts)
                if ts := at(1):
                    qk_product(ts)
                if ts := at(0):
                    normalise(ts)
                if ts := at(1):
                    qk_reduce(ts)
                if ts := at(2):
                    attend(ts)

            pipeline(dve, NT, 1, 3, RING + 1, step, odd=1)


def route_stage(nc, kept, w_o, b_o, w_router, w_gu, b_gate, b_up, w_down, b_down, ident, upper, table, steps,
                h_dram, att_dram, routed, h2_dram):
    gu_hi, gu_lo, inv_scale, id16 = kept["gu_hi"], kept["gu_lo"], kept["inv_scale"], kept["id16"]
    bu, step_tab, banks = kept["bu"], kept["step_tab"], kept["banks"]
    ATTT_BANK, Y_BANK, Z2T_BANK, RL_BANK, R_BANK = banks[0:5]
    with ExitStack() as ctx:
        def sb(name, shape, dt=F32):
            return ctx.enter_context(nc.sbuf_tensor(name, shape, dt))

        def sem(name):
            return ctx.enter_context(nc.semaphore(name))

        wo = sb("wo", [P, KC, C])
        bo = sb("bo", [1, C])
        wr = sb("wr", [P, KC, E])
        gu_in = sb("gu_in", [P, GU])
        tab = sb("tab", [P, T_COLS])
        id32 = sb("id32b", [P, P])
        upper32 = sb("upper32", [P, P])
        upper16 = sb("upper16", [P, P], BF16)
        ones16 = sb("ones16", [P, P], BF16)
        ones_row = sb("ones_row_b", [1, P])
        half = sb("half_b", [P, 1])
        steps_in = sb("steps_in", [1, NJ + NR])
        sel = sb("sel", [1, 3, NJ, E])
        tiles_cmp = sb("tiles_cmp", [1, E, NR])
        step_f = sb("step_f", [1, 4, NJ])
        h = sb("h_ring", [P, RING, C])
        att = sb("att_rows", [P, RING, C])
        attt = sb("attt", [P, 2, KC, P])
        stats2 = sb("stats2", [P, 6])
        mv2 = sb("mv2", [P, 2, 2])
        rstd2 = sb("rstd2", [P, 2, 2])
        z2 = sb("z2", [P, 2, C])
        z2t = sb("z2t", [P, 2, KC, P])
        zx = sb("zx", [P, RING, TOPK, ROW])
        rl = sb("rl", [P, E])
        top = sb("top", [P, 2, E])
        neg_top = sb("neg_top", [P, 2, 1])
        ex = sb("ex", [P, 2, E + 1])
        top_i = sb("top_i", [P, E], U32)
        top_f = sb("top_f", [P, TOPK])
        rsum = sb("rsum", [P, 1])
        pk = sb("pk", [P, TOPK])
        den = sb("den", [P, 2])
        mask = sb("mask", [P, 2, TOPK, E])
        mask16 = sb("mask16", [P, 2, E], BF16)
        count = sb("count", [P, E])
        ranks = sb("ranks", [P, E])
        ranked = sb("ranked", [P, TOPK, E])
        slot_f = sb("slot_f", [P, TOPK])
        slot = sb("slot", [P, 2, TOPK], U32)
        target = sb("target", [P, TOPK])
        gmax = sb("gmax", [P, 5])
        pad_row = sb("pad_row", [P, ROW])
        pad_f = sb("pad_f", [P, RT, E + 1])
        pad_slot = sb("pad_slot", [P, RT, E + 1], U32)
        n_f = sb("n_f", [1, 5, E])

        consts, filled, cast, pads_filled = sem("consts_b"), sem("filled_b"), sem("cast"), sem("pads_filled")
        h_loaded = [sem(f"h_loaded{s}") for s in range(RING)]
        att_loaded = [sem(f"att_loaded{s}") for s in range(RING)]
        h2_stored = [sem(f"h2_stored{s}") for s in range(RING)]
        attt_done, attt_copied, y_done, h2_done = sem("attt_done"), sem("attt_copied"), sem("y_done"), sem("h2_done")
        stats2_done, eps2_added, rstd2_done, z2_done = (sem(n) for n in ("stats2_done", "eps2_added", "rstd2_done", "z2_done"))
        z2t_done, z2t_copied, rl_done, rl_read = sem("z2t_done"), sem("z2t_copied"), sem("rl_done"), sem("rl_read")
        sorted_done, ex_done, zx_done = sem("sorted_done"), sem("ex_done"), sem("zx_done")
        mask_done, rank_done, slot_done, rank_read = sem("mask_done"), sem("rank_done"), sem("slot_done"), sem("rank_read")
        scattered = [sem(f"scattered{s}") for s in range(RING)]
        gu_loaded, gmax_done, gmax_all = sem("gu_loaded"), sem("gmax_done"), sem("gmax_all")
        scale_done, gu_hi_done, gu_split = sem("scale_done"), sem("gu_hi_done"), sem("gu_split")
        pad_slots_done, padded, expert_loaded = sem("pad_slots_done"), sem("padded"), sem("expert_loaded")
        links = {n: sem(f"{n}_link") for n in ("stats2", "zx", "sort", "weight", "slot", "scale", "table")}

        N_CONSTS = 16 * 8
        block = ctx.enter_context(nc.Block())

        def run(eng, step):
            pipeline(eng, NT, 1, 5, 2 * RING + 1, step, odd=1)

        def preparing(m):
            return None if m is None or isinstance(m, int) and m < -2 else m + 3

        @block.sync
        def _(sp):
            def load(dst, src, s):
                sp.dma_start(dst, src).then_inc(s, 16)

            load(id32[:, :], ident, consts)
            load(wo[:, :, :], w_o, consts)
            load(bo[:, :], b_o, consts)
            load(gu_in[:, :], w_gu[0], gu_loaded)
            load(wr[:, :, :], w_router, consts)
            load(tab[:, :], table, consts)
            load(steps_in[:, :], steps, consts)
            load(upper32[:, :], upper, consts)
            load(bu[:, :], b_up, consts)

            def step(at, u, m):
                if ts := at(-1):
                    (q, s), r = ts, rows_of(ts)
                    n = q * RING + s
                    wait(sp, h2_stored[s], 16 * q)
                    apart(sp)
                    wait(sp, z2_done, n - 3)
                    sp.dma_start(h[0:r, s, :], rows_at(h_dram, n * P, r)).then_inc(h_loaded[s], 16)
                    wait(sp, attt_done, n - 3)
                    if is_cls(ts):
                        src = att_dram.rearrange("b h n d -> b (h n d)")[:, 0:C]
                    else:
                        src = rows_at(att_rows, q * (S + 1) + 1, S).rearrange("(p t) c -> p t c", t=TPB)[:, s, :]
                    sp.dma_start(att[0:r, s, :], src).then_inc(att_loaded[s], 16)
                if u == 0 and (e := preparing(m)) is not None:
                    sp.wait_ge(gu_split, e)
                    sp.dma_start(gu_in[:, :], dyn_row(w_gu, e)).then_inc(gu_loaded, 16)
                if ts := at(2):
                    (q, s), r = ts, rows_of(ts)
                    n = q * RING + s
                    sp.wait_ge(h2_done, n + 1)
                    sp.dma_start(rows_at(h2_dram, n * P, r), h[0:r, s, :]).then_inc(h2_stored[s], 16)

            att_rows = att_dram.rearrange("b h n d -> (b h n d)").rearrange("(r c) -> r c", c=C)
            run(sp, step)
            load(kept["bg"][:, :], b_gate, expert_loaded)
            load(kept["down"][:, :], w_down, expert_loaded)
            load(kept["bd"][:, :], b_down.broadcast_to([P, E * C]), expert_loaded)
            for s in range(RING):
                sp.wait_ge(h2_stored[s], 16 * ((NT - 1 - s) // RING + 1))
            sp.wait_ge(expert_loaded, 48)

        @block.gpsimd
        def _(pool):
            pool.memset(half[:, :], -0.5).then_inc(filled, 1)
            pool.memset(ones16[:, :], 1.0).then_inc(filled, 1)
            pool.memset(ones_row[:, :], 1.0).then_inc(filled, 1)
            pool.memset(pad_row[:, :], 0.0).then_inc(pads_filled, 1)
            pool.wait_ge(pads_filled, 1)
            pool.wait_ge(consts, N_CONSTS)
            pool.tensor_copy(pad_row[:, ROW - 1:ROW].bitcast(U32), tab[:, T_FAR:T_FAR + 1]).then_inc(pads_filled, 1)
            pool.tensor_copy(upper16[:, :], upper32[:, :]).then_inc(cast, 1)
            pool.tensor_copy(id16[:, :], id32[:, :]).then_inc(cast, 1)

            def weight_max(e):
                pool.wait_ge(gmax_done, e + 1)
                apart(pool)
                pool.partition_all_reduce(gmax[:, 1:2], gmax[:, 0:1], P, bass.bass_isa.ReduceOp.max).then_inc(gmax_all, 1)

            def inverse_root(ts, ready, used, added, done, m, r_):
                (q, s), r = ts, rows_of(ts)
                n = q * RING + s
                pool.wait_ge(ready, n + 1)
                wait(pool, used, n - 1)
                apart(pool)
                pool.tensor_scalar(r_[0:r, s % 2, 0:1], m[0:r, s % 2, 1:2], EPS, None, ALU.add).then_inc(added, 1)
                pool.wait_ge(added, n + 1)
                pool.tensor_tensor(r_[0:r, s % 2, 1:2], r_[0:r, s % 2, 0:1], half[0:r, :], ALU.pow).then_inc(done, 1)

            def step(at, u, m):
                if ts := at(5):
                    (q, s), r = ts, rows_of(ts)
                    pool.wait_ge(zx_done, q * RING + s + 1)
                    pool.wait_ge(slot_done, q * RING + s + 1)
                    apart(pool)
                    for k in range(TOPK):
                        pool.indirect_dma_start(
                            out=routed[:, :], out_offset=bass.IndirectOffsetOnAxis(ap=slot[0:r, s % 2, k:k + 1], axis=0),
                            in_=zx[0:r, s, k, :], in_offset=None).then_inc(scattered[s], 16)
                if ts := at(1):
                    inverse_root(ts, stats2_done, z2_done, eps2_added, rstd2_done, mv2, rstd2)
                if u == 1 and (e := preparing(m)) is not None:
                    weight_max(e)

            weight_max(0)
            run(pool, step)
            pool.wait_ge(pads_filled, 2)
            pool.wait_ge(pad_slots_done, 1)
            for i, e in ((i, e) for i in range(RT) for e in range(E + 1)):
                pool.indirect_dma_start(
                    out=routed[:, :], out_offset=bass.IndirectOffsetOnAxis(ap=pad_slot[:, i, e:e + 1], axis=0),
                    in_=pad_row[:, :], in_offset=None).then_inc(padded, 16)
            pool.wait_ge(padded, 16 * RT * (E + 1))
            for s in range(RING):
                pool.wait_ge(scattered[s], 16 * TOPK * ((NT - 1 - s) // RING + 1))

        @block.scalar
        def _(act):
            def copy(done, dst, src):
                act.activation(dst, src, ACT.Copy).then_inc(done, 1)

            def split_high(e):
                act.wait_ge(scale_done, e + 1)
                dst = gu_hi[:, e * GU:(e + 1) * GU] if isinstance(e, int) else gu_hi[:, bass.ds(e * GU, GU)]
                act.activation(dst, gu_in[:, :], ACT.Copy, scale=gmax[:, 4:5]).then_inc(gu_hi_done, 1)

            def step(at, u, m):
                if ts := at(3):
                    (q, s), r = ts, rows_of(ts)
                    n = q * RING + s
                    act.wait_ge(sorted_done, n + 1)
                    wait(act, zx_done, n - 1)
                    act.activation(ex[0:r, s % 2, 0:E], top[0:r, s % 2, :], ACT.Exp, bias=neg_top[0:r, s % 2, :],
                                   accum_out=ex[0:r, s % 2, E:E + 1]).then_inc(ex_done, 1)
                if ts := at(0):
                    (q, s), r = ts, rows_of(ts)
                    n = q * RING + s
                    act.wait_ge(attt_done, n + 1)
                    wait(act, y_done, n - 1)
                    copy(attt_copied, attt[:, s % 2, :, 0:r], ATTT_BANK[:, 0:KC * P].rearrange("p (k t) -> p k t", k=KC)[:, :, 0:r])
                if ts := at(2):
                    (q, s), r = ts, rows_of(ts)
                    n = q * RING + s
                    act.wait_ge(z2t_done, n + 1)
                    wait(act, rl_done, n - 1)
                    copy(z2t_copied, z2t[:, s % 2, :, 0:r], Z2T_BANK[:, 0:KC * P].rearrange("p (k t) -> p k t", k=KC)[:, :, 0:r])
                if u == 2 and (e := preparing(m)) is not None:
                    split_high(e)

            split_high(0)
            run(act, step)

        @block.tensor
        def _(pe):
            def transpose(bank, src, r):
                for c in range(KC):
                    last = pe.transpose(bank[:, c * P:c * P + r], src[0:r, c * P:(c + 1) * P], id32[0:r, 0:r])
                return last

            def step(at, u, m):
                if ts := at(1):
                    (q, s), r = ts, rows_of(ts)
                    n = q * RING + s
                    pe.wait_ge(attt_copied, n + 1)
                    wait(pe, h2_done, n)
                    pe.matmul(Y_BANK[0:r, 0:C], ones_row[:, 0:r], bo[:, :], start=True, stop=False)
                    for c in range(KC):
                        last = pe.matmul(Y_BANK[0:r, 0:C], attt[:, s % 2, c, 0:r], wo[:, c, :], start=False, stop=c == KC - 1)
                    last.then_inc(y_done, 1)
                if ts := at(4):
                    (q, s), r = ts, rows_of(ts)
                    n = q * RING + s
                    pe.wait_ge(mask_done, n + 1)
                    wait(pe, rank_read, n)
                    pe.matmul(R_BANK[0:r, E:2 * E], upper16[0:r, 0:r], mask16[0:r, s % 2, :], start=True, stop=True)
                    pe.matmul(R_BANK[:, 2 * E:3 * E], ones16[0:r, :], mask16[0:r, s % 2, :], start=True, stop=True).then_inc(rank_done, 1)
                if ts := at(3):
                    (q, s), r = ts, rows_of(ts)
                    n = q * RING + s
                    pe.wait_ge(z2t_copied, n + 1)
                    wait(pe, rl_read, n)
                    for c in range(KC):
                        last = pe.matmul(RL_BANK[0:r, 0:E], z2t[:, s % 2, c, 0:r], wr[:, c, :], start=c == 0, stop=c == KC - 1)
                    last.then_inc(rl_done, 1)
                if ts := at(0):
                    (q, s), r = ts, rows_of(ts)
                    n = q * RING + s
                    pe.wait_ge(att_loaded[s], 16 * (q + 1))
                    wait(pe, attt_copied, n)
                    transpose(ATTT_BANK, att[:, s, :], r).then_inc(attt_done, 1)
                if ts := at(2):
                    (q, s), r = ts, rows_of(ts)
                    n = q * RING + s
                    pe.wait_ge(z2_done, n + 1)
                    wait(pe, z2t_copied, n)
                    transpose(Z2T_BANK, z2[:, s % 2, :], r).then_inc(z2t_done, 1)

            pe.wait_ge(consts, N_CONSTS)
            pe.wait_ge(cast, 2)
            pe.wait_ge(filled, 3)
            run(pe, step)

        @block.vector
        def _(dve):
            chain = {n: Chain(dve, links[n], per) for n, per in
                     dict(stats2=1, zx=2, sort=5, weight=5, slot=3, scale=4, table=40).items()}
            dve.wait_ge(consts, N_CONSTS)
            dve.tensor_copy(count[:, :], tab[:, T_BASE:T_BASE + E])
            dve.tensor_copy(target[:, :], tab[:, T_TARGET:T_TARGET + TOPK])

            def weight_size(e):
                dve.wait_ge(gu_loaded, 16 * (e + 1))
                dve.tensor_reduce(gmax[:, 0:1], gu_in[:, :], AX.X, ALU.max, apply_absolute_value=True).then_inc(gmax_done, 1)

            def weight_scale(e):
                c = chain["scale"]
                c.start(e)
                dve.wait_ge(gmax_all, e + 1)
                c.link(dve.tensor_scalar(gmax[:, 2:3].bitcast(U32), gmax[:, 1:2].bitcast(U32), 0x7F800000, None, ALU.bitwise_and))
                c.link(dve.tensor_scalar(gmax[:, 2:3], gmax[:, 2:3], 2.0 ** -60, None, ALU.max))
                c.link(dve.reciprocal(gmax[:, 3:4], gmax[:, 2:3]))
                c.link(dve.tensor_scalar(gmax[:, 4:5], gmax[:, 3:4], WS, None, ALU.mult))
                inv = inv_scale[:, e:e + 1] if isinstance(e, int) else inv_scale[:, bass.ds(e, 1)]
                b = bu[:, e * MC:(e + 1) * MC] if isinstance(e, int) else bu[:, bass.ds(e * MC, MC)]
                dve.tensor_scalar(inv, gmax[:, 2:3], 1.0 / (WS * ZS), None, ALU.mult)
                dve.tensor_scalar(b, b, gmax[:, 4:5], ZS, ALU.mult, ALU.mult).then_inc(scale_done, 1)

            def split_low(e):
                dve.wait_ge(gu_hi_done, e + 1)
                lo, hi = ((t[:, e * GU:(e + 1) * GU] if isinstance(e, int) else t[:, bass.ds(e * GU, GU)]) for t in (gu_lo, gu_hi))
                dve.scalar_tensor_tensor(lo, gu_in[:, :], gmax[:, 4:5], hi, ALU.mult, ALU.subtract).then_inc(gu_split, 1)

            def slots_of(ts):
                (q, s), r = ts, rows_of(ts)
                n = q * RING + s
                c = chain["slot"]
                c.start(n)
                dve.wait_ge(rank_done, n + 1)
                c.link(dve.tensor_tensor(ranks[0:r, :], R_BANK[0:r, E:2 * E], count[0:r, :], ALU.add))
                c.link(dve.tensor_tensor(ranked[0:r, :, :], mask[0:r, s % 2, :, :],
                                         ranks[0:r, :].unsqueeze(1).broadcast_to([r, TOPK, E]), ALU.mult))
                c.link(dve.tensor_reduce(slot_f[0:r, :], ranked[0:r, :, :], AX.X, ALU.add))
                wait(dve, scattered[(s + 2) % RING], 16 * TOPK * (q + s // 2))
                dve.tensor_copy(slot[0:r, s % 2, :], slot_f[0:r, :]).then_inc(slot_done, 1)
                dve.tensor_tensor(count[:, :], R_BANK[:, 2 * E:3 * E], count[:, :], ALU.add).then_inc(rank_read, 1)

            def residual(ts):
                (q, s), r = ts, rows_of(ts)
                n = q * RING + s
                dve.wait_ge(y_done, n + 1)
                dve.wait_ge(h_loaded[s], 16 * (q + 1))
                dve.tensor_tensor(h[0:r, s, :], Y_BANK[0:r, 0:C], h[0:r, s, :], ALU.add).then_inc(h2_done, 1)
                dve.wait_ge(h2_done, n + 1)
                chain["stats2"].start(n)
                chain["stats2"].link(dve.bn_stats(stats2[0:r, :], h[0:r, s, :]))
                apart(dve)
                dve.bn_aggr(mv2[0:r, s % 2, :], stats2[0:r, :]).then_inc(stats2_done, 1)

            def normalise2(ts):
                (q, s), r = ts, rows_of(ts)
                n = q * RING + s
                c = chain["zx"]
                c.start(n)
                dve.wait_ge(rstd2_done, n + 1)
                wait(dve, z2t_done, n - 1)
                dve.tensor_scalar(z2[0:r, s % 2, :], h[0:r, s, :], mv2[0:r, s % 2, 0:1], rstd2[0:r, s % 2, 1:2],
                                  ALU.subtract, ALU.mult).then_inc(z2_done, 1)
                wait(dve, scattered[s], 16 * TOPK * q)
                dve.wait_ge(z2_done, n + 1)
                halves = [zx[0:r, s, k, 0:C].bitcast(F16) for k in range(TOPK)]
                c.link(dve.tensor_scalar(halves[0][:, 0:C], z2[0:r, s % 2, :], ZS, None, ALU.mult))
                c.link(dve.scalar_tensor_tensor(halves[0][:, C:], z2[0:r, s % 2, :], ZS, halves[0][:, 0:C], ALU.mult, ALU.subtract))
                dve.tensor_copy(halves[1], halves[0])

            def route(ts):
                (q, s), r = ts, rows_of(ts)
                n = q * RING + s
                c = chain["sort"]
                c.start(n)
                dve.wait_ge(rl_done, n + 1)
                dve.tensor_copy(rl[0:r, :], RL_BANK[0:r, 0:E]).then_inc(rl_read, 1)
                dve.wait_ge(rl_read, n + 1)
                apart(dve)
                c.link(dve.max(top[0:r, s % 2, :], rl[0:r, :]))
                dve.tensor_scalar(neg_top[0:r, s % 2, :], top[0:r, s % 2, 0:1], -1.0, None, ALU.mult).then_inc(sorted_done, 1)
                c.link(dve.max_index(top_i[0:r, :], top[0:r, s % 2, :], rl[0:r, :]))
                c.link(dve.tensor_copy(top_f[0:r, :], top_i[0:r, 0:TOPK]))
                for k in range(TOPK):
                    c.link(dve.tensor_scalar(mask[0:r, s % 2, k, :], tab[0:r, T_IOTA:T_IOTA + E], top_f[0:r, k:k + 1], None, ALU.is_equal))
                wait(dve, rank_done, n - 1)
                dve.tensor_tensor(mask16[0:r, s % 2, :], mask[0:r, s % 2, 0, :], mask[0:r, s % 2, 1, :], ALU.add).then_inc(mask_done, 1)

            def weights_of(ts):
                (q, s), r = ts, rows_of(ts)
                n = q * RING + s
                c = chain["weight"]
                c.start(n)
                dve.wait_ge(ex_done, n + 1)
                c.link(dve.reciprocal(rsum[0:r, :], ex[0:r, s % 2, E:E + 1]))
                c.link(dve.tensor_scalar(pk[0:r, :], ex[0:r, s % 2, 0:TOPK], rsum[0:r, :], None, ALU.mult))
                c.link(dve.tensor_scalar(den[0:r, 0:1], pk[0:r, 0:1], pk[0:r, 1:2], 1e-8, ALU.add, ALU.add))
                c.link(dve.reciprocal(den[0:r, 1:2], den[0:r, 0:1]))
                dve.tensor_scalar(zx[0:r, s, :, C], pk[0:r, :], den[0:r, 1:2], None, ALU.mult)
                c.link(dve.tensor_copy(zx[0:r, s, :, C + 1].bitcast(U32), target[0:r, :]))
                dve.tensor_scalar(target[:, :], target[:, :], float(TOPK * P), None, ALU.add).then_inc(zx_done, 1)

            def step(at, u, m):
                if ts := at(2):
                    normalise2(ts)
                if ts := at(4):
                    slots_of(ts)
                    weights_of(ts)
                if ts := at(3):
                    route(ts)
                if ts := at(1):
                    residual(ts)
                if u == 0 and (e := preparing(m)) is not None:
                    weight_size(e)
                if u == 1 and (e := preparing(m)) is not None:
                    weight_scale(e)
                if u == 2 and (e := preparing(m)) is not None:
                    split_low(e)

            weight_size(0)
            weight_scale(0)
            split_low(0)
            run(dve, step)

            c = chain["table"]
            c.start(0)
            dve.wait_ge(rank_read, NT)
            for i in range(RT):
                dve.tensor_scalar(pad_f[:, i, 0:E], count[:, :], tab[:, T_PART:T_PART + 1], float(i * P), ALU.add, ALU.add)
                c.link(dve.tensor_scalar(pad_f[:, i, E:E + 1], tab[:, T_PART:T_PART + 1], float(E * REG + i * P), None, ALU.add))
            dve.tensor_copy(pad_slot[:, :, :], pad_f[:, :, :]).then_inc(pad_slots_done, 1)
            rows_, tiles_, end_, begin_, start_ = (n_f[:, i, :] for i in range(5))
            c.link(dve.tensor_tensor(rows_, count[0:1, :], tab[0:1, T_BASE:T_BASE + E], ALU.subtract))
            c.link(dve.tensor_tensor(tiles_cmp[:, :, :], rows_.unsqueeze(2).broadcast_to([1, E, NR]),
                                     steps_in[:, NJ:].unsqueeze(1).broadcast_to([1, E, NR]), ALU.is_gt))
            c.link(dve.tensor_reduce(tiles_, tiles_cmp[:, :, :], AX.X, ALU.add))
            c.link(dve.tensor_tensor_scan(end_, tiles_, tiles_, 0.0, ALU.add, ALU.bypass))
            c.link(dve.tensor_tensor(begin_, end_, tiles_, ALU.subtract))
            c.link(dve.scalar_tensor_tensor(start_, begin_, -float(TR), tab[0:1, T_BASE:T_BASE + E], ALU.mult, ALU.add))
            j_ = steps_in[:, 0:NJ]
            j_b = j_.unsqueeze(2).broadcast_to([1, NJ, E])
            past, reached, mine = (sel[:, i, :, :] for i in range(3))
            c.link(dve.tensor_tensor(past, j_b, end_.unsqueeze(1).broadcast_to([1, NJ, E]), ALU.is_ge))
            c.link(dve.tensor_tensor(reached, j_b, begin_.unsqueeze(1).broadcast_to([1, NJ, E]), ALU.is_ge))
            c.link(dve.tensor_tensor(mine, reached, past, ALU.subtract))
            c.link(dve.tensor_tensor(mine, mine, start_.unsqueeze(1).broadcast_to([1, NJ, E]), ALU.mult))
            expert_, row_, used_, tmp_ = (step_f[:, i, :] for i in range(4))
            c.link(dve.tensor_reduce(expert_, past, AX.X, ALU.add))
            c.link(dve.tensor_reduce(tmp_, mine, AX.X, ALU.add))
            c.link(dve.scalar_tensor_tensor(row_, j_, float(TR), tmp_, ALU.mult, ALU.add))
            c.link(dve.tensor_scalar(used_, expert_, float(E), None, ALU.is_lt))
            c.link(dve.tensor_scalar(row_, row_, -float(E * REG), None, ALU.add))
            c.link(dve.tensor_tensor(row_, row_, used_, ALU.mult))
            c.link(dve.tensor_scalar(step_tab[:, NJ:], row_, float(E * REG), None, ALU.add))
            c.link(dve.tensor_scalar(step_tab[:, 0:NJ], expert_, float(E - 1), None, ALU.min))


def expert_stage(nc, kept, routed, expert_out):
    gu_hi, gu_lo, down, bg, bu, bd = (kept[n] for n in ("gu_hi", "gu_lo", "down", "bg", "bu", "bd"))
    inv_scale, id16, step_tab, banks = (kept[n] for n in ("inv_scale", "id16", "step_tab", "banks"))
    GU_BANK, ZT_BANK, Y_BANK = banks[0:4], banks[4:6], banks[6:8]
    with ExitStack() as ctx:
        def sb(name, shape, dt=F32):
            return ctx.enter_context(nc.sbuf_tensor(name, shape, dt))

        def sem(name):
            return ctx.enter_context(nc.semaphore(name))

        zg = sb("zg", [P, RING, RT, ROW])
        zt = sb("zt", [P, 2, 2 * KC, TR], F16)
        sg = sb("sg", [P, MC, TR])
        hid = sb("hid", [P, 2, MC, TR])
        ye = sb("ye", [P, 2, RT, C])
        yw = sb("yw", [P, 2, RT, C])
        loaded = [sem(f"loaded{s}") for s in range(RING)]
        stored = [sem("stored0"), sem("stored1")]
        zt_done, zt_copied, gu_done = sem("zt_done"), sem("zt_copied"), sem("gu_done")
        silu_done, hid_done, y_done, ye_done, yw_done = (sem(n) for n in ("silu_done", "hid_done", "ye_psum", "ye_done", "yw_done"))
        block = ctx.enter_context(nc.Block())

        def expert(eng, n):
            return eng.value_load(step_tab[0:1, n:n + 1] if isinstance(n, int) else step_tab[0:1, bass.ds(n, 1)],
                                  min_val=0, max_val=E - 1)

        def run(eng, step):
            pipeline(eng, NJ, 2, 1, 6, step)

        @block.sync
        def _(sp):
            def step(at, u, m):
                if ts := at(-2):
                    q, s = ts
                    n = q * RING + s
                    wait(sp, stored[s % 2], 16 * RT * (2 * q + s // 2 - 1))
                    i = NJ + n
                    row = sp.value_load(step_tab[0:1, i:i + 1] if isinstance(i, int) else step_tab[0:1, bass.ds(i, 1)],
                                        min_val=0, max_val=E * REG)
                    sp.dma_start(zg[:, s, :, :], routed[bass.ds(row, TR), :].rearrange("(p t) r -> p t r", t=RT)).then_inc(loaded[s], 16)

            run(sp, step)

        @block.gpsimd
        def _(pool):
            def step(at, u, m):
                if ts := at(1):
                    q, s = ts
                    n = q * RING + s
                    for t in range(RT):
                        pool.wait_ge(yw_done, n * RT + t + 1)
                        apart(pool)
                        pool.indirect_dma_start(
                            out=expert_out[:, :],
                            out_offset=bass.IndirectOffsetOnAxis(ap=zg[:, s, t, ROW - 1:ROW].bitcast(U32), axis=0),
                            in_=yw[:, s % 2, t, :], in_offset=None, bounds_check=OUT_ROWS - 1, oob_is_err=False).then_inc(stored[s % 2], 16)

            run(pool, step)
            pool.wait_ge(stored[0], 16 * RT * (NJ // 2))
            pool.wait_ge(stored[1], 16 * RT * (NJ // 2))

        @block.scalar
        def _(act):
            def step(at, u, m):
                if ts := at(0):
                    q, s = ts
                    n = q * RING + s
                    e = expert(act, n)
                for c in range(MC):
                    if at(0):
                        act.wait_ge(gu_done, n * MC + c + 1)
                        wait(act, hid_done, n * MC + c + 1 - MC)
                        act.activation(sg[:, c, :], GU_BANK[c][:, 0:TR], ACT.Silu,
                                       scale=inv_scale[:, bass.ds(e, 1)], bias=bg[:, bass.ds(e * MC + c, 1)]).then_inc(silu_done, 1)
                    if c == 0 and (ts := at(1)):
                        q1, s1 = ts
                        wait(act, stored[s1 % 2], 16 * RT * (2 * q1 + s1 // 2))
                        for t in range(RT):
                            act.wait_ge(ye_done, (q1 * RING + s1) * RT + t + 1)
                            act.activation(yw[:, s1 % 2, t, :], ye[:, s1 % 2, t, :], ACT.Copy, scale=zg[:, s1, t, C:C + 1]).then_inc(yw_done, 1)
                if ts := at(-1):
                    q, s = ts
                    n = q * RING + s
                    act.wait_ge(zt_done, n + 1)
                    wait(act, gu_done, (n - 1) * MC)
                    act.activation(zt[:, s % 2, :, :].rearrange("p k t -> p (k t)"), ZT_BANK[s % 2][:, :].bitcast(F16), ACT.Copy).then_inc(zt_copied, 1)

            run(act, step)

        @block.vector
        def _(dve):
            def step(at, u, m):
                if ts := at(1):
                    q, s = ts
                    n = q * RING + s
                    e = expert(dve, n)
                    for t in range(RT):
                        dve.wait_ge(y_done, n * RT + t + 1)
                        wait(dve, yw_done, (n - 2) * RT + t + 1)
                        dve.scalar_tensor_tensor(ye[:, s % 2, t, :], Y_BANK[t][:, 0:C], inv_scale[:, bass.ds(e, 1)],
                                                 bd[:, bass.ds(e * C, C)], ALU.mult, ALU.add).then_inc(ye_done, 1)
                if ts := at(0):
                    q, s = ts
                    n = q * RING + s
                    e = expert(dve, n)
                    wait(dve, y_done, (n - 1) * RT)
                    for c in range(MC):
                        dve.wait_ge(silu_done, n * MC + c + 1)
                        dve.scalar_tensor_tensor(hid[:, s % 2, c, :], GU_BANK[c][:, TR:2 * TR], bu[:, bass.ds(e * MC + c, 1)],
                                                 sg[:, c, :], ALU.add, ALU.mult).then_inc(hid_done, 1)

            run(dve, step)

        @block.tensor
        def _(pe):
            def step(at, u, m):
                if ts := at(0):
                    q, s = ts
                    n = q * RING + s
                    e = expert(pe, n)

                def gate_up(c):
                    wait(pe, hid_done, n * MC + c + 1 - MC)
                    for half_ in range(2):
                        dst = GU_BANK[c][:, half_ * TR:(half_ + 1) * TR]
                        for k in range(KC):
                            at_ = e * GU + (k * 2 * M + half_ * M + c * P)
                            hi, lo = gu_hi[:, bass.ds(at_, P)], gu_lo[:, bass.ds(at_, P)]
                            z_hi, z_lo = zt[:, s % 2, k, :], zt[:, s % 2, KC + k, :]
                            pe.matmul(dst, hi, z_hi, start=k == 0, stop=False)
                            pe.matmul(dst, hi, z_lo, start=False, stop=False)
                            last = pe.matmul(dst, lo, z_hi, start=False, stop=k == KC - 1)
                    last.then_inc(gu_done, 1)

                def project(c):
                    pe.wait_ge(hid_done, n * MC + c + 1)
                    for t in range(RT):
                        if c == 0:
                            wait(pe, ye_done, (n - 1) * RT + t + 1)
                        last = pe.matmul(Y_BANK[t][:, 0:C], hid[:, s % 2, c, t * P:(t + 1) * P],
                                         down[:, bass.ds(e * (MC * C) + c * C, C)], start=c == 0, stop=c == MC - 1)
                        if c == MC - 1:
                            last.then_inc(y_done, 1)

                if at(0):
                    pe.wait_ge(zt_copied, n + 1)
                    for c in range(MC):
                        gate_up(c)
                        if c >= 2:
                            project(c - 2)
                if ts := at(-1):
                    q1, s1 = ts
                    pe.wait_ge(loaded[s1], 16 * (q1 + 1))
                    wait(pe, zt_copied, q1 * RING + s1 - 1)
                    bank = ZT_BANK[s1 % 2][:, :].bitcast(F16)
                    for t in range(RT):
                        halves = zg[:, s1, t, 0:C].bitcast(F16)
                        for c in range(2 * KC):
                            last = pe.transpose(bank[:, c * TR + t * P:c * TR + (t + 1) * P], halves[:, c * P:(c + 1) * P], id16[:, :])
                    last.then_inc(zt_done, 1)
                if at(0):
                    project(MC - 2)
                    project(MC - 1)

            run(pe, step)


def dyn_batch(ap, n):
    if isinstance(n, int):
        return ap[n]
    return ap[bass.ds(n, 1)].rearrange("a p t n -> (a p) t n")


def combine_stage(nc, expert_out, h2_dram, out):
    SP_ = S // P
    with ExitStack() as ctx:
        def sb(name, shape, dt=F32):
            return ctx.enter_context(nc.sbuf_tensor(name, shape, dt))

        def sem(name):
            return ctx.enter_context(nc.semaphore(name))

        eo = sb("eo", [P, 2, SP_, TOPK, C])
        hh = sb("hh", [P, 2, SP_, C])
        oo = sb("oo", [P, 2, SP_, C])
        cls_eo = sb("cls_eo", [B, TOPK, C])
        cls_h = sb("cls_h", [B, C])
        in_loaded = [sem("in_loaded0"), sem("in_loaded1")]
        summed, half_summed = sem("summed"), sem("half_summed")
        out_stored = [sem("out_stored0"), sem("out_stored1")]
        cls_in, cls_sum, cls_out = sem("cls_in"), sem("cls_sum"), sem("cls_out")
        block = ctx.enter_context(nc.Block())
        eo_v = expert_out[0:TOPK * B * S, :].rearrange("(b t p k) c -> b p t (k c)", b=B, p=P, k=TOPK)
        h_v = h2_dram[0:B * S, :].rearrange("(b t p) c -> b p t c", b=B, p=P)

        @block.sync
        def _(sp):
            sp.dma_start(cls_eo[:, :, :], expert_out[TOPK * B * S:, :].rearrange("(b k) c -> b k c", k=TOPK)).then_inc(cls_in, 16)
            sp.dma_start(cls_h[:, :], h2_dram[B * S:, :]).then_inc(cls_in, 16)

            def load(m):
                for s in range(2):
                    wait(sp, summed, m * 2 + s - 1)
                    sp.dma_start(eo[:, s, :, :, :].rearrange("p t k c -> p t (k c)"), dyn_batch(eo_v, m * 2 + s)).then_inc(in_loaded[s], 16)
                    sp.dma_start(hh[:, s, :, :], dyn_batch(h_v, m * 2 + s)).then_inc(in_loaded[s], 16)

            load(0)
            with sp.Fori(1, B // 2) as m:
                load(m)

        @block.vector
        def _(dve):
            dve.wait_ge(cls_in, 32)
            dve.tensor_tensor(cls_eo[:, 0, :], cls_eo[:, 0, :], cls_eo[:, 1, :], ALU.add).then_inc(cls_sum, 1)
            dve.wait_ge(cls_sum, 1)
            dve.tensor_tensor(cls_h[:, :], cls_h[:, :], cls_eo[:, 0, :], ALU.add).then_inc(cls_sum, 1)

            def add(m):
                for s in range(2):
                    dve.wait_ge(in_loaded[s], m * 32 + 32)
                    wait(dve, out_stored[s], m * 16)
                    dve.tensor_tensor(oo[:, s, :, :], eo[:, s, :, 0, :], eo[:, s, :, 1, :], ALU.add).then_inc(half_summed, 1)
                    dve.wait_ge(half_summed, m * 2 + s + 1)
                    dve.tensor_tensor(oo[:, s, :, :], oo[:, s, :, :], hh[:, s, :, :], ALU.add).then_inc(summed, 1)

            add(0)
            with dve.Fori(1, B // 2) as m:
                add(m)

        @block.scalar
        def _(act):
            act.wait_ge(cls_sum, 2)
            act.dma_start(out[:, 0, :], cls_h[:, :]).then_inc(cls_out, 16)
            with act.Fori(0, B // 2) as m:
                for s in range(2):
                    act.wait_ge(summed, m * 2 + s + 1)
                    dst = out[bass.ds(m * 2 + s, 1), 1:, :].rearrange("b (p s) c -> (b p) (s c)", s=SP_)
                    act.dma_start(dst, oo[:, s, :, :].rearrange("p s c -> p (s c)")).then_inc(out_stored[s], 16)
            act.wait_ge(cls_out, 16)
            act.wait_ge(out_stored[0], 16 * (B // 2))
            act.wait_ge(out_stored[1], 16 * (B // 2))


def kernel(x, cls_tok, L0_tok_weight, L0_tok_weighted_sum, L0_attn_w_qkv, L0_attn_b_qkv, L0_attn_w_out, L0_attn_b_out,
           L0_ffn_W_router, L0_ffn_W_gate, L0_ffn_b_gate, L0_ffn_W_up, L0_ffn_b_up, L0_ffn_W_out, L0_ffn_b_out):
    import numpy as np
    import concourse.bacc as bacc
    from concourse.bass_utils import run_bass_kernel_spmd as run

    def chunked(w):
        return w.reshape(w.shape[0] // P, P, w.shape[1]).transpose(1, 0, 2)

    a = {k: np.asarray(v) for k, v in dict(
        x=x, cls=cls_tok, tw=L0_tok_weight, tws=L0_tok_weighted_sum, wqkv=L0_attn_w_qkv, bqkv=L0_attn_b_qkv,
        wo=L0_attn_w_out, bo=L0_attn_b_out, wr=L0_ffn_W_router, wg=L0_ffn_W_gate, bg=L0_ffn_b_gate, wu=L0_ffn_W_up,
        bu=L0_ffn_b_up, wd=L0_ffn_W_out, bd=L0_ffn_b_out).items()}
    perm = np.concatenate([np.arange(2 * C), 2 * C + np.arange(C).reshape(NH, HD).T.ravel()])
    gu = np.stack([a["wg"], a["wu"]], 2).reshape(E, KC, P, 2 * M).transpose(0, 2, 1, 3).reshape(E, P, GU)
    table = np.zeros((P, T_COLS), np.float32)
    table[:, T_IOTA:T_IOTA + E] = np.arange(E)
    table[:, T_BASE:T_BASE + E] = np.arange(E) * REG
    table[:, T_TARGET:T_TARGET + TOPK] = np.arange(P)[:, None] * TOPK + np.arange(TOPK)
    table[:, T_FAR] = FAR
    table[:, T_PART] = np.arange(P)
    arrays = dict(
        x_t=a["x"].reshape(B, P, TPB, KC, P, D1).transpose(0, 2, 4, 5, 3, 1).reshape(NT - 1, P, XC * P),
        cls=a["cls"].reshape(1, C),
        tok_w=a["tw"].T,
        tok_ws=chunked(a["tws"].T),
        w_qkv=chunked(a["wqkv"][perm].T),
        b_qkv=a["bqkv"][perm].reshape(1, 3 * C),
        w_o=chunked(a["wo"].T),
        b_o=a["bo"].reshape(1, C),
        w_router=chunked(a["wr"]),
        w_gu=gu,
        b_gate=a["bg"].reshape(E, MC, P).transpose(2, 0, 1).reshape(P, E * MC),
        b_up=a["bu"].reshape(E, MC, P).transpose(2, 0, 1).reshape(P, E * MC),
        w_down=a["wd"].reshape(E, MC, P, C).transpose(2, 0, 1, 3).reshape(P, E * MC * C),
        b_down=a["bd"].reshape(1, E * C),
        ident=np.eye(P, dtype=np.float32),
        upper=np.triu(np.ones((P, P), np.float32), 1),
        table=table,
        steps=np.concatenate([np.arange(NJ), TR * np.arange(NR)]).astype(np.float32).reshape(1, -1),
    )
    nc = bacc.Bacc("TRN2", target_bir_lowering=False, num_devices=1)
    ins, aps = {}, {}
    for name, v in arrays.items():
        ins[f"in_{name}"] = np.ascontiguousarray(v)
        aps[name] = nc.dram_tensor(f"in_{name}", v.shape, mybir.dt.from_np(v.dtype), kind="ExternalInput").ap()
    aps["out"] = nc.dram_tensor("result", (B, S + 1, C), F32, kind="ExternalOutput").ap()
    vit_block(nc, **aps)
    return run(nc, [ins], core_ids=[0]).results[0]["result"]
```

```python
import concourse.bass as bass
from concourse import mybir
from contextlib import ExitStack

F32 = mybir.dt.float32
F16 = mybir.dt.float16
BF16 = mybir.dt.bfloat16
I32 = mybir.dt.int32
U32 = mybir.dt.uint32
ALU = mybir.AluOpType
ACT = mybir.ActivationFunctionType
AX = mybir.AxisListType

B, S, C, D1 = 8, 512, 256, 4
NH, HD = 16, 16
E, M, TOPK = 8, 512, 2
P = 128
KC = C // P
XC = C * D1 // P
MC = M // P
GU = KC * 2 * M
TPB = S // P
NT = B * TPB + 1
NTOK = B * (S + 1)
RING = 4
TRING = 2 * TPB
RT = 2
TR = RT * P
REG = NTOK + TR
NJ = (NTOK * TOPK + E * (TR - 1)) // TR
NR = NTOK // TR + 1
ROW = C + 2
OUT_ROWS = NTOK * TOPK
FAR = 1 << 20
ZS = 256.0
WS = 16384.0
DVE_HEADS, MIXED_HEADS, PE_HEADS = 7, 3, 6
SUM_HEADS = DVE_HEADS + MIXED_HEADS
SCALE = float(C) ** -0.5
EPS = 1e-5
T_IOTA, T_BASE, T_TARGET, T_FAR = 0, E, 2 * E, 2 * E + TPB * TOPK
T_COLS = T_FAR + 1


def tile_at(t, n, ring):
    return (t // ring, t % ring) if 0 <= t < n else None


def pipeline(eng, n, ahead, behind, first, step, odd=0, ring=RING):
    loops = (n - odd - ahead - first) // ring
    for i in range(-ahead, first):
        step(lambda lag, i=i: tile_at(i - lag, n, ring), (i - first) % ring, (i - first) // ring)
    with eng.Fori(0, loops) as m:
        for u in range(ring):
            step(lambda lag, u=u: (m + (first + u - lag) // ring, (first + u - lag) % ring), u, m)
    for i in range(first + loops * ring, n + behind):
        step(lambda lag, i=i: tile_at(i - lag, n, ring), (i - first) % ring, (i - first) // ring)


def wait(eng, sem, value):
    if not isinstance(value, int) or value > 0:
        eng.wait_ge(sem, value)


def apart(eng):
    eng.nop(nofuse=True)


class Chain:

    def __init__(self, eng, sem, per):
        self.eng, self.sem, self.per = eng, sem, per

    def start(self, n):
        self.base, self.k = n * self.per, 0

    def link(self, ins):
        ins.then_inc(self.sem, 1)
        self.k += 1
        assert self.k <= self.per
        self.eng.wait_ge(self.sem, self.base + self.k)


def is_cls(ts, ring=RING):
    return isinstance(ts[0], int) and ts[0] * ring + ts[1] == NT - 1


def rows_of(ts, ring=RING):
    return B if is_cls(ts, ring) else P


def at_tile(ts):
    return ts[0] * TRING + ts[1], ts[1], rows_of(ts, TRING)


def split_bias(dve, done, rows, parts, rest, one_hot):
    k = 0

    def link(ins):
        nonlocal k
        ins.then_inc(done, 1)
        k += 1
        dve.wait_ge(done, k)

    for i in range(3):
        link(dve.tensor_copy(parts[:, i, :], rows if i == 0 else rest))
        if i < 2:
            link(dve.tensor_tensor(rest, rows if i == 0 else rest, parts[:, i, :], ALU.subtract))
    link(dve.tensor_scalar(parts[:, 0, :], parts[:, 0, :], one_hot[:, 0:1], None, ALU.mult))
    for i in (1, 2):
        link(dve.scalar_tensor_tensor(parts[:, 0, :], parts[:, i, :], one_hot[:, i:i + 1], parts[:, 0, :], ALU.mult, ALU.add))


def rows_at(ap, start, n):
    return ap[start:start + n, :] if isinstance(start, int) else ap[bass.ds(start, n), :]


def of_tile(t, n, r):
    return t[0:r, n, :] if isinstance(n, int) else t[0:r, bass.ds(n, 1), :].rearrange("p a c -> p (a c)")


def dyn_row(ap, n):
    if isinstance(n, int):
        return ap[n]
    return ap[bass.ds(n, 1)].rearrange("a p n -> (a p) n")


def vit_block(nc, x_t, cls, tok_w, tok_ws, w_qkv, b_qkv, w_o, b_o, w_router, w_gu, b_gate, b_up,
              w_down, b_down, ident, upper, table, steps, out):
    with ExitStack() as ctx:
        ctx.enter_context(nc.allow_low_precision("fp16 halves of fp32 values; masks of zeros and ones"))

        def sb(name, shape, dt=F32):
            return ctx.enter_context(nc.sbuf_tensor(name, shape, dt))

        routed = nc.dram_tensor("routed", [E * REG + TR, ROW], F32, kind="Internal").ap()
        expert_out = nc.dram_tensor("expert_out", [OUT_ROWS, C], F32, kind="Internal").ap()
        att_dram = nc.dram_tensor("att_dram", [B, NH, S + 1, HD], F32, kind="Internal").ap()

        h = sb("h", [P, NT, C])
        banks = [ctx.enter_context(nc.psum_tensor(f"bank{i}", [P, 512], F32)) for i in range(8)]
        later = dict(
            wo=(sb("wo", [P, KC, C]), w_o),
            bo=(sb("bo", [3, C]), b_o.broadcast_to([3, C])),
            wr=(sb("wr", [P, KC, E]), w_router),
            tab=(sb("tab", [P, T_COLS]), table),
            id32=(sb("id32", [P, P]), ident),
            upper32=(sb("upper32", [P, P]), upper),
            steps_in=(sb("steps_in", [1, NJ + NR]), steps),
            bu=(sb("bu", [P, E * MC]), b_up),
            bg=(sb("bg", [P, E * MC]), b_gate),
            down=(sb("down", [P, E * MC * C]), w_down),
            bd=(sb("bd", [P, E * C]), b_down.broadcast_to([P, E * C])),
        )
        attend_stage(nc, banks, later, x_t, cls, tok_w, tok_ws, w_qkv, b_qkv, h, att_dram)
        with ExitStack() as experts:
            def expert_sb(name, shape, dt=F32):
                return experts.enter_context(nc.sbuf_tensor(name, shape, dt))

            kept = {name: t for name, (t, _) in later.items()} | dict(
                gu_hi=expert_sb("gu_hi", [P, E * GU], F16),
                gu_lo=expert_sb("gu_lo", [P, E * GU], F16),
                inv_scale=expert_sb("inv_scale", [P, E]),
                id16=expert_sb("id16", [P, P], F16),
                step_tab=expert_sb("step_tab", [1, 2 * NJ], I32),
                banks=banks,
            )
            route_stage(nc, kept, w_gu, h, att_dram, routed)
            expert_stage(nc, kept, routed, expert_out)
        combine_stage(nc, expert_out, h, out)


def attend_stage(nc, banks, later, x_t, cls, tok_w, tok_ws, w_qkv, b_qkv, h, att_dram):
    H_BANK, QK_BANK, V_BANK, Z1T_BANK = banks[0:4]
    L_BANK, A_BANK = banks[4:6], banks[6:8]
    id32, ident = later["id32"]
    with ExitStack() as ctx:
        def sb(name, shape, dt=F32):
            return ctx.enter_context(nc.sbuf_tensor(name, shape, dt))

        def sem(name):
            return ctx.enter_context(nc.semaphore(name))

        xs = sb("xs", [P, 2, XC * P])
        wtok = sb("wtok", [P, XC, C])
        wqkv = sb("wqkv", [P, KC, 3 * C])
        bqkv = sb("bqkv", [3, 3 * C])
        ones16 = sb("ones16_a", [3, P], BF16)
        half = sb("half", [P, 1])
        stats = sb("stats", [P, RING, 3])
        squares = sb("squares", [P, C])
        rstd = sb("rstd", [P, 2, 3])
        z1 = sb("z1", [P, 2, C])
        z1t = sb("z1t", [P, 2, KC, P])
        qkv = sb("qkv", [P, TRING, 3 * C])
        prod = sb("prod", [P, DVE_HEADS * NH * HD])
        mixed_q = sb("mixed_q", [P, 2, MIXED_HEADS * NH * HD])
        mixed_v = sb("mixed_v", [P, 2, MIXED_HEADS * NH * HD])
        pq = sb("pq", [P, 2, HD, PE_HEADS * NH])
        pv = sb("pv", [P, 2, NH, PE_HEADS * HD])
        tokw = prod[:, 0:D1 * C].rearrange("p (d c) -> p d c", d=D1)
        tokws = prod[:, D1 * C:(D1 + KC) * C].rearrange("p (k c) -> p k c", k=KC)
        bias_rest = pq[0:3, 0, :, :].rearrange("p d a -> p (d a)")[:, 0:3 * C]
        bias_parts = sb("bias_parts", [3, 3, 3 * C], BF16)
        logits = sb("logits", [P, RING, NH * NH])
        lmax = sb("lmax", [P, NH])
        prob = sb("prob", [P, 2, NH * NH])
        psums = sb("psums", [P, NH])
        pinv = sb("pinv", [P, RING, NH])
        att = sb("att", [P, TRING, C])

        first_consts, consts, later_consts = sem("first_consts"), sem("consts"), sem("later_consts")
        filled, wtok_ready, bias_split = sem("filled"), sem("wtok_ready"), sem("bias_split_a")
        x_loaded = [sem("x_loaded0"), sem("x_loaded1")]
        cls_loaded, h_done, h_copied = sem("cls_loaded"), sem("h_done"), sem("h_copied")
        stats_done, eps_added, root_done, rstd_done = (sem(n) for n in ("stats_done", "eps_added", "root_done", "rstd_done"))
        mean_done = sem("mean_done")
        z1_done, z1t_done, z1t_copied = sem("z1_done"), sem("z1t_done"), sem("z1t_copied")
        qkv_done, qkv_copied = sem("qkv_done"), sem("qkv_copied")
        pq_done, pq_summed, logits_gathered, logits_summed = (sem(n) for n in ("pq_done", "pq_summed", "logits_gathered", "logits_summed"))
        logits_done, prob_done = sem("logits_done"), sem("prob_done")
        mixed_q_done, mixed_q_summed, mixed_v_done, mixed_v_summed = (sem(n) for n in ("mixed_q_done", "mixed_q_summed", "mixed_v_done", "mixed_v_summed"))
        values_gathered = sem("values_gathered")
        pv_done, pv_summed, prod_done, att_summed = (sem(n) for n in ("pv_done", "pv_summed", "prod_done", "att_summed"))
        att_done = sem("att_done")
        att_stored = [sem(f"att_stored{s}") for s in range(TRING)]
        links = {n: sem(f"{n}_link") for n in ("qk", "max", "sum")}

        N_CONSTS = 16 * 3
        block = ctx.enter_context(nc.Block())

        def run(eng, step):
            pipeline(eng, NT, 2, 8, TRING + 6, step, odd=1, ring=TRING)

        @block.sync
        def _(sp):
            def load(dst, src, s):
                sp.dma_start(dst, src).then_inc(s, 16)

            load(tokw[:, :, :], tok_w.unsqueeze(0).broadcast_to([P, D1, C]), first_consts)
            load(tokws[:, :, :], tok_ws, first_consts)
            for t in range(2):
                load(xs[:, t, :], x_t[t], x_loaded[t])
            load(h[0:B, NT - 1, :], cls.broadcast_to([B, C]), cls_loaded)
            load(id32[:, :], ident, consts)
            load(wqkv[:, :, :], w_qkv, consts)
            load(bqkv[:, :], b_qkv.broadcast_to([3, 3 * C]), consts)

            def step(at, u, m):
                if (ts := at(-2)) and isinstance(ts[0], int) and at_tile(ts)[0] == 4:
                    for name, (dst, src) in later.items():
                        if name != "id32":
                            load(dst[:], src, later_consts)
                if (ts := at(-2)) and not is_cls(ts, TRING):
                    n, s, r = at_tile(ts)
                    if not isinstance(n, int) or n >= 2:
                        wait(sp, h_done, n - 1)
                        load(xs[:, s % 2, :], dyn_row(x_t, n), x_loaded[s % 2])
                if ts := at(8):
                    n, s, r = at_tile(ts)
                    if is_cls(ts, TRING):
                        dst = att_dram[:, :, 0, :]
                    else:
                        b = ts[0] * (TRING // TPB) + s // TPB
                        dst = att_dram[b] if isinstance(b, int) else att_dram[bass.ds(b, 1)].rearrange("b h n d -> (b h) n d")
                        dst = dst[:, 1:, :].rearrange("h (p t) d -> p t h d", t=TPB)[:, s % TPB, :, :]
                    sp.wait_ge(att_done, n + 1)
                    sp.dma_start(dst, att[0:r, s, :].rearrange("p (h d) -> p h d", h=NH)).then_inc(att_stored[s], 16)

            run(sp, step)
            sp.wait_ge(later_consts, 16 * (len(later) - 1))
            for s in range(TRING):
                tiles = (NT - 1 - s) // TRING + 1
                sp.wait_ge(att_stored[s], 16 * tiles)

        @block.gpsimd
        def _(pool):
            pool.memset(half[:, :], -0.5).then_inc(filled, 1)
            pool.memset(ones16[:, :], 1.0).then_inc(filled, 1)
            pool.wait_ge(filled, 1)

            def values(ts, first, heads, dst, done):
                n, s, r = at_tile(ts)
                p_ = prob[0:r, s % 2, first * NH:(first + heads) * NH].rearrange("p (h g) -> p h g", h=heads)
                v_ = qkv[0:r, s, 2 * C:].rearrange("p (d g) -> p d g", g=NH)
                shape = [r, heads, HD, NH]
                pool.tensor_tensor(dst, p_.unsqueeze(2).broadcast_to(shape), v_.unsqueeze(1).broadcast_to(shape), ALU.mult).then_inc(done, 1)

            def keys(ts, first, heads, dst, done):
                n, s, r = at_tile(ts)
                q_ = qkv[0:r, s, first * HD:(first + heads) * HD].rearrange("p (h d) -> p h d", h=heads)
                k_ = qkv[0:r, s, C:2 * C].rearrange("p (g d) -> p g d", g=NH)
                shape = [r, heads, NH, HD]
                pool.tensor_tensor(dst, q_.unsqueeze(2).broadcast_to(shape), k_.unsqueeze(1).broadcast_to(shape), ALU.mult).then_inc(done, 1)

            def step(at, u, m):
                if ts := at(6):
                    n, s, r = at_tile(ts)
                    pool.wait_ge(prob_done, n + 1)
                    wait(pool, mixed_v_summed, n - 1)
                    wait(pool, pv_summed, n - 1)
                    values(ts, DVE_HEADS, MIXED_HEADS, mixed_v[0:r, s % 2, :].rearrange("p (h d g) -> p h d g", h=MIXED_HEADS, d=HD), mixed_v_done)
                    values(ts, SUM_HEADS, PE_HEADS, pv[0:r, s % 2, :, :].rearrange("p g (h d) -> p h d g", h=PE_HEADS), pv_done)
                if ts := at(3):
                    n, s, r = at_tile(ts)
                    pool.wait_ge(qkv_copied, n + 1)
                    wait(pool, mixed_q_summed, n - 1)
                    wait(pool, pq_summed, n - 1)
                    keys(ts, DVE_HEADS, MIXED_HEADS, mixed_q[0:r, s % 2, :].rearrange("p (h g d) -> p h g d", h=MIXED_HEADS, g=NH), mixed_q_done)
                    keys(ts, SUM_HEADS, PE_HEADS, pq[0:r, s % 2, :, :].rearrange("p d (h g) -> p h g d", h=PE_HEADS), pq_done)
                if ts := at(0):
                    n, s, r = at_tile(ts)
                    pool.wait_ge(stats_done, n + 1)
                    wait(pool, z1_done, n - 1)
                    apart(pool)
                    pool.tensor_scalar(rstd[0:r, s % 2, 0:1], stats[0:r, s % RING, 2:3], 1.0 / C, EPS, ALU.mult, ALU.add).then_inc(eps_added, 1)
                    pool.wait_ge(eps_added, n + 1)
                    pool.tensor_tensor(rstd[0:r, s % 2, 1:2], rstd[0:r, s % 2, 0:1], half[0:r, :], ALU.pow).then_inc(root_done, 1)
                    pool.wait_ge(root_done, n + 1)
                    pool.tensor_tensor(rstd[0:r, s % 2, 2:3], stats[0:r, s % RING, 1:2], rstd[0:r, s % 2, 1:2], ALU.mult).then_inc(rstd_done, 1)

            pool.wait_ge(bias_split, 8)
            run(pool, step)

        @block.scalar
        def _(act):
            def copy(done, dst, src):
                act.activation(dst, src, ACT.Copy).then_inc(done, 1)

            def step(at, u, m):
                if ts := at(0):
                    n, s, r = at_tile(ts)
                    of = stats[0:r, s % RING, :]
                    if is_cls(ts, TRING):
                        act.wait_ge(cls_loaded, 16)
                        act.activation(of_tile(h, n, r), of_tile(h, n, r), ACT.Copy, accum_out=of[:, 0:1]).then_inc(h_copied, 1)
                    act.wait_ge(h_copied, n + 1)
                    act.activation(of[:, 1:2], of[:, 0:1], ACT.Copy, scale=-1.0 / C).then_inc(mean_done, 1)
                if ts := at(1):
                    n, s, r = at_tile(ts)
                    act.wait_ge(rstd_done, n + 1)
                    wait(act, z1t_done, n - 1)
                    apart(act)
                    act.activation(z1[0:r, s % 2, :], of_tile(h, n, r), ACT.Identity, scale=rstd[0:r, s % 2, 1:2],
                                   bias=rstd[0:r, s % 2, 2:3]).then_inc(z1_done, 1)
                if ts := at(0):
                    n, s, r = at_tile(ts)
                    act.wait_ge(mean_done, n + 1)
                    wait(act, stats_done, n)
                    apart(act)
                    act.activation(squares[0:r, :], of_tile(h, n, r), ACT.Square, bias=stats[0:r, s % RING, 1:2],
                                   accum_out=stats[0:r, s % RING, 2:3]).then_inc(stats_done, 1)
                if ts := at(5):
                    n, s, r = at_tile(ts)
                    act.wait_ge(logits_done, n + 1)
                    wait(act, att_summed, n - 1)
                    wait(act, pv_done, n - 1)
                    act.activation(prob[0:r, s % 2, :], logits[0:r, s % RING, :], ACT.Exp, scale=SCALE).then_inc(prob_done, 1)
                if ts := at(2):
                    n, s, r = at_tile(ts)
                    act.wait_ge(qkv_done, n + 1)
                    wait(act, prod_done, n + 1 - TRING)
                    wait(act, pv_done, n + 1 - TRING)
                    act.activation(qkv[0:r, s, 0:2 * C], QK_BANK[0:r, :], ACT.Copy)
                    copy(qkv_copied, qkv[0:r, s, 2 * C:], V_BANK[0:r, 0:C])
                if ts := at(1):
                    n, s, r = at_tile(ts)
                    act.wait_ge(z1t_done, n + 1)
                    wait(act, qkv_done, n - 1)
                    copy(z1t_copied, z1t[:, s % 2, :, 0:r], Z1T_BANK[:, 0:KC * P].rearrange("p (k t) -> p k t", k=KC)[:, :, 0:r])
                if (ts := at(-1)) and not is_cls(ts, TRING):
                    n, s, r = at_tile(ts)
                    act.wait_ge(h_done, n + 1)
                    apart(act)
                    act.activation(of_tile(h, n, P), H_BANK[:, 0:C], ACT.Copy, accum_out=stats[:, s % RING, 0:1]).then_inc(h_copied, 1)

            run(act, step)

        @block.tensor
        def _(pe):
            def summed(bank, products, r, done):
                for i in range(0, HD, 2):
                    last = pe.matmul(bank[0:r, 0:2 * PE_HEADS * NH], id32[0:r, 0:r], products[:, i:i + 2, :].rearrange("p i a -> p (i a)"),
                                     start=i == 0, stop=i == HD - 2)
                last.then_inc(done, 1)

            def step(at, u, m):
                if ts := at(4):
                    n, s, r = at_tile(ts)
                    pe.wait_ge(pq_done, n + 1)
                    wait(pe, logits_gathered, n - 1)
                    summed(L_BANK[s % 2], pq[0:r, s % 2, :, :], r, pq_summed)
                if ts := at(7):
                    n, s, r = at_tile(ts)
                    pe.wait_ge(pv_done, n + 1)
                    wait(pe, values_gathered, n - 1)
                    summed(A_BANK[s % 2], pv[0:r, s % 2, :, :], r, pv_summed)
                if ts := at(2):
                    n, s, r = at_tile(ts)
                    if isinstance(n, int) and n == 0:
                        pe.wait_ge(filled, 2)
                        pe.wait_ge(bias_split, 8)
                    pe.wait_ge(z1t_copied, n + 1)
                    wait(pe, qkv_copied, n)
                    for bank, lo, hi in ((QK_BANK, 0, 2 * C), (V_BANK, 2 * C, 3 * C)):
                        pe.matmul(bank[0:r, 0:hi - lo], ones16[:, 0:r], bias_parts[:, 0, lo:hi], start=True, stop=False)
                        for c in range(KC):
                            last = pe.matmul(bank[0:r, 0:hi - lo], z1t[:, s % 2, c, 0:r], wqkv[:, c, lo:hi],
                                             start=False, stop=c == KC - 1)
                    last.then_inc(qkv_done, 1)
                if ts := at(1):
                    n, s, r = at_tile(ts)
                    if isinstance(n, int) and n == 0:
                        pe.wait_ge(consts, N_CONSTS)
                    pe.wait_ge(z1_done, n + 1)
                    wait(pe, z1t_copied, n)
                    for c in range(KC):
                        last = pe.transpose(Z1T_BANK[:, c * P:c * P + r], z1[0:r, s % 2, c * P:(c + 1) * P], id32[0:r, 0:r])
                    last.then_inc(z1t_done, 1)
                if (ts := at(-1)) and not is_cls(ts, TRING):
                    n, s, r = at_tile(ts)
                    pe.wait_ge(x_loaded[s % 2], 16 * (ts[0] * (TRING // 2) + s // 2 + 1))
                    wait(pe, h_copied, n)
                    for c in range(XC):
                        last = pe.matmul(H_BANK[:, 0:C], xs[:, s % 2, c * P:(c + 1) * P], wtok[:, c, :],
                                         start=c == 0, stop=c == XC - 1)
                    last.then_inc(h_done, 1)

            pe.wait_ge(wtok_ready, XC)
            run(pe, step)

        @block.vector
        def _(dve):
            chain = {n: Chain(dve, links[n], per) for n, per in dict(qk=1, max=1, sum=2).items()}

            dve.wait_ge(first_consts, 32)
            for d in range(D1):
                for c in range(KC):
                    dve.tensor_tensor(wtok[:, d * KC + c, :], tokws[:, c, :], tokw[:, d, :], ALU.mult).then_inc(wtok_ready, 1)
            dve.wait_ge(wtok_ready, XC)
            dve.wait_ge(consts, N_CONSTS)
            split_bias(dve, bias_split, bqkv[:, :], bias_parts, bias_rest, id32[0:3, 0:3])

            def halves_sum(bank, dst, done):
                dve.tensor_reduce(dst, bank[:, 0:2 * PE_HEADS * NH].rearrange("p (i a) -> p a i", i=2), AX.X, ALU.add).then_inc(done, 1)

            def gather_logits(ts):
                n, s, r = at_tile(ts)
                dve.wait_ge(pq_summed, n + 1)
                wait(dve, prob_done, n - 3)
                halves_sum(L_BANK[s % 2][0:r, :], logits[0:r, s % RING, SUM_HEADS * NH:], logits_gathered)

            def gather_values(ts):
                n, s, r = at_tile(ts)
                dve.wait_ge(pv_summed, n + 1)
                halves_sum(A_BANK[s % 2][0:r, :], att[0:r, s, SUM_HEADS * HD:], values_gathered)

            def subtract_largest(ts):
                n, s, r = at_tile(ts)
                dve.wait_ge(logits_gathered, n + 1)
                dve.wait_ge(logits_summed, n + 1)
                dve.wait_ge(mixed_q_summed, n + 1)
                lg = logits[0:r, s % RING, :].rearrange("p (h g) -> p h g", h=NH)
                chain["max"].start(n)
                chain["max"].link(dve.tensor_reduce(lmax[0:r, :], lg, AX.X, ALU.max))
                dve.tensor_tensor(lg, lg, lmax[0:r, :].unsqueeze(2).broadcast_to([r, NH, NH]), ALU.subtract).then_inc(logits_done, 1)

            def qk_product(ts):
                n, s, r = at_tile(ts)
                dve.wait_ge(qkv_copied, n + 1)
                wait(dve, logits_summed, n)
                wait(dve, att_summed, n - 3)
                chain["qk"].start(n)
                q_ = qkv[0:r, s, 0:DVE_HEADS * HD].rearrange("p (h d) -> p h d", h=DVE_HEADS)
                k_ = qkv[0:r, s, C:2 * C].rearrange("p (g d) -> p g d", g=NH)
                dve.tensor_tensor(
                    prod[0:r, :].rearrange("p (h g d) -> p h g d", h=DVE_HEADS, g=NH),
                    q_.unsqueeze(2).broadcast_to([r, DVE_HEADS, NH, HD]),
                    k_.unsqueeze(1).broadcast_to([r, DVE_HEADS, NH, HD]), ALU.mult).then_inc(links["qk"], 1)

            def scale_result(ts):
                n, s, r = at_tile(ts)
                dve.wait_ge(values_gathered, n + 1)
                dve.wait_ge(att_summed, n + 1)
                dve.wait_ge(mixed_v_summed, n + 1)
                heads = att[0:r, s, :].rearrange("p (h d) -> p h d", h=NH)
                dve.tensor_tensor(heads, heads, pinv[0:r, s % RING, :].unsqueeze(2).broadcast_to([r, NH, HD]), ALU.mult).then_inc(att_done, 1)

            def mixed_sum(ts, products, dst, done, summed):
                n, s, r = at_tile(ts)
                dve.wait_ge(done, n + 1)
                dve.tensor_reduce(dst[0:r, DVE_HEADS * NH:SUM_HEADS * NH], products[0:r, s % 2, :].rearrange("p (a d) -> p a d", d=HD),
                                  AX.X, ALU.add).then_inc(summed, 1)

            def qk_sum(ts):
                n, s, r = at_tile(ts)
                wait(dve, prob_done, n - 3)
                dve.wait_ge(links["qk"], n + 1)
                dve.tensor_reduce(logits[0:r, s % RING, 0:DVE_HEADS * NH], prod[0:r, :].rearrange("p (a d) -> p a d", d=HD),
                                  AX.X, ALU.add).then_inc(logits_summed, 1)

            def attend(ts, before):
                n, s, r = at_tile(ts)
                dve.wait_ge(prob_done, n + 1)
                if before:
                    dve.wait_ge(logits_summed, at_tile(before)[0] + 1)
                else:
                    wait(dve, att_summed, n)
                p_ = prob[0:r, s % 2, :].rearrange("p (h g) -> p h g", h=NH)
                v_ = qkv[0:r, s, 2 * C:].rearrange("p (d g) -> p d g", g=NH)
                dve.tensor_tensor(
                    prod[0:r, :].rearrange("p (h d g) -> p h d g", h=DVE_HEADS, d=HD),
                    p_[:, 0:DVE_HEADS, :].unsqueeze(2).broadcast_to([r, DVE_HEADS, HD, NH]),
                    v_.unsqueeze(1).broadcast_to([r, DVE_HEADS, HD, NH]), ALU.mult).then_inc(prod_done, 1)
                c = chain["sum"]
                c.start(n)
                c.link(dve.tensor_reduce(psums[0:r, :], p_, AX.X, ALU.add))
                c.link(dve.reciprocal(pinv[0:r, s % RING, :], psums[0:r, :]))
                wait(dve, att_stored[s], 16 * ts[0])
                dve.wait_ge(prod_done, n + 1)
                dve.tensor_reduce(att[0:r, s, 0:DVE_HEADS * HD], prod[0:r, :].rearrange("p (a g) -> p a g", g=NH),
                                  AX.X, ALU.add).then_inc(att_summed, 1)

            def step(at, u, m):
                if ts := at(5):
                    gather_logits(ts)
                if ts := at(8):
                    gather_values(ts)
                if ts := at(5):
                    subtract_largest(ts)
                if ts := at(7):
                    mixed_sum(ts, mixed_v, att[:, ts[1], :], mixed_v_done, mixed_v_summed)
                if ts := at(3):
                    qk_product(ts)
                if ts := at(8):
                    scale_result(ts)
                if ts := at(3):
                    qk_sum(ts)
                if ts := at(4):
                    mixed_sum(ts, mixed_q, logits[:, ts[1] % RING, :], mixed_q_done, mixed_q_summed)
                if ts := at(6):
                    attend(ts, at(3))

            run(dve, step)


def route_stage(nc, kept, w_gu, h, att_dram, routed):
    gu_hi, gu_lo, inv_scale, id16 = kept["gu_hi"], kept["gu_lo"], kept["inv_scale"], kept["id16"]
    bu, step_tab, banks = kept["bu"], kept["step_tab"], kept["banks"]
    wo, bo, wr, tab, id32, upper32, steps_in = (kept[n] for n in ("wo", "bo", "wr", "tab", "id32", "upper32", "steps_in"))
    ATTT_BANK, Z2T_BANK, R_BANK = banks[0:3]
    Y_BANK, RL_BANK = banks[3:5], banks[5:7]
    with ExitStack() as ctx:
        def sb(name, shape, dt=F32):
            return ctx.enter_context(nc.sbuf_tensor(name, shape, dt))

        def sem(name):
            return ctx.enter_context(nc.semaphore(name))

        bo_rest = sb("bo_rest", [3, C])
        bo_parts = sb("bo_parts", [3, 3, C], BF16)
        gu_in = sb("gu_in", [P, GU])
        upper16 = sb("upper16", [P, P], BF16)
        ones16 = sb("ones16", [P, P], BF16)
        half = sb("half_b", [P, 1])
        sel = sb("sel", [1, 3, NJ, E])
        tiles_cmp = sb("tiles_cmp", [1, E, NR])
        step_f = sb("step_f", [1, 4, NJ])
        att = sb("att_rows", [P, TRING, C])
        attt = sb("attt", [P, 2, KC, P])
        stats2 = sb("stats2", [P, 2, 6])
        mv2 = sb("mv2", [P, 2, 2])
        rstd2 = sb("rstd2", [P, 2, 3])
        z2 = sb("z2", [P, 2, C])
        z2t = sb("z2t", [P, 2, KC, P])
        zx = sb("zx", [P, TRING, TOPK, ROW])
        rl = sb("rl", [P, TPB, E])
        top = sb("top", [P, TPB, E])
        below = sb("below", [P, TPB, E])
        ex = sb("ex", [P, 2, TPB, E])
        top_i = sb("top_i", [P, TPB, E], U32)
        top_f = sb("top_f", [P, TPB, TOPK])
        total = sb("total", [P, 2, TPB])
        pk = sb("pk", [P, TPB, TOPK])
        den = sb("den", [P, 2, TPB])
        mask = sb("mask", [P, 2, TPB, TOPK, E])
        mask16 = sb("mask16", [P, TPB, E], BF16)
        count = sb("count", [P, E])
        ranks = sb("ranks", [P, TPB, E])
        ranked = sb("ranked", [P, TPB, TOPK, E])
        slot_f = sb("slot_f", [P, TPB, TOPK])
        slot = sb("slot", [P, 2, TPB, TOPK], U32)
        target = sb("target", [P, TPB, TOPK])
        gmax = sb("gmax", [P, 5])
        pad_rows = sb("pad_rows", [P, RT, ROW])
        pad_at = sb("pad_at", [1, E], I32)
        n_f = sb("n_f", [1, 5, E])

        filled, cast, pads_filled = sem("filled_b"), sem("cast"), sem("pads_filled")
        bias_split = sem("bias_split")
        att_loaded = [sem(f"att_loaded{s}") for s in range(TRING)]
        attt_done, attt_copied, y_done, h2_done = sem("attt_done"), sem("attt_copied"), sem("y_done"), sem("h2_done")
        stats2_done, eps2_added, rstd2_done, z2_done = (sem(n) for n in ("stats2_done", "eps2_added", "rstd2_done", "z2_done"))
        root2_done = sem("root2_done")
        high_done, low_done, rows_copied = sem("high_done"), sem("low_done"), sem("rows_copied")
        z2t_done, z2t_copied, rl_done, rl_read = sem("z2t_done"), sem("z2t_copied"), sem("rl_done"), sem("rl_read")
        below_done, ex_done, weights_done = sem("below_done"), sem("ex_done"), sem("weights_done")
        mask_done, rank_done, slot_done, rank_read = sem("mask_done"), sem("rank_done"), sem("slot_done"), sem("rank_read")
        scattered = [sem(f"scattered{s}") for s in range(TRING)]
        gu_loaded, gmax_done, gmax_all = sem("gu_loaded"), sem("gmax_done"), sem("gmax_all")
        scale_done, gu_hi_done, gu_split = sem("scale_done"), sem("gu_hi_done"), sem("gu_split")
        pad_at_done, padded = sem("pad_at_done"), sem("padded")
        links = {n: sem(f"{n}_link") for n in ("stats2", "sort", "weight", "slot", "scale", "table")}

        block = ctx.enter_context(nc.Block())

        def run(eng, step):
            pipeline(eng, NT, 1, 9, TRING + 4, step, odd=1, ring=TRING)

        def preparing(u, m):
            if u % TPB:
                return None
            e = m * 2 + (3 + u // TPB)
            return None if isinstance(e, int) and not 0 <= e < E else e

        def at_group(ts):
            q, s = ts
            if is_cls(ts, TRING):
                return q * 2 + s // TPB, s // TPB, s, 1, B
            if s % TPB == TPB - 1:
                return q * 2 + s // TPB, s // TPB, s - (TPB - 1), TPB, P
            return None

        @block.sync
        def _(sp):
            att_rows = att_dram.rearrange("b h n d -> (b h n d)").rearrange("(r c) -> r c", c=C)

            def step(at, u, m):
                if ts := at(-1):
                    n, s, r = at_tile(ts)
                    q = ts[0]
                    wait(sp, attt_done, n + 1 - TRING)
                    apart(sp)
                    if is_cls(ts, TRING):
                        src = att_dram.rearrange("b h n d -> b (h n d)")[:, 0:C]
                    else:
                        batch = q * (TRING // TPB) + s // TPB
                        src = rows_at(att_rows, batch * (S + 1) + 1, S).rearrange("(p t) c -> p t c", t=TPB)[:, s % TPB, :]
                    sp.dma_start(att[0:r, s, :], src).then_inc(att_loaded[s], 16)
                if (e := preparing(u, m)) is not None:
                    wait(sp, gu_split, e)
                    sp.dma_start(gu_in[:, :], dyn_row(w_gu, e)).then_inc(gu_loaded, 16)

            run(sp, step)
            sp.wait_ge(pads_filled, RT + 1)
            sp.dma_start(routed[E * REG:, :].rearrange("(p t) r -> p t r", t=RT), pad_rows[:, :, :]).then_inc(padded, 16)
            sp.wait_ge(pad_at_done, 1)
            for e in range(E):
                row = sp.value_load(pad_at[0:1, e:e + 1], min_val=e * REG, max_val=e * REG + NTOK)
                sp.dma_start(routed[bass.ds(row, TR), :].rearrange("(p t) r -> p t r", t=RT), pad_rows[:, :, :]).then_inc(padded, 16)
            sp.wait_ge(padded, 16 * (E + 1))

        @block.gpsimd
        def _(pool):
            pool.memset(half[:, :], -0.5).then_inc(filled, 1)
            pool.memset(ones16[:, :], 1.0).then_inc(filled, 1)
            pool.memset(pad_rows[:, :, :], 0.0).then_inc(pads_filled, 1)
            pool.wait_ge(pads_filled, 1)
            for t in range(RT):
                pool.tensor_copy(pad_rows[:, t, ROW - 1:ROW].bitcast(U32), tab[:, T_FAR:T_FAR + 1]).then_inc(pads_filled, 1)
            pool.tensor_copy(upper16[:, :], upper32[:, :]).then_inc(cast, 1)
            pool.tensor_copy(id16[:, :], id32[:, :]).then_inc(cast, 1)

            def weight_max(e):
                pool.wait_ge(gmax_done, e + 1)
                apart(pool)
                pool.partition_all_reduce(gmax[:, 1:2], gmax[:, 0:1], P, bass.bass_isa.ReduceOp.max).then_inc(gmax_all, 1)

            def inverse_root(ts):
                n, s, r = at_tile(ts)
                pool.wait_ge(stats2_done, n + 1)
                wait(pool, z2_done, n - 1)
                apart(pool)
                pool.tensor_scalar(rstd2[0:r, s % 2, 0:1], mv2[0:r, s % 2, 1:2], EPS, None, ALU.add).then_inc(eps2_added, 1)
                pool.wait_ge(eps2_added, n + 1)
                pool.tensor_tensor(rstd2[0:r, s % 2, 1:2], rstd2[0:r, s % 2, 0:1], half[0:r, :], ALU.pow).then_inc(root2_done, 1)
                pool.wait_ge(root2_done, n + 1)
                apart(pool)
                pool.tensor_scalar(rstd2[0:r, s % 2, 2:3], mv2[0:r, s % 2, 0:1], rstd2[0:r, s % 2, 1:2], -1.0, ALU.mult, ALU.mult).then_inc(rstd2_done, 1)

            def step(at, u, m):
                if ts := at(9):
                    n, s, r = at_tile(ts)
                    group = ts[0] * 2 + s // TPB + 1
                    pool.wait_ge(rows_copied, n + 1)
                    pool.wait_ge(weights_done, group)
                    pool.wait_ge(slot_done, group)
                    apart(pool)
                    for k in range(TOPK):
                        pool.indirect_dma_start(
                            out=routed[:, :],
                            out_offset=bass.IndirectOffsetOnAxis(ap=slot[0:r, s // TPB, s % TPB, k:k + 1], axis=0),
                            in_=zx[0:r, s, k, :], in_offset=None).then_inc(scattered[s], 16)
                if ts := at(1):
                    inverse_root(ts)
                if u >= 1 and (e := preparing(u - 1, m)) is not None:
                    weight_max(e)

            run(pool, step)
            for s in range(TRING):
                pool.wait_ge(scattered[s], 16 * TOPK * ((NT - 1 - s) // TRING + 1))

        @block.scalar
        def _(act):
            def copy(done, dst, src):
                act.activation(dst, src, ACT.Copy).then_inc(done, 1)

            def split_high(e):
                act.wait_ge(scale_done, e + 1)
                dst = gu_hi[:, e * GU:(e + 1) * GU] if isinstance(e, int) else gu_hi[:, bass.ds(e * GU, GU)]
                act.activation(dst, gu_in[:, :], ACT.Copy, scale=gmax[:, 4:5]).then_inc(gu_hi_done, 1)

            def step(at, u, m):
                if ts := at(0):
                    n, s, r = at_tile(ts)
                    act.wait_ge(attt_done, n + 1)
                    wait(act, y_done, n - 1)
                    copy(attt_copied, attt[:, s % 2, :, 0:r], ATTT_BANK[:, 0:KC * P].rearrange("p (k t) -> p k t", k=KC)[:, :, 0:r])
                if ts := at(3):
                    n, s, r = at_tile(ts)
                    act.wait_ge(z2_done, n + 1)
                    wait(act, scattered[s], 16 * TOPK * ts[0])
                    act.activation(zx[0:r, s, 0, 0:C].bitcast(F16)[:, 0:C], z2[0:r, s % 2, :], ACT.Copy, scale=ZS).then_inc(high_done, 1)
                if ts := at(5):
                    if of := at_group(ts):
                        g, odd_, s0, tiles, r = of
                        act.wait_ge(below_done, g + 1)
                        wait(act, weights_done, g)
                        act.activation(ex[0:r, odd_, 0:tiles, :], below[0:r, 0:tiles, :], ACT.Exp).then_inc(ex_done, 1)
                if ts := at(3):
                    n, s, r = at_tile(ts)
                    act.wait_ge(z2t_done, n + 1)
                    wait(act, rl_done, n - 1)
                    copy(z2t_copied, z2t[:, s % 2, :, 0:r], Z2T_BANK[:, 0:KC * P].rearrange("p (k t) -> p k t", k=KC)[:, :, 0:r])
                if ts := at(4):
                    n, s, r = at_tile(ts)
                    act.wait_ge(low_done, n + 1)
                    act.activation(zx[0:r, s, 1, 0:C].bitcast(F16), zx[0:r, s, 0, 0:C].bitcast(F16), ACT.Copy).then_inc(rows_copied, 1)
                if ts := at(2):
                    n, s, r = at_tile(ts)
                    act.wait_ge(rstd2_done, n + 1)
                    wait(act, z2t_done, n - 1)
                    wait(act, low_done, n - 1)
                    apart(act)
                    act.activation(z2[0:r, s % 2, :], of_tile(h, n, r), ACT.Identity, scale=rstd2[0:r, s % 2, 1:2],
                                   bias=rstd2[0:r, s % 2, 2:3]).then_inc(z2_done, 1)
                if u >= 2 and (e := preparing(u - 2, m)) is not None:
                    split_high(e)

            run(act, step)

        @block.tensor
        def _(pe):
            def transpose(bank, src, r):
                for c in range(KC):
                    last = pe.transpose(bank[:, c * P:c * P + r], src[0:r, c * P:(c + 1) * P], id32[0:r, 0:r])
                return last

            def step(at, u, m):
                if ts := at(0):
                    n, s, r = at_tile(ts)
                    pe.wait_ge(att_loaded[s], 16 * (ts[0] + 1))
                    wait(pe, attt_copied, n)
                    transpose(ATTT_BANK, att[:, s, :], r).then_inc(attt_done, 1)
                if ts := at(1):
                    n, s, r = at_tile(ts)
                    if isinstance(n, int) and n == 0:
                        pe.wait_ge(cast, 2)
                        pe.wait_ge(filled, 2)
                        pe.wait_ge(bias_split, 8)
                    pe.wait_ge(attt_copied, n + 1)
                    wait(pe, h2_done, n - 1)
                    pe.matmul(Y_BANK[s % 2][0:r, 0:C], ones16[0:3, 0:r], bo_parts[:, 0, :], start=True, stop=False)
                    for c in range(KC):
                        last = pe.matmul(Y_BANK[s % 2][0:r, 0:C], attt[:, s % 2, c, 0:r], wo[:, c, :], start=False, stop=c == KC - 1)
                    last.then_inc(y_done, 1)
                if ts := at(3):
                    n, s, r = at_tile(ts)
                    pe.wait_ge(z2_done, n + 1)
                    wait(pe, z2t_copied, n)
                    transpose(Z2T_BANK, z2[:, s % 2, :], r).then_inc(z2t_done, 1)
                if (ts := at(6)) and (of := at_group(ts)):
                    g, odd_, s0, tiles, r = of
                    pe.wait_ge(mask_done, g + 1)
                    wait(pe, rank_read, g)
                    pe.matmul(R_BANK[0:r, 0:tiles * E], upper16[0:r, 0:r], mask16[0:r, 0:tiles, :], start=True, stop=tiles == 1)
                    for t in range(1, tiles):
                        pe.matmul(R_BANK[0:r, t * E:tiles * E], ones16[0:r, 0:r], mask16[0:r, 0:tiles - t, :], start=False, stop=t == tiles - 1)
                    for t in range(tiles):
                        last = pe.matmul(R_BANK[:, TPB * E:(TPB + 1) * E], ones16[0:r, :], mask16[0:r, t, :], start=t == 0, stop=t == tiles - 1)
                    last.then_inc(rank_done, 1)
                if ts := at(4):
                    n, s, r = at_tile(ts)
                    pe.wait_ge(z2t_copied, n + 1)
                    if s % TPB == 0:
                        wait(pe, rl_read, ts[0] * 2 + s // TPB - 1)
                    for c in range(KC):
                        last = pe.matmul(RL_BANK[s // TPB][0:r, (s % TPB) * E:(s % TPB + 1) * E], z2t[:, s % 2, c, 0:r], wr[:, c, :],
                                         start=c == 0, stop=c == KC - 1)
                    last.then_inc(rl_done, 1)

            run(pe, step)

        @block.vector
        def _(dve):
            chain = {n: Chain(dve, links[n], per) for n, per in
                     dict(stats2=1, sort=4, weight=5, slot=3, scale=4, table=20).items()}
            dve.tensor_copy(count[:, :], tab[:, T_BASE:T_BASE + E])
            dve.tensor_copy(target[:, :, :].rearrange("p t k -> p (t k)"), tab[:, T_TARGET:T_FAR])
            split_bias(dve, bias_split, bo[:, :], bo_parts, bo_rest[:, :], id32[0:3, 0:3])

            def weight_size(e):
                dve.wait_ge(gu_loaded, 16 * (e + 1))
                dve.tensor_reduce(gmax[:, 0:1], gu_in[:, :], AX.X, ALU.max, apply_absolute_value=True).then_inc(gmax_done, 1)

            def weight_scale(e):
                c = chain["scale"]
                c.start(e)
                dve.wait_ge(gmax_all, e + 1)
                c.link(dve.tensor_scalar(gmax[:, 2:3].bitcast(U32), gmax[:, 1:2].bitcast(U32), 0x7F800000, None, ALU.bitwise_and))
                c.link(dve.tensor_scalar(gmax[:, 2:3], gmax[:, 2:3], 2.0 ** -60, None, ALU.max))
                c.link(dve.reciprocal(gmax[:, 3:4], gmax[:, 2:3]))
                c.link(dve.tensor_scalar(gmax[:, 4:5], gmax[:, 3:4], WS, None, ALU.mult))
                inv = inv_scale[:, e:e + 1] if isinstance(e, int) else inv_scale[:, bass.ds(e, 1)]
                b = bu[:, e * MC:(e + 1) * MC] if isinstance(e, int) else bu[:, bass.ds(e * MC, MC)]
                dve.tensor_scalar(inv, gmax[:, 2:3], 1.0 / (WS * ZS), None, ALU.mult)
                dve.tensor_scalar(b, b, gmax[:, 4:5], ZS, ALU.mult, ALU.mult).then_inc(scale_done, 1)

            def split_low(e):
                dve.wait_ge(gu_hi_done, e + 1)
                lo, hi = ((t[:, e * GU:(e + 1) * GU] if isinstance(e, int) else t[:, bass.ds(e * GU, GU)]) for t in (gu_lo, gu_hi))
                dve.scalar_tensor_tensor(lo, gu_in[:, :], gmax[:, 4:5], hi, ALU.mult, ALU.subtract).then_inc(gu_split, 1)

            def residual(ts):
                n, s, r = at_tile(ts)
                dve.wait_ge(y_done, n + 1)
                row = of_tile(h, n, r)
                dve.tensor_tensor(row, Y_BANK[s % 2][0:r, 0:C], row, ALU.add).then_inc(h2_done, 1)
                dve.wait_ge(h2_done, n + 1)
                wait(dve, rstd2_done, n - 1)
                apart(dve)
                chain["stats2"].start(n)
                chain["stats2"].link(dve.bn_stats(stats2[0:r, s % 2, :], row))
                apart(dve)
                dve.bn_aggr(mv2[0:r, s % 2, :], stats2[0:r, s % 2, :]).then_inc(stats2_done, 1)

            def split_row(ts):
                n, s, r = at_tile(ts)
                dve.wait_ge(high_done, n + 1)
                halves = zx[0:r, s, 0, 0:C].bitcast(F16)
                dve.scalar_tensor_tensor(halves[:, C:], z2[0:r, s % 2, :], ZS, halves[:, 0:C], ALU.mult, ALU.subtract).then_inc(low_done, 1)

            def route(g, odd_, s0, tiles, r, n):
                c = chain["sort"]
                c.start(g)
                dve.wait_ge(rl_done, n + 1)
                dve.tensor_copy(rl[0:r, 0:tiles, :].rearrange("p t e -> p (t e)"), RL_BANK[odd_][0:r, 0:tiles * E]).then_inc(rl_read, 1)
                dve.wait_ge(rl_read, g + 1)
                apart(dve)
                for t in range(tiles):
                    last = dve.max(top[0:r, t, :], rl[0:r, t, :])
                c.link(last)
                apart(dve)
                for t in range(tiles):
                    last = dve.max_index(top_i[0:r, t, :], top[0:r, t, :], rl[0:r, t, :])
                last.then_inc(c.sem, 1)
                wait(dve, ex_done, g)
                dve.tensor_tensor(below[0:r, 0:tiles, :], top[0:r, 0:tiles, :], top[0:r, 0:tiles, 0:1].broadcast_to([r, tiles, E]),
                                  ALU.subtract).then_inc(below_done, 1)
                c.k += 1
                dve.wait_ge(c.sem, c.base + c.k)
                c.link(dve.tensor_copy(top_f[0:r, 0:tiles, :], top_i[0:r, 0:tiles, 0:TOPK]))
                every = [r, tiles, TOPK, E]
                c.link(dve.tensor_tensor(mask[0:r, odd_, 0:tiles, :, :],
                                         tab[0:r, T_IOTA:T_IOTA + E].unsqueeze(1).unsqueeze(1).broadcast_to(every),
                                         top_f[0:r, 0:tiles, :].unsqueeze(3).broadcast_to(every), ALU.is_equal))
                wait(dve, rank_done, g)
                dve.tensor_tensor(mask16[0:r, 0:tiles, :], mask[0:r, odd_, 0:tiles, 0, :], mask[0:r, odd_, 0:tiles, 1, :], ALU.add).then_inc(mask_done, 1)

            def weights_of(g, odd_, s0, tiles, r):
                c = chain["weight"]
                c.start(g)
                dve.wait_ge(ex_done, g + 1)
                both = [r, tiles, TOPK]
                places = slice(s0, s0 + tiles)
                c.link(dve.tensor_reduce(total[0:r, 0, 0:tiles], ex[0:r, odd_, 0:tiles, :], AX.X, ALU.add))
                c.link(dve.reciprocal(total[0:r, 1, 0:tiles], total[0:r, 0, 0:tiles]))
                c.link(dve.tensor_tensor(pk[0:r, 0:tiles, :], ex[0:r, odd_, 0:tiles, 0:TOPK],
                                         total[0:r, 1, 0:tiles].unsqueeze(2).broadcast_to(both), ALU.mult))
                c.link(dve.scalar_tensor_tensor(den[0:r, 0, 0:tiles], pk[0:r, 0:tiles, 0], 1e-8, pk[0:r, 0:tiles, 1], ALU.add, ALU.add))
                dve.tensor_copy(zx[0:r, places, :, C + 1].bitcast(U32), target[0:r, 0:tiles, :])
                c.link(dve.reciprocal(den[0:r, 1, 0:tiles], den[0:r, 0, 0:tiles]))
                dve.tensor_tensor(zx[0:r, places, :, C], pk[0:r, 0:tiles, :], den[0:r, 1, 0:tiles].unsqueeze(2).broadcast_to(both),
                                  ALU.mult).then_inc(weights_done, 1)
                dve.tensor_scalar(target[:, :, :], target[:, :, :], float(TOPK * TPB * P), None, ALU.add)

            def slots_of(g, odd_, s0, tiles, r):
                c = chain["slot"]
                c.start(g)
                dve.wait_ge(rank_done, g + 1)
                c.link(dve.tensor_tensor(ranks[0:r, 0:tiles, :], R_BANK[0:r, 0:tiles * E].rearrange("p (t e) -> p t e", t=tiles),
                                         count[0:r, :].unsqueeze(1).broadcast_to([r, tiles, E]), ALU.add))
                c.link(dve.tensor_tensor(ranked[0:r, 0:tiles, :, :], mask[0:r, odd_, 0:tiles, :, :],
                                         ranks[0:r, 0:tiles, :].unsqueeze(2).broadcast_to([r, tiles, TOPK, E]), ALU.mult))
                c.link(dve.tensor_reduce(slot_f[0:r, 0:tiles, :], ranked[0:r, 0:tiles, :, :], AX.X, ALU.add))
                dve.tensor_copy(slot[0:r, odd_, 0:tiles, :], slot_f[0:r, 0:tiles, :]).then_inc(slot_done, 1)
                dve.tensor_tensor(count[:, :], R_BANK[:, TPB * E:(TPB + 1) * E], count[:, :], ALU.add).then_inc(rank_read, 1)

            def step(at, u, m):
                if (ts := at(5)) and (of := at_group(ts)):
                    route(*of, at_tile(ts)[0])
                if (ts := at(6)) and (of := at_group(ts)):
                    weights_of(*of)
                    slots_of(*of)
                if ts := at(1):
                    residual(ts)
                if ts := at(3):
                    split_row(ts)
                if u >= 1 and (e := preparing(u - 1, m)) is not None:
                    weight_size(e)
                if u >= 2 and (e := preparing(u - 2, m)) is not None:
                    weight_scale(e)
                if u >= 3 and (e := preparing(u - 3, m)) is not None:
                    split_low(e)

            run(dve, step)

            c = chain["table"]
            c.start(0)
            dve.wait_ge(rank_read, NT // TPB + 1)
            dve.tensor_copy(pad_at[:, :], count[0:1, :]).then_inc(pad_at_done, 1)
            rows_, tiles_, end_, begin_, start_ = (n_f[:, i, :] for i in range(5))
            c.link(dve.tensor_tensor(rows_, count[0:1, :], tab[0:1, T_BASE:T_BASE + E], ALU.subtract))
            c.link(dve.tensor_tensor(tiles_cmp[:, :, :], rows_.unsqueeze(2).broadcast_to([1, E, NR]),
                                     steps_in[:, NJ:].unsqueeze(1).broadcast_to([1, E, NR]), ALU.is_gt))
            c.link(dve.tensor_reduce(tiles_, tiles_cmp[:, :, :], AX.X, ALU.add))
            c.link(dve.tensor_tensor_scan(end_, tiles_, tiles_, 0.0, ALU.add, ALU.bypass))
            c.link(dve.tensor_tensor(begin_, end_, tiles_, ALU.subtract))
            c.link(dve.scalar_tensor_tensor(start_, begin_, -float(TR), tab[0:1, T_BASE:T_BASE + E], ALU.mult, ALU.add))
            j_ = steps_in[:, 0:NJ]
            j_b = j_.unsqueeze(2).broadcast_to([1, NJ, E])
            past, reached, mine = (sel[:, i, :, :] for i in range(3))
            c.link(dve.tensor_tensor(past, j_b, end_.unsqueeze(1).broadcast_to([1, NJ, E]), ALU.is_ge))
            c.link(dve.tensor_tensor(reached, j_b, begin_.unsqueeze(1).broadcast_to([1, NJ, E]), ALU.is_ge))
            c.link(dve.tensor_tensor(mine, reached, past, ALU.subtract))
            c.link(dve.tensor_tensor(mine, mine, start_.unsqueeze(1).broadcast_to([1, NJ, E]), ALU.mult))
            expert_, row_, used_, tmp_ = (step_f[:, i, :] for i in range(4))
            c.link(dve.tensor_reduce(expert_, past, AX.X, ALU.add))
            c.link(dve.tensor_reduce(tmp_, mine, AX.X, ALU.add))
            c.link(dve.scalar_tensor_tensor(row_, j_, float(TR), tmp_, ALU.mult, ALU.add))
            c.link(dve.tensor_scalar(used_, expert_, float(E), None, ALU.is_lt))
            c.link(dve.tensor_scalar(row_, row_, -float(E * REG), None, ALU.add))
            c.link(dve.tensor_tensor(row_, row_, used_, ALU.mult))
            c.link(dve.tensor_scalar(step_tab[:, NJ:], row_, float(E * REG), None, ALU.add))
            c.link(dve.tensor_scalar(step_tab[:, 0:NJ], expert_, float(E - 1), None, ALU.min))


def expert_stage(nc, kept, routed, expert_out):
    gu_hi, gu_lo, down, bg, bu, bd = (kept[n] for n in ("gu_hi", "gu_lo", "down", "bg", "bu", "bd"))
    inv_scale, id16, step_tab, banks = (kept[n] for n in ("inv_scale", "id16", "step_tab", "banks"))
    GU_BANK, ZT_BANK, Y_BANK = banks[0:4], banks[4:6], banks[6:8]
    with ExitStack() as ctx:
        def sb(name, shape, dt=F32):
            return ctx.enter_context(nc.sbuf_tensor(name, shape, dt))

        def sem(name):
            return ctx.enter_context(nc.semaphore(name))

        zg = sb("zg", [P, RING, RT, ROW])
        zt = sb("zt", [P, 2, 2 * KC, TR], F16)
        sg = sb("sg", [P, MC, TR])
        hid = sb("hid", [P, 2, MC, TR])
        ye = sb("ye", [P, 2, RT, C])
        yw = sb("yw", [P, 2, RT, C])
        loaded = [sem(f"loaded{s}") for s in range(RING)]
        stored = [sem("stored0"), sem("stored1")]
        zt_done, zt_copied, gu_done = sem("zt_done"), sem("zt_copied"), sem("gu_done")
        silu_done, hid_done, y_done, ye_done, yw_done = (sem(n) for n in ("silu_done", "hid_done", "ye_psum", "ye_done", "yw_done"))
        block = ctx.enter_context(nc.Block())

        def expert(eng, n):
            return eng.value_load(step_tab[0:1, n:n + 1] if isinstance(n, int) else step_tab[0:1, bass.ds(n, 1)],
                                  min_val=0, max_val=E - 1)

        def run(eng, step):
            pipeline(eng, NJ, 2, 1, 6, step)

        @block.sync
        def _(sp):
            def step(at, u, m):
                if ts := at(-2):
                    q, s = ts
                    n = q * RING + s
                    wait(sp, stored[s % 2], 16 * RT * (2 * q + s // 2 - 1))
                    i = NJ + n
                    row = sp.value_load(step_tab[0:1, i:i + 1] if isinstance(i, int) else step_tab[0:1, bass.ds(i, 1)],
                                        min_val=0, max_val=E * REG)
                    sp.dma_start(zg[:, s, :, :], routed[bass.ds(row, TR), :].rearrange("(p t) r -> p t r", t=RT)).then_inc(loaded[s], 16)

            run(sp, step)

        @block.gpsimd
        def _(pool):
            def step(at, u, m):
                if ts := at(1):
                    q, s = ts
                    n = q * RING + s
                    for t in range(RT):
                        pool.wait_ge(yw_done, n * RT + t + 1)
                        apart(pool)
                        pool.indirect_dma_start(
                            out=expert_out[:, :],
                            out_offset=bass.IndirectOffsetOnAxis(ap=zg[:, s, t, ROW - 1:ROW].bitcast(U32), axis=0),
                            in_=yw[:, s % 2, t, :], in_offset=None, bounds_check=OUT_ROWS - 1, oob_is_err=False).then_inc(stored[s % 2], 16)

            run(pool, step)
            pool.wait_ge(stored[0], 16 * RT * (NJ // 2))
            pool.wait_ge(stored[1], 16 * RT * (NJ // 2))

        @block.scalar
        def _(act):
            def step(at, u, m):
                if ts := at(0):
                    q, s = ts
                    n = q * RING + s
                    e = expert(act, n)
                for c in range(MC):
                    if at(0):
                        act.wait_ge(gu_done, n * MC + c + 1)
                        wait(act, hid_done, n * MC + c + 1 - MC)
                        act.activation(sg[:, c, :], GU_BANK[c][:, 0:TR], ACT.Silu,
                                       scale=inv_scale[:, bass.ds(e, 1)], bias=bg[:, bass.ds(e * MC + c, 1)]).then_inc(silu_done, 1)
                    if c == 0 and (ts := at(1)):
                        q1, s1 = ts
                        wait(act, stored[s1 % 2], 16 * RT * (2 * q1 + s1 // 2))
                        for t in range(RT):
                            act.wait_ge(ye_done, (q1 * RING + s1) * RT + t + 1)
                            act.activation(yw[:, s1 % 2, t, :], ye[:, s1 % 2, t, :], ACT.Copy, scale=zg[:, s1, t, C:C + 1]).then_inc(yw_done, 1)
                if ts := at(-1):
                    q, s = ts
                    n = q * RING + s
                    act.wait_ge(zt_done, n + 1)
                    wait(act, gu_done, (n - 1) * MC)
                    act.activation(zt[:, s % 2, :, :].rearrange("p k t -> p (k t)"), ZT_BANK[s % 2][:, :].bitcast(F16), ACT.Copy).then_inc(zt_copied, 1)

            run(act, step)

        @block.vector
        def _(dve):
            def step(at, u, m):
                if ts := at(1):
                    q, s = ts
                    n = q * RING + s
                    e = expert(dve, n)
                    for t in range(RT):
                        dve.wait_ge(y_done, n * RT + t + 1)
                        wait(dve, yw_done, (n - 2) * RT + t + 1)
                        dve.scalar_tensor_tensor(ye[:, s % 2, t, :], Y_BANK[t][:, 0:C], inv_scale[:, bass.ds(e, 1)],
                                                 bd[:, bass.ds(e * C, C)], ALU.mult, ALU.add).then_inc(ye_done, 1)
                if ts := at(0):
                    q, s = ts
                    n = q * RING + s
                    e = expert(dve, n)
                    wait(dve, y_done, (n - 1) * RT)
                    for c in range(MC):
                        dve.wait_ge(silu_done, n * MC + c + 1)
                        dve.scalar_tensor_tensor(hid[:, s % 2, c, :], GU_BANK[c][:, TR:2 * TR], bu[:, bass.ds(e * MC + c, 1)],
                                                 sg[:, c, :], ALU.add, ALU.mult).then_inc(hid_done, 1)

            run(dve, step)

        @block.tensor
        def _(pe):
            def step(at, u, m):
                if ts := at(0):
                    q, s = ts
                    n = q * RING + s
                    e = expert(pe, n)

                def gate_up(c):
                    wait(pe, hid_done, n * MC + c + 1 - MC)
                    for half_ in range(2):
                        dst = GU_BANK[c][:, half_ * TR:(half_ + 1) * TR]
                        for k in range(KC):
                            at_ = e * GU + (k * 2 * M + half_ * M + c * P)
                            hi, lo = gu_hi[:, bass.ds(at_, P)], gu_lo[:, bass.ds(at_, P)]
                            z_hi, z_lo = zt[:, s % 2, k, :], zt[:, s % 2, KC + k, :]
                            pe.matmul(dst, hi, z_hi, start=k == 0, stop=False)
                            pe.matmul(dst, hi, z_lo, start=False, stop=False)
                            last = pe.matmul(dst, lo, z_hi, start=False, stop=k == KC - 1)
                    last.then_inc(gu_done, 1)

                def project(c):
                    pe.wait_ge(hid_done, n * MC + c + 1)
                    for t in range(RT):
                        if c == 0:
                            wait(pe, ye_done, (n - 1) * RT + t + 1)
                        last = pe.matmul(Y_BANK[t][:, 0:C], hid[:, s % 2, c, t * P:(t + 1) * P],
                                         down[:, bass.ds(e * (MC * C) + c * C, C)], start=c == 0, stop=c == MC - 1)
                        if c == MC - 1:
                            last.then_inc(y_done, 1)

                if at(0):
                    pe.wait_ge(zt_copied, n + 1)
                    for c in range(MC):
                        gate_up(c)
                        if c >= 2:
                            project(c - 2)
                if ts := at(-1):
                    q1, s1 = ts
                    pe.wait_ge(loaded[s1], 16 * (q1 + 1))
                    wait(pe, zt_copied, q1 * RING + s1 - 1)
                    bank = ZT_BANK[s1 % 2][:, :].bitcast(F16)
                    for t in range(RT):
                        halves = zg[:, s1, t, 0:C].bitcast(F16)
                        for c in range(2 * KC):
                            last = pe.transpose(bank[:, c * TR + t * P:c * TR + (t + 1) * P], halves[:, c * P:(c + 1) * P], id16[:, :])
                    last.then_inc(zt_done, 1)
                if at(0):
                    project(MC - 2)
                    project(MC - 1)

            run(pe, step)


def combine_stage(nc, expert_out, h, out):
    with ExitStack() as ctx:
        def sb(name, shape, dt=F32):
            return ctx.enter_context(nc.sbuf_tensor(name, shape, dt))

        def sem(name):
            return ctx.enter_context(nc.semaphore(name))

        eo = sb("eo", [P, B, TPB, TOPK, C])
        cls_eo = sb("cls_eo", [B, TOPK, C])
        in_loaded = [sem(f"in_loaded{b}") for b in range(B)]
        half_summed, summed, out_stored = sem("half_summed"), sem("summed"), sem("out_stored")
        cls_in, cls_sum = sem("cls_in"), sem("cls_sum")
        block = ctx.enter_context(nc.Block())

        @block.sync
        def _(sp):
            for b in range(B):
                rows = expert_out[b * S * TOPK:(b + 1) * S * TOPK, :].rearrange("(t p k) c -> p t (k c)", p=P, k=TOPK)
                sp.dma_start(eo[:, b, :, :, :].rearrange("p t k c -> p t (k c)"), rows).then_inc(in_loaded[b], 16)
            sp.dma_start(cls_eo[:, :, :], expert_out[TOPK * B * S:, :].rearrange("(b k) c -> b k c", k=TOPK)).then_inc(cls_in, 16)

        @block.vector
        def _(dve):
            for b in range(B):
                first = eo[:, b, :, 0, :]
                dve.wait_ge(in_loaded[b], 16)
                dve.tensor_tensor(first, first, eo[:, b, :, 1, :], ALU.add).then_inc(half_summed, 1)
                dve.wait_ge(half_summed, b + 1)
                dve.tensor_tensor(first, first, h[:, b * TPB:(b + 1) * TPB, :], ALU.add).then_inc(summed, 1)
            dve.wait_ge(cls_in, 16)
            dve.tensor_tensor(cls_eo[:, 0, :], cls_eo[:, 0, :], cls_eo[:, 1, :], ALU.add).then_inc(cls_sum, 1)
            dve.wait_ge(cls_sum, 1)
            dve.tensor_tensor(cls_eo[:, 0, :], h[0:B, NT - 1, :], cls_eo[:, 0, :], ALU.add).then_inc(cls_sum, 1)

        @block.scalar
        def _(act):
            for b in range(B):
                act.wait_ge(summed, b + 1)
                act.dma_start(out[b, 1:, :].rearrange("(p t) c -> p t c", t=TPB), eo[:, b, :, 0, :]).then_inc(out_stored, 16)
            act.wait_ge(cls_sum, 2)
            act.dma_start(out[:, 0, :], cls_eo[:, 0, :]).then_inc(out_stored, 16)
            act.wait_ge(out_stored, 16 * (B + 1))


def kernel(x, cls_tok, L0_tok_weight, L0_tok_weighted_sum, L0_attn_w_qkv, L0_attn_b_qkv, L0_attn_w_out, L0_attn_b_out,
           L0_ffn_W_router, L0_ffn_W_gate, L0_ffn_b_gate, L0_ffn_W_up, L0_ffn_b_up, L0_ffn_W_out, L0_ffn_b_out):
    import numpy as np
    import concourse.bacc as bacc
    from concourse.bass_utils import run_bass_kernel_spmd as run

    def chunked(w):
        return w.reshape(w.shape[0] // P, P, w.shape[1]).transpose(1, 0, 2)

    a = {k: np.asarray(v) for k, v in dict(
        x=x, cls=cls_tok, tw=L0_tok_weight, tws=L0_tok_weighted_sum, wqkv=L0_attn_w_qkv, bqkv=L0_attn_b_qkv,
        wo=L0_attn_w_out, bo=L0_attn_b_out, wr=L0_ffn_W_router, wg=L0_ffn_W_gate, bg=L0_ffn_b_gate, wu=L0_ffn_W_up,
        bu=L0_ffn_b_up, wd=L0_ffn_W_out, bd=L0_ffn_b_out).items()}
    perm = np.concatenate([np.arange(2 * C), 2 * C + np.arange(C).reshape(NH, HD).T.ravel()])
    gu = np.stack([a["wg"], a["wu"]], 2).reshape(E, KC, P, 2 * M).transpose(0, 2, 1, 3).reshape(E, P, GU)
    table = np.zeros((P, T_COLS), np.float32)
    table[:, T_IOTA:T_IOTA + E] = np.arange(E)
    table[:, T_BASE:T_BASE + E] = np.arange(E) * REG
    table[:, T_TARGET:T_FAR] = ((np.arange(TPB) * P + np.arange(P)[:, None])[:, :, None] * TOPK + np.arange(TOPK)).reshape(P, -1)
    table[:, T_FAR] = FAR
    arrays = dict(
        x_t=a["x"].reshape(B, P, TPB, KC, P, D1).transpose(0, 2, 4, 5, 3, 1).reshape(NT - 1, P, XC * P),
        cls=a["cls"].reshape(1, C),
        tok_w=a["tw"].T,
        tok_ws=chunked(a["tws"].T),
        w_qkv=chunked(a["wqkv"][perm].T),
        b_qkv=a["bqkv"][perm].reshape(1, 3 * C),
        w_o=chunked(a["wo"].T),
        b_o=a["bo"].reshape(1, C),
        w_router=chunked(a["wr"]),
        w_gu=gu,
        b_gate=a["bg"].reshape(E, MC, P).transpose(2, 0, 1).reshape(P, E * MC),
        b_up=a["bu"].reshape(E, MC, P).transpose(2, 0, 1).reshape(P, E * MC),
        w_down=a["wd"].reshape(E, MC, P, C).transpose(2, 0, 1, 3).reshape(P, E * MC * C),
        b_down=a["bd"].reshape(1, E * C),
        ident=np.eye(P, dtype=np.float32),
        upper=np.triu(np.ones((P, P), np.float32), 1),
        table=table,
        steps=np.concatenate([np.arange(NJ), TR * np.arange(NR)]).astype(np.float32).reshape(1, -1),
    )
    nc = bacc.Bacc("TRN2", target_bir_lowering=False, num_devices=1)
    ins, aps = {}, {}
    for name, v in arrays.items():
        ins[f"in_{name}"] = np.ascontiguousarray(v)
        aps[name] = nc.dram_tensor(f"in_{name}", v.shape, mybir.dt.from_np(v.dtype), kind="ExternalInput").ap()
    aps["out"] = nc.dram_tensor("result", (B, S + 1, C), F32, kind="ExternalOutput").ap()
    vit_block(nc, **aps)
    return run(nc, [ins], core_ids=[0]).results[0]["result"]
```
